# Optimizing a Trainium2 kernel written in Bass

```python
import numpy as np
import jax
import jax.numpy as jnp

def _softmax(x, axis=-1):
    return jax.nn.softmax(x, axis=axis)

def _gelu(x):
    return jax.nn.gelu(x, approximate=True)

def _silu(x):
    return jax.nn.silu(x)

def _sigmoid(x):
    return jax.nn.sigmoid(x)

def _layernorm(x, axis=-1, eps=1e-05):
    m = jnp.mean(x, axis=axis, keepdims=True)
    v = jnp.var(x, axis=axis, keepdims=True)
    return (x - m) / jnp.sqrt(v + eps)

def _scatter_add(tgt, idx, src, axis=0):
    return tgt.at[idx].add(src)

def _segment_sum(src, seg, n):
    return jax.ops.segment_sum(src, seg, n)
kernel_name = 'mk_flamingo_gated_d1_seqx_r2_031799'

def setup_inputs(seed: int=0):
    np.random.seed(seed)
    _w = jnp.asarray

    def _rec_inputs():
        import jax
        import jax.numpy as jnp
        _rk = jax.random.key(seed)
        x = -0.0002928 + 1 * jax.random.normal(jax.random.fold_in(_rk, 1), (4, 1024, 512), jnp.float32)
        _lenS = 1024 - jax.random.randint(jax.random.fold_in(_rk, 7), (4,), 0, max(1, 1024 // 4) + 1, jnp.int32)
        _lenS2 = 1024 - jax.random.randint(jax.random.fold_in(_rk, 8), (4,), 0, max(1, 1024 // 4) + 1, jnp.int32)
        _ctx_1024P = jax.random.normal(jax.random.fold_in(_rk, 11), (4, 16, 512), jnp.float32)
        _ctx_1024c = jax.random.dirichlet(jax.random.fold_in(_rk, 511), 0.3 * jnp.ones((16,), jnp.float32), (4, 1024))
        _ctx_1024t = jnp.einsum('bsk,bkd->bsd', _ctx_1024c, _ctx_1024P)
        _ctx_1024t = _ctx_1024t * jax.lax.rsqrt(jnp.mean(jnp.square(_ctx_1024t)) + 1e-12) * 0.953939
        ctx_1024 = -1.39393e-06 + 0.999914 * (_ctx_1024t + 0.3 * jax.random.normal(jax.random.fold_in(_rk, 611), (4, 1024, 512), jnp.float32))
        _g = jax.random.normal(jax.random.fold_in(_rk, 9001), (2, 1), jnp.float32)
        _g = jnp.sign(_g) * jnp.maximum(jnp.abs(_g), 1.0) + (_g == 0) * 1.0
        g_xattn = _g[0]
        g_ffn = _g[1]
        return (x, ctx_1024, g_xattn, g_ffn)
    x, ctx_1024, g_xattn, g_ffn = _rec_inputs()

    def _L0_xattn_setup():
        import jax, jax.numpy as jnp
        import numpy as np
        DIM = 512
        NUM_HEADS = 16
        HEAD_DIM = DIM // NUM_HEADS
        key = jax.random.key(seed)
        ks = jax.random.split(key, 11)
        B, N, C = (2, 1024, DIM)
        s = 1.0 / np.sqrt(C)
        inp = {'q': jax.random.normal(ks[0], (B, N, C), jnp.float32), 'k': jax.random.normal(ks[1], (B, N, C), jnp.float32), 'v': jax.random.normal(ks[2], (B, N, C), jnp.float32), 'Wq': jax.random.normal(ks[3], (C, C), jnp.float32) * s, 'bq': jnp.zeros((C,), jnp.float32), 'Wk': jax.random.normal(ks[4], (C, C), jnp.float32) * s, 'bk': jnp.zeros((C,), jnp.float32), 'Wv': jax.random.normal(ks[5], (C, C), jnp.float32) * s, 'bv': jnp.zeros((C,), jnp.float32), 'Wo': jax.random.normal(ks[6], (C, C), jnp.float32) * s, 'bo': jnp.zeros((C,), jnp.float32)}
        return inp
    _L0_xattn_all = _L0_xattn_setup()
    _L0_xattn_in = {k: v for k, v in _L0_xattn_all.items() if k in ('Wq', 'bq', 'Wk', 'bk', 'Wv', 'bv', 'Wo', 'bo')}
    del _L0_xattn_all

    def _L0_ffn_setup():
        import math
        import jax, jax.numpy as jnp
        import numpy as np
        NUM_EXPERTS = 16
        TOP_K = 2
        CAPACITY_FACTOR = 1.25
        key = jax.random.key(seed)
        k1, k2, k3, k4 = jax.random.split(key, 4)
        d, dff, E = (512, 2048, NUM_EXPERTS)
        x = jax.random.normal(k1, (4, 1024, d), dtype=jnp.float32)
        router_w = jax.random.normal(k2, (E, d), dtype=jnp.float32) * d ** (-0.5)
        router_b = jnp.zeros((E,), dtype=jnp.float32)
        w1 = jax.random.normal(k3, (E, d, dff), dtype=jnp.float32) * 0.02
        b1 = jnp.zeros((E, dff), dtype=jnp.float32)
        w2 = jax.random.normal(k4, (E, dff, d), dtype=jnp.float32) * 0.02
        b2 = jnp.zeros((E, d), dtype=jnp.float32)
        return {'x': x, 'router_w': router_w, 'router_b': router_b, 'w1': w1, 'b1': b1, 'w2': w2, 'b2': b2}
    _L0_ffn_all = _L0_ffn_setup()
    _L0_ffn_in = {k: v for k, v in _L0_ffn_all.items() if k in ('router_w', 'router_b', 'w1', 'b1', 'w2', 'b2')}
    del _L0_ffn_all
    return {'x': x, 'ctx_1024': ctx_1024, 'g_xattn': g_xattn, 'g_ffn': g_ffn, 'L0_xattn_Wq': _L0_xattn_in['Wq'], 'L0_xattn_bq': _L0_xattn_in['bq'], 'L0_xattn_Wk': _L0_xattn_in['Wk'], 'L0_xattn_bk': _L0_xattn_in['bk'], 'L0_xattn_Wv': _L0_xattn_in['Wv'], 'L0_xattn_bv': _L0_xattn_in['bv'], 'L0_xattn_Wo': _L0_xattn_in['Wo'], 'L0_xattn_bo': _L0_xattn_in['bo'], 'L0_ffn_router_w': _L0_ffn_in['router_w'], 'L0_ffn_router_b': _L0_ffn_in['router_b'], 'L0_ffn_w1': _L0_ffn_in['w1'], 'L0_ffn_b1': _L0_ffn_in['b1'], 'L0_ffn_w2': _L0_ffn_in['w2'], 'L0_ffn_b2': _L0_ffn_in['b2']}

def reference(x, ctx_1024, g_xattn, g_ffn, L0_xattn_Wq, L0_xattn_bq, L0_xattn_Wk, L0_xattn_bk, L0_xattn_Wv, L0_xattn_bv, L0_xattn_Wo, L0_xattn_bo, L0_ffn_router_w, L0_ffn_router_b, L0_ffn_w1, L0_ffn_b1, L0_ffn_w2, L0_ffn_b2):
    import jax
    import jax.numpy as jnp

    def _L0_xattn_ref(q, k, v, Wq, bq, Wk, bk, Wv, bv, Wo, bo):
        import jax, jax.numpy as jnp
        import numpy as np
        DIM = 512
        NUM_HEADS = 16
        HEAD_DIM = DIM // NUM_HEADS
        B, Nq, C = q.shape
        Nkv = k.shape[1]
        H, D = (NUM_HEADS, HEAD_DIM)
        qh = (q @ Wq.T + bq).reshape(B, Nq, H, D).transpose(0, 2, 1, 3)
        kh = (k @ Wk.T + bk).reshape(B, Nkv, H, D).transpose(0, 2, 1, 3)
        vh = (v @ Wv.T + bv).reshape(B, Nkv, H, D).transpose(0, 2, 1, 3)
        scale = D ** (-0.5)
        attn = jax.nn.softmax(jnp.einsum('bhqd,bhkd->bhqk', qh, kh) * scale, axis=-1)
        out = jnp.einsum('bhqk,bhkd->bhqd', attn, vh)
        out = out.transpose(0, 2, 1, 3).reshape(B, Nq, C)
        return out @ Wo.T + bo

    def _L0_ffn_ref(x, router_w, router_b, w1, b1, w2, b2):
        import math
        import jax, jax.numpy as jnp
        import numpy as np
        NUM_EXPERTS = 16
        TOP_K = 2
        CAPACITY_FACTOR = 1.25
        E, k = (NUM_EXPERTS, TOP_K)
        B, S, d = x.shape
        tokens = B * S
        capacity = max(1, int(math.ceil(CAPACITY_FACTOR * tokens * k / E)))
        x2d = x.reshape(tokens, d)
        logits = x2d @ router_w.T + router_b
        vals, idx = jax.lax.top_k(logits, k)
        gates = jax.nn.softmax(vals, axis=-1)
        flat_e = idx.reshape(-1)
        oh = (flat_e[:, None] == jnp.arange(E)[None, :]).astype(jnp.int32)
        pos = jnp.take_along_axis(jnp.cumsum(oh, axis=0) - 1, flat_e[:, None], axis=1)[:, 0]
        kept = pos < capacity
        kept2 = kept.reshape(tokens, k)
        denom = jnp.sum(gates * kept2, axis=-1, keepdims=True)
        gates = jnp.where(kept2, gates / (denom + 1e-09), 0.0)
        slot = flat_e * capacity + pos
        slot_safe = jnp.where(kept, slot, E * capacity)
        x_rep = jnp.repeat(x2d, k, axis=0)
        buf = jnp.zeros((E * capacity + 1, d), x.dtype).at[slot_safe].set(x_rep)
        packed = buf[:E * capacity].reshape(E, capacity, d)
        h = jax.nn.gelu(jnp.einsum('ecd,edf->ecf', packed, w1) + b1[:, None, :], approximate=False)
        expert_out = jnp.einsum('ecf,efd->ecd', h, w2) + b2[:, None, :]
        eflat = expert_out.reshape(E * capacity, d)
        gathered = eflat[jnp.clip(slot, 0, E * capacity - 1)]
        w = (gates.reshape(-1) * kept.astype(x.dtype))[:, None]
        out = (gathered * w).reshape(tokens, k, d).sum(axis=1)
        return out.reshape(B, S, d)
    x = x + jnp.tanh(g_xattn[0]) * _L0_xattn_ref(_layernorm(x, axis=-1), ctx_1024, ctx_1024, L0_xattn_Wq, L0_xattn_bq, L0_xattn_Wk, L0_xattn_bk, L0_xattn_Wv, L0_xattn_bv, L0_xattn_Wo, L0_xattn_bo)
    x = x + jnp.tanh(g_ffn[0]) * _L0_ffn_ref(_layernorm(x, axis=-1), L0_ffn_router_w, L0_ffn_router_b, L0_ffn_w1, L0_ffn_b1, L0_ffn_w2, L0_ffn_b2)
    return x

_drawn_inputs = setup_inputs


def setup_inputs(seed=0):
    import zlib

    import numpy as np

    out = dict(_drawn_inputs(seed))
    spreads = {'L0_xattn_bq': (0.0, 0.1),
     'L0_xattn_bk': (0.0, 0.1),
     'L0_xattn_bv': (0.0, 0.1),
     'L0_xattn_bo': (0.0, 0.1),
     'L0_ffn_router_b': (0.0, 0.1),
     'L0_ffn_b1': (0.0, 0.1),
     'L0_ffn_b2': (0.0, 0.1)}
    factors = {}
    for name, (base, spread) in spreads.items():
        noise = np.random.default_rng([zlib.crc32(name.encode()), seed]).standard_normal(out[name].shape)
        drawn = base * np.exp(spread * noise) if base else spread * noise
        out[name] = jnp.asarray(drawn.astype(out[name].dtype))
    for name, factor in factors.items():
        out[name] = (out[name] * factor).astype(out[name].dtype)
    return out
```

```python
from contextlib import ExitStack

import concourse.bass as bass
from concourse import mybir

F32 = mybir.dt.float32
F32R = mybir.dt.float32r
BF16 = mybir.dt.bfloat16
I32 = mybir.dt.int32
U32 = mybir.dt.uint32
ALU = mybir.AluOpType
ACT = mybir.ActivationFunctionType
AX_X = mybir.AxisListType.X
ds = bass.ds

P = 128
EPS = 1e-5


class Shapes:

    def __init__(self, x, w1):
        self.B, self.S, self.D = x.shape
        self.E, _, self.F = w1.shape
        self.H = 16
        self.HD = self.D // self.H
        self.TOP = 2
        self.TOK = self.B * self.S
        self.CAP = -(-5 * self.TOK * self.TOP // (4 * self.E))
        self.KT = self.D // P
        self.CH = 512
        self.NCH = self.TOK // self.CH
        self.TPC = self.CH // P
        self.NT = self.TOK // P


def split_matmul(pe, out, w_hi, w_lo, m_hi, m_lo, first, last):
    pe.matmul(out, w_hi, m_hi, start=first, stop=False)
    pe.matmul(out, w_hi, m_lo, start=False, stop=False)
    return pe.matmul(out, w_lo, m_hi, start=False, stop=last)


def settle(engine, passed):
    engine.sem_inc(passed, 1)


def make_identity(nc, pool, ident, ready):
    pool.memset(ident[:, :], 0.0).then_inc(ready, 1)
    pool.wait_ge(ready, 1)
    pool.affine_select(out=ident[:, :], in_=ident[:, :], compare_op=ALU.not_equal, fill=1.0, base=0,
                       pattern=[[-1, P]], channel_multiplier=1).then_inc(ready, 1)


def project_inputs(nc, z, a, scr):
    KT, CH, TPC, NCH, D = z.KT, z.CH, z.TPC, z.NCH, z.D
    with ExitStack() as ctx:
        def sb(name, shape, dt=F32):
            return ctx.enter_context(nc.sbuf_tensor(name, shape, dt))

        def sem(name):
            return ctx.enter_context(nc.semaphore(name))

        ident = sb("pi_ident", [P, P])
        eps = sb("pi_eps", [P, 1])
        w_raw = sb("pi_w_raw", [P, 3, KT, D])
        wT_hi = sb("pi_wT_hi", [P, 3, KT, D], F32R)
        wT_lo = sb("pi_wT_lo", [P, 3, KT, D], F32R)
        b_qk = sb("pi_b_qk", [P, 2, KT])
        b_v = sb("pi_b_v", [P, D])
        x_raw = sb("pi_x_raw", [P, TPC, D])
        c_raw = sb("pi_c_raw", [P, TPC, D])
        xn = sb("pi_xn", [P, TPC, D])
        stats = sb("pi_stats", [P, TPC, 6])
        mv = sb("pi_mv", [P, TPC, 2])
        std = sb("pi_std", [P, TPC])
        rstd = sb("pi_rstd", [P, TPC])
        xT = [sb("pi_xT_hi", [P, KT, CH], F32R), sb("pi_xT_lo", [P, KT, CH], F32R)]
        cT = [sb("pi_cT_hi", [P, KT, CH], F32R), sb("pi_cT_lo", [P, KT, CH], F32R)]
        qk_out = sb("pi_qk_out", [P, 2, 2, KT, CH], F32R)
        v_out = sb("pi_v_out", [P, TPC, D])
        turned = ctx.enter_context(nc.psum_tensor("pi_turned", [P, 4, 512], F32))
        projected = ctx.enter_context(nc.psum_tensor("pi_projected", [P, 4, 512], F32))

        dve_passed = sem("pi_dve_passed")
        ident_ready, eps_ready = sem("pi_ident_ready"), sem("pi_eps_ready")
        w_loaded, b_loaded = sem("pi_w_loaded"), sem("pi_b_loaded")
        x_loaded, c_loaded = sem("pi_x_loaded"), sem("pi_c_loaded")
        var_ready, std_ready, rstd_ready = sem("pi_var_ready"), sem("pi_std_ready"), sem("pi_rstd_ready")
        xn_ready = sem("pi_xn_ready")
        turn_done, hi_done, lo_done = sem("pi_turn_done"), sem("pi_hi_done"), sem("pi_lo_done")
        proj_done = sem("pi_proj_done")
        qk_hi_done, proj_read = sem("pi_qk_hi_done"), sem("pi_proj_read")
        stored = [sem(f"pi_stored{i}") for i in range(5)]

        WU = 3 * KT

        def x_units(n):
            return WU + TPC + 2 * TPC * n

        def c_units(n):
            return x_units(n) + TPC

        with nc.Block() as block:
            @block.sync
            def _(sp):
                for i, w in enumerate(("Wq", "Wk", "Wv")):
                    sp.dma_start(w_raw[:, i], a[w].rearrange("(m p) c -> p m c", p=P)).then_inc(w_loaded, 16)
                with nc.allow_non_contiguous_dma(reason="512 elements each"):
                    sp.dma_start(b_qk[:, 0, :], a["bq"].rearrange("(m p) -> p m", p=P)).then_inc(b_loaded, 16)
                    sp.dma_start(b_qk[:, 1, :], a["bk"].rearrange("(m p) -> p m", p=P)).then_inc(b_loaded, 16)
                sp.dma_start(b_v[:, :], a["bv"].rearrange("(o c) -> o c", o=1).to_broadcast([P, D])).then_inc(b_loaded, 16)

                def load(dst, src, n, done):
                    sp.dma_start(dst[:, :, :], src[ds(n * CH, CH), :].rearrange("(t p) c -> p t c", p=P)).then_inc(done, 16)

                load(x_raw, a["x"], 0, x_loaded)
                load(c_raw, a["ctx"], 0, c_loaded)
                sp.wait_ge(xn_ready, TPC)
                load(x_raw, a["x"], 1, x_loaded)
                with sp.Fori(0, NCH - 2) as n:
                    sp.wait_ge(turn_done, c_units(n))
                    load(c_raw, a["ctx"], n + 1, c_loaded)
                    sp.wait_ge(xn_ready, TPC * (n + 2))
                    load(x_raw, a["x"], n + 2, x_loaded)
                sp.wait_ge(turn_done, c_units(NCH - 2))
                load(c_raw, a["ctx"], NCH - 1, c_loaded)

            @block.gpsimd
            def _(pool):
                pool.memset(eps[:, :], EPS).then_inc(eps_ready, 1)
                make_identity(nc, pool, ident, ident_ready)
                with pool.Fori(0, NCH) as n:
                    for i in range(4):
                        t, part = i // 2, i % 2
                        if part == 0:
                            pool.wait_ge(qk_hi_done, 2 * KT * n + KT * (t + 1))
                        else:
                            pool.wait_ge(proj_read, 3 * KT * n + KT * (t + 1))
                        pool.dma_start(scr["qk"][t, part].rearrange("g p n -> p g n")[:, :, ds(n * CH, CH)],
                                       qk_out[:, t, part].bitcast(F32)).then_inc(stored[i], 16)
                    pool.wait_ge(proj_read, 3 * KT * n + 3 * KT)
                    pool.dma_start(scr["v"][ds(n * CH, CH), :].rearrange("(t p) c -> p t c", p=P),
                                   v_out[:, :, :]).then_inc(stored[4], 16)
                for i in range(5):
                    pool.wait_ge(stored[i], 16 * NCH)

            def unit_hi(u, bank, dst):
                nc.scalar.wait_ge(turn_done, u + 1)
                nc.scalar.activation(dst, turned[:, bank, :].rearrange("p (k t) -> p k t", t=P), ACT.Copy).then_inc(hi_done, 1)

            def unit_lo(u, bank, dst, hi):
                nc.vector.wait_ge(hi_done, u + 1)
                nc.vector.tensor_tensor(dst, turned[:, bank, :].rearrange("p (k t) -> p k t", t=P), hi.bitcast(F32),
                                        ALU.subtract).then_inc(lo_done, 1)

            def w_part(w, k):
                return w[:, k // KT, k % KT, :].rearrange("p (k t) -> p k t", t=P)

            @block.scalar
            def _(act):
                def std_of(n):
                    act.wait_ge(var_ready, n + 1)
                    act.activation(std[:, :], mv[:, :, 1], ACT.Sqrt, bias=eps[:, 0:1]).then_inc(std_ready, 1)

                def qk_hi(n, t):
                    act.wait_ge(stored[2 * t], 16 * n)
                    for m in range(KT):
                        o = 3 * KT * n + KT * t + m
                        act.wait_ge(proj_done, o + 1)
                        act.activation(qk_out[:, t, 0, m, :], projected[:, m, :], ACT.Identity,
                                       bias=b_qk[:, t, m:m + 1]).then_inc(qk_hi_done, 1)

                act.wait_ge(eps_ready, 1)
                act.wait_ge(b_loaded, 48)
                for k in range(WU):
                    unit_hi(k, k % 4, w_part(wT_hi, k))
                std_of(0)
                for t in range(TPC):
                    unit_hi(WU + t, t, xT[0][:, :, t * P:(t + 1) * P])

                def chunk(n, last):
                    if not last:
                        std_of(n + 1)
                    for t in range(TPC):
                        unit_hi(x_units(n) + t, t, cT[0][:, :, t * P:(t + 1) * P])
                    qk_hi(n, 0)
                    if not last:
                        for t in range(TPC):
                            unit_hi(c_units(n) + t, t, xT[0][:, :, t * P:(t + 1) * P])
                    qk_hi(n, 1)

                with act.Fori(0, NCH - 1) as n:
                    chunk(n, False)
                chunk(NCH - 1, True)

            @block.vector
            def _(dve):
                def normalise(n):
                    dve.wait_ge(x_loaded, 16 * (n + 1))
                    for t in range(TPC):
                        last = dve.bn_stats(stats[:, t, :], x_raw[:, t, :])
                    last.then_inc(rstd_ready, 1)
                    dve.wait_ge(rstd_ready, 2 * n + 1)
                    settle(dve, dve_passed)
                    for t in range(TPC):
                        last = dve.bn_aggr(mv[:, t, :], stats[:, t, :])
                    last.then_inc(var_ready, 1)
                    dve.wait_ge(std_ready, n + 1)
                    dve.reciprocal(rstd[:, :], std[:, :]).then_inc(rstd_ready, 1)
                    dve.wait_ge(rstd_ready, 2 * n + 2)
                    if not isinstance(n, int) or n > 0:
                        dve.wait_ge(turn_done, x_units(n) - 2 * TPC)
                    for t in range(TPC):
                        dve.tensor_scalar(xn[:, t, :], x_raw[:, t, :], mv[:, t, 0:1], rstd[:, t:t + 1],
                                          ALU.subtract, ALU.mult).then_inc(xn_ready, 1)

                def qk_lo(n, t):
                    dve.wait_ge(stored[2 * t + 1], 16 * n)
                    for m in range(KT):
                        dve.wait_ge(qk_hi_done, 2 * KT * n + KT * t + m + 1)
                        dve.scalar_tensor_tensor(out=qk_out[:, t, 1, m, :], in0=projected[:, m, :],
                                                 scalar=b_qk[:, t, m:m + 1], in1=qk_out[:, t, 0, m, :].bitcast(F32),
                                                 op0=ALU.add, op1=ALU.subtract).then_inc(proj_read, 1)

                dve.wait_ge(b_loaded, 48)
                for k in range(WU):
                    unit_lo(k, k % 4, w_part(wT_lo, k), w_part(wT_hi, k))
                normalise(0)
                for t in range(TPC):
                    sl = slice(t * P, (t + 1) * P)
                    unit_lo(WU + t, t, xT[1][:, :, sl], xT[0][:, :, sl])

                def chunk(n, last):
                    if not last:
                        normalise(n + 1)
                    for t in range(TPC):
                        sl = slice(t * P, (t + 1) * P)
                        unit_lo(x_units(n) + t, t, cT[1][:, :, sl], cT[0][:, :, sl])
                    qk_lo(n, 0)
                    if not last:
                        for t in range(TPC):
                            sl = slice(t * P, (t + 1) * P)
                            unit_lo(c_units(n) + t, t, xT[1][:, :, sl], xT[0][:, :, sl])
                    qk_lo(n, 1)
                    dve.wait_ge(stored[4], 16 * n)
                    for t in range(TPC):
                        dve.wait_ge(proj_done, 3 * KT * n + 2 * KT + t + 1)
                        dve.tensor_tensor(v_out[:, t, :], projected[:, t, :], b_v[:, :], ALU.add).then_inc(proj_read, 1)

                with dve.Fori(0, NCH - 1) as n:
                    chunk(n, False)
                chunk(NCH - 1, True)

            @block.tensor
            def _(pe):
                def turn(u, bank, src, free):
                    if free:
                        pe.wait_ge(lo_done, u - 3)
                    for k in range(KT):
                        last = pe.transpose(turned[:, bank, k * P:(k + 1) * P], src(k), ident[:, :])
                    last.then_inc(turn_done, 1)

                def turn_x(n):
                    for t in range(TPC):
                        pe.wait_ge(xn_ready, TPC * n + t + 1)
                        turn(x_units(n) - TPC + t, t, lambda k: xn[:, t, k * P:(k + 1) * P], True)

                def project_qk(n, t, src, ready):
                    pe.wait_ge(lo_done, ready)
                    for m in range(KT):
                        if t or not isinstance(n, int) or n > 0:
                            pe.wait_ge(proj_read, 3 * KT * n + KT * t + m + 1 - 4)
                        for k in range(KT):
                            last = split_matmul(pe, projected[:, m, :], wT_hi[:, t, k, m * P:(m + 1) * P],
                                                wT_lo[:, t, k, m * P:(m + 1) * P], src[0][:, k, :], src[1][:, k, :],
                                                k == 0, k == KT - 1)
                        last.then_inc(proj_done, 1)

                pe.wait_ge(ident_ready, 2)
                pe.wait_ge(w_loaded, 48)
                for k in range(WU):
                    turn(k, k % 4, lambda m: w_raw[:, k // KT, m, (k % KT) * P:(k % KT + 1) * P], k >= 4)
                turn_x(0)

                def chunk(n, first, last):
                    pe.wait_ge(c_loaded, 16 * (n + 1))
                    for t in range(TPC):
                        turn(x_units(n) + t, t, lambda k: c_raw[:, t, k * P:(k + 1) * P], True)
                    project_qk(n, 0, xT, x_units(n))
                    if not last:
                        turn_x(n + 1)
                    project_qk(n, 1, cT, c_units(n))
                    for t in range(TPC):
                        pe.wait_ge(proj_read, 3 * KT * n + 2 * KT + t + 1 - 4)
                        for k in range(KT):
                            last_mm = split_matmul(pe, projected[:, t, :], cT[0][:, k, t * P:(t + 1) * P],
                                                   cT[1][:, k, t * P:(t + 1) * P], wT_hi[:, 2, k, :], wT_lo[:, 2, k, :],
                                                   k == 0, k == KT - 1)
                        last_mm.then_inc(proj_done, 1)

                chunk(0, True, False)
                with pe.Fori(1, NCH - 1) as n:
                    chunk(n, False, False)
                chunk(NCH - 1, False, True)


def attend(nc, z, scr):
    B, S, HD, KT = z.B, z.S, z.HD, z.KT
    HPG = P // HD
    G_ALL = B * z.H // HPG
    PAIRS = G_ALL // 2
    QT = S // P
    QH = S // 512
    STEPS = QT * QH
    UNITS = HPG * QT
    ROWS = 3 * HD
    SCALE = float(HD) ** -0.5
    RING = 8
    HP = HPG - 1
    SPREAD = [3 if t in (0, 3, 6, 9) else 2 for t in range(STEPS - 2)] + [0, 0]
    TURN_STEP = STEPS - 2
    assert sum(SPREAD) == UNITS and HPG == 4 and QH == 2

    with ExitStack() as ctx:
        def sb(name, shape, dt=F32):
            return ctx.enter_context(nc.sbuf_tensor(name, shape, dt))

        def ps(name, shape):
            return ctx.enter_context(nc.psum_tensor(name, shape, F32))

        def sem(name):
            return ctx.enter_context(nc.semaphore(name))

        ident = sb("at_ident", [P, P])
        ones = sb("at_ones", [P, HD])
        q_st = [sb(f"at_q{e}", [P, HPG, S], F32R) for e in range(2)]
        k_st = [sb(f"at_k{e}", [P, HPG, S], F32R) for e in range(2)]
        v_sb = [sb(f"at_v{e}", [P, QT, P]) for e in range(2)]
        maxima = [sb(f"at_max{e}", [P, P]) for e in range(2)]
        neg_max = [sb(f"at_negmax{e}", [UNITS, P], F32R) for e in range(2)]
        probs = [sb(f"at_probs{r}", [P, HPG, 512]) for r in range(RING)]
        psum_k = [sb(f"at_keysum{h}", [P, HPG, 512]) for h in range(QH)]
        o_raw = [sb(f"at_o_raw{h}", [P, 512]) for h in range(QH)]
        den_t = sb("at_den_t", [P, 512])
        recip_t = sb("at_recip_t", [P, 512 // 32])
        recip = sb("at_recip", [P, 512])
        o_out = [sb(f"at_o_out{h}", [P, 512]) for h in range(QH)]
        unit_ps = [ps(f"at_unit_ps{i}", [P, 2, 512]) for i in range(2)]
        score_ps = [ps(f"at_score_ps{i}", [P, 512]) for i in range(2)]
        pv_ps = ps("at_pv_ps", [P, 512])
        den_ps = ps("at_den_ps", [P, 512])

        const_ready = sem("at_const_ready")
        ident_ready = sem("at_ident_ready")
        qk_loaded = [[sem(f"at_qk_loaded{e}{j}") for j in range(HPG)] for e in range(2)]
        v_loaded = [sem(f"at_v_loaded{e}") for e in range(2)]
        max_loaded = [sem(f"at_max_loaded{e}") for e in range(2)]
        unit_done, unit_read = sem("at_unit_done"), sem("at_unit_read")
        score_done, exp_done = sem("at_score_done"), sem("at_exp_done")
        pv_done, pv_read = sem("at_pv_done"), sem("at_pv_read")
        added = sem("at_added")
        added_last = sem("at_added_last")
        den_done, recip_done, o_done = sem("at_den_done"), sem("at_recip_done"), sem("at_o_done")
        o_stored = [sem(f"at_o_stored{h}") for h in range(QH)]

        def whole(G):
            return isinstance(G, int)

        with nc.Block() as block:
            @block.sync
            def _(sp):
                def load(G, e):
                    b, g = G // 4, G % 4
                    if not (whole(G) and G < 2):
                        sp.wait_ge(score_done, HPG * STEPS * (G - 1))
                    for j in range(HPG):
                        for dst, t, parts in ((q_st[e], 0, (0, 1, 0)), (k_st[e], 1, (0, 0, 1))):
                            for r, part in enumerate(parts):
                                src = scr["qk"][t, part].rearrange("g p n -> (g p) n")
                                sp.dma_start(dst[r * HD:(r + 1) * HD, j, :].bitcast(F32),
                                             src[ds(g * P + j * HD, HD), ds(b * S, S)]).then_inc(qk_loaded[e][j], 16)
                        if j == 0:
                            if not (whole(G) and G < 2):
                                sp.wait_ge(pv_done, STEPS * (G - 1))
                            sp.dma_start(v_sb[e][:, :, :], scr["v"][ds(b * S, S), ds(g * P, P)]
                                         .rearrange("(k p) c -> p k c", p=P)).then_inc(v_loaded[e], 16)

                def store(G, h):
                    b, g = G // 4, G % 4
                    sp.wait_ge(o_done, QH * G + h + 1)
                    sp.dma_start(scr["o"][ds(g * P, P), ds(b * S + h * 512, 512)], o_out[h][:, :]).then_inc(o_stored[h], 16)

                def load_max(G, e):
                    sp.wait_ge(unit_read, (UNITS + 1) * (G + 1))
                    sp.dma_start(q_st[e][ROWS:ROWS + 1, :, :].bitcast(F32).rearrange("o j (t n) -> o (j t) n", n=P),
                                 neg_max[e][:, :].bitcast(F32)).then_inc(max_loaded[e], 16)

                load(0, 0)
                load_max(0, 0)

                def pair(i, first, last):
                    load(2 * i + 1, 1)
                    if not first:
                        store(2 * i - 1, 1)
                    store(2 * i, 0)
                    load_max(2 * i + 1, 1)
                    if not last:
                        load(2 * i + 2, 0)
                    store(2 * i, 1)
                    store(2 * i + 1, 0)
                    if not last:
                        load_max(2 * i + 2, 0)

                pair(0, True, False)
                with sp.Fori(1, PAIRS - 1) as i:
                    pair(i, False, False)
                pair(PAIRS - 1, False, True)
                store(G_ALL - 1, 1)
                for h in range(QH):
                    sp.wait_ge(o_stored[h], 16 * G_ALL)

            @block.gpsimd
            def _(pool):
                make_identity(nc, pool, ident, ident_ready)

                def group(G, first):
                    for h in range(QH):
                        for k in range(1, QT):
                            T = QT * h + k
                            pool.wait_ge(exp_done, HPG * (STEPS * G + T + 1))
                            if k == 1 and not first:
                                pool.wait_ge(den_done, QH * (G - 1) + h + 1)
                            if k > 1 or h > 0 or not first:
                                pool.wait_ge(added, (QT - 1) * (QH * G + h) + k - 1)
                            before = probs[(T - 1) % RING] if k == 1 else psum_k[h]
                            pool.tensor_tensor(psum_k[h][:, 0:HP, :], probs[T % RING][:, 0:HP, :], before[:, 0:HP, :],
                                               ALU.add).then_inc(added, 1)

                group(0, True)
                with pool.Fori(1, G_ALL) as G:
                    group(G, False)

            @block.scalar
            def _(act):
                def exps(G, T, first):
                    for j in range(HPG):
                        n = HPG * (STEPS * G + T) + j
                        if j == 0:
                            if T >= RING:
                                k = T - RING
                                act.wait_ge(pv_done, STEPS * G + k + 1)
                                for add in (added, added_last):
                                    act.wait_ge(add, (QT - 1) * (QH * G + k // QT) + max(k % QT, 1))
                            elif not first:
                                k = STEPS + T - RING
                                act.wait_ge(pv_done, STEPS * (G - 1) + k + 1)
                                for add in (added, added_last):
                                    act.wait_ge(add, (QT - 1) * (QH * (G - 1) + 1) + max(k % QT, 1))
                        act.wait_ge(score_done, n + 1)
                        act.activation(probs[T % RING][:, j, :], score_ps[j % 2][:, :], ACT.Exp,
                                       scale=SCALE).then_inc(exp_done, 1)

                def read_pv(G, h, first=False):
                    act.wait_ge(pv_done, STEPS * G + QT * (h + 1))
                    if not first:
                        act.wait_ge(o_done, QH * (G - 1) + h + 1)
                    act.activation(o_raw[h][:, :], pv_ps[:, :], ACT.Copy).then_inc(pv_read, 1)

                def group(G, first):
                    for T in range(STEPS):
                        exps(G, T, first)
                        if T == 0 and not first:
                            read_pv(G - 1, 1, whole(G) and G == 1)
                        if T == QT:
                            read_pv(G, 0, first)

                group(0, True)
                group(1, False)
                with act.Fori(2, G_ALL) as G:
                    group(G, False)
                read_pv(G_ALL - 1, 1)

            @block.vector
            def _(dve):
                dve.memset(ones[:, :], 1.0)
                for e in range(2):
                    dve.memset(k_st[e][ROWS:ROWS + 1, :, :].bitcast(F32), 1.0)
                    last = dve.memset(maxima[e][:, :], 0.0)
                last.then_inc(const_ready, 1)
                dve.wait_ge(const_ready, 1)

                def unit(G, e, u):
                    dve.wait_ge(unit_done, (UNITS + 1) * G + u + 1)
                    dve.tensor_reduce(maxima[e][:, u:u + 1], unit_ps[(e + u) % 2][:, :, :].rearrange("p a b -> p (a b)"),
                                      AX_X, ALU.max).then_inc(unit_read, 1)

                def read_turn(G, e, use):
                    dve.wait_ge(unit_done, (UNITS + 1) * (G + 1))
                    dve.wait_ge(max_loaded[e], 16 * use)
                    dve.tensor_scalar(neg_max[e][:, :], unit_ps[(e + UNITS) % 2][0:UNITS, 0, 0:P], -1.0, None,
                                      ALU.mult).then_inc(unit_read, 1)

                def invert(G, h, stage):
                    if stage == 0:
                        dve.wait_ge(den_done, QH * G + h + 1)
                        dve.transpose(den_t[:, :], den_ps[:, :]).then_inc(recip_done, 1)
                    elif stage == 1:
                        dve.wait_ge(recip_done, 3 * (QH * G + h) + 1)
                        dve.reciprocal(recip_t[:, :], den_t[:, :].rearrange("p (b c) -> p b c", c=32)[:, :, 0]).then_inc(recip_done, 1)
                    else:
                        dve.wait_ge(recip_done, 3 * (QH * G + h) + 2)
                        dve.transpose(recip[:, :], recip_t[:, :].unsqueeze(2).to_broadcast([P, 512 // 32, 32])).then_inc(recip_done, 1)

                def normalise(G, h):
                    dve.wait_ge(recip_done, 3 * (QH * G + h) + 3)
                    dve.wait_ge(pv_read, QH * G + h + 1)
                    dve.wait_ge(o_stored[h], 16 * G)
                    dve.tensor_tensor(o_out[h][:, :], o_raw[h][:, :], recip[:, :], ALU.mult).then_inc(o_done, 1)

                def add_keys(G, T, first):
                    h, k = T // QT, T % QT
                    if k == 0:
                        return
                    dve.wait_ge(exp_done, HPG * (STEPS * G + T + 1))
                    if k == 1 and not first:
                        dve.wait_ge(den_done, QH * (G - 1) + h + 1)
                    if k > 1 or h > 0 or not first:
                        dve.wait_ge(added_last, (QT - 1) * (QH * G + h) + k - 1)
                    before = probs[(T - 1) % RING] if k == 1 else psum_k[h]
                    dve.tensor_tensor(psum_k[h][:, HP, :], probs[T % RING][:, HP, :], before[:, HP, :],
                                      ALU.add).then_inc(added_last, 1)

                def results(G, T, first):
                    for Gh, h, T0 in ((G - 1, 1, 3), (G, 0, QT + 3)):
                        if T in (T0, T0 + 1) and not (first and h == 1):
                            if T == T0:
                                invert(Gh, h, 0)
                                yield
                                invert(Gh, h, 1)
                            else:
                                invert(Gh, h, 2)
                                yield
                                normalise(Gh, h)

                def group(G, e, i, first, last):
                    u = 0
                    for T in range(STEPS):
                        stages = results(G, T, first)
                        if not last:
                            for _ in range(SPREAD[T]):
                                unit(G + 1, 1 - e, u)
                                u += 1
                                next(stages, None)
                            if T == TURN_STEP:
                                read_turn(G + 1, 1 - e, i + e)
                        add_keys(G, T, first)
                        for _ in stages:
                            pass

                for u in range(UNITS):
                    unit(0, 0, u)
                read_turn(0, 0, 0)
                group(0, 0, 0, True, False)
                group(1, 1, 0, False, False)
                with dve.Fori(1, PAIRS - 1) as i:
                    for e in range(2):
                        group(2 * i + e, e, i, False, False)
                group(G_ALL - 2, 0, PAIRS - 1, False, False)
                group(G_ALL - 1, 1, PAIRS - 1, False, True)
                for stage in range(3):
                    invert(G_ALL - 1, 1, stage)
                normalise(G_ALL - 1, 1)

            @block.tensor
            def _(pe):
                def unit(G, e, u, use):
                    n = (UNITS + 1) * G + u
                    j, qt = u // QT, u % QT
                    if qt == 0:
                        pe.wait_ge(qk_loaded[e][j], 96 * use)
                    if not (whole(n) and n < 2):
                        pe.wait_ge(unit_read, n - 1)
                    out = unit_ps[(e + u) % 2]
                    for h in range(2):
                        last = pe.matmul(out[:, h, :], q_st[e][0:ROWS, j, qt * P:(qt + 1) * P],
                                         k_st[e][0:ROWS, j, h * 512:(h + 1) * 512], start=True, stop=True)
                    last.then_inc(unit_done, 1)

                def turn(G, e):
                    pe.wait_ge(unit_read, (UNITS + 1) * G + UNITS)
                    pe.transpose(unit_ps[(e + UNITS) % 2][:, 0, 0:P], maxima[e][:, :], ident[:, :]).then_inc(unit_done, 1)

                def score(G, e, T, j, use):
                    h, k = T // QT, T % QT
                    n = HPG * (STEPS * G + T) + j
                    if T == 0 and j == 0:
                        pe.wait_ge(max_loaded[e], 16 * use)
                    if not (whole(n) and n < 2):
                        pe.wait_ge(exp_done, n - 1)
                    pe.matmul(score_ps[j % 2][:, :], k_st[e][0:ROWS + 1, j, k * P:(k + 1) * P],
                              q_st[e][0:ROWS + 1, j, h * 512:(h + 1) * 512], start=True, stop=True).then_inc(score_done, 1)

                def times_v(G, e, T):
                    h, k = T // QT, T % QT
                    if k == 0 and not (whole(G) and G == 0 and h == 0):
                        pe.wait_ge(pv_read, QH * G + h)
                    pe.wait_ge(exp_done, HPG * (STEPS * G + T + 1))
                    for j in range(HPG):
                        last = pe.matmul(pv_ps[j * HD:(j + 1) * HD, :], v_sb[e][:, k, j * HD:(j + 1) * HD],
                                         probs[T % RING][:, j, :], start=(k == 0), stop=(k == QT - 1),
                                         tile_position=(0, j * HD))
                    last.then_inc(pv_done, 1)

                def denominators(G, h):
                    pe.wait_ge(added, (QT - 1) * (QH * G + h + 1))
                    pe.wait_ge(added_last, (QT - 1) * (QH * G + h + 1))
                    if not (whole(G) and G == 0 and h == 0):
                        pe.wait_ge(recip_done, 3 * (QH * G + h - 1) + 1)
                    for j in range(HPG):
                        last = pe.matmul(den_ps[j * HD:(j + 1) * HD, :], ones[:, :], psum_k[h][:, j, :],
                                         start=True, stop=True, tile_position=(0, j * HD))
                    last.then_inc(den_done, 1)

                def group(G, e, i, first, last):
                    u = 0
                    for T in range(STEPS):
                        if T == 0:
                            pe.wait_ge(v_loaded[e], 16 * (i + 1))
                        n = 0 if last else SPREAD[T]
                        nxt = (G, e, T + 1, i + 1) if T + 1 < STEPS else (G + 1, 1 - e, 0, i + e + 1)
                        go = T + 1 < STEPS or not last
                        for j in range(HPG):
                            if go:
                                score(nxt[0], nxt[1], nxt[2], j, nxt[3])
                            if j == 1:
                                times_v(G, e, T)
                            if j >= 1 and n > 0:
                                unit(G + 1, 1 - e, u, i + e + 1)
                                u, n = u + 1, n - 1
                        if T == TURN_STEP and not last:
                            turn(G + 1, 1 - e)
                        if T == 2 and not first:
                            denominators(G - 1, 1)
                        if T == QT + 2:
                            denominators(G, 0)

                pe.wait_ge(const_ready, 1)
                pe.wait_ge(ident_ready, 2)
                for u in range(UNITS):
                    unit(0, 0, u, 1)
                turn(0, 0)
                for j in range(HPG):
                    score(0, 0, 0, j, 1)
                group(0, 0, 0, True, False)
                group(1, 1, 0, False, False)
                with pe.Fori(1, PAIRS - 1) as i:
                    for e in range(2):
                        group(2 * i + e, e, i, False, False)
                group(G_ALL - 2, 0, PAIRS - 1, False, False)
                group(G_ALL - 1, 1, PAIRS - 1, False, True)
                denominators(G_ALL - 1, 1)


def route(nc, z, a, scr, keep):
    KT, CH, TPC, NCH, D, E, CAP, TOP = z.KT, z.CH, z.TPC, z.NCH, z.D, z.E, z.CAP, z.TOP
    SLOTS = E * CAP
    FAR = 100000.0
    PICKS = TPC * TOP
    with ExitStack() as ctx:
        def sb(name, shape, dt=F32):
            return ctx.enter_context(nc.sbuf_tensor("rt_" + name, shape, dt))

        def sem(name):
            return ctx.enter_context(nc.semaphore("rt_" + name))

        ident = sb("ident", [P, P])
        eps = sb("eps", [P, 1])
        wo_raw = sb("wo_raw", [P, KT, D])
        woT = [sb("woT_hi", [P, KT, D], F32R), sb("woT_lo", [P, KT, D], F32R)]
        rw = sb("rw", [E, D])
        rwT = sb("rwT", [P, KT, E])
        rb = sb("rb", [P, E])
        bo = sb("bo", [P, D])
        gate = sb("gate", [P, 2])
        tanh_g = sb("tanh_g", [P, 2])
        tanh_bo = sb("tanh_bo", [P, D])
        iota_i = sb("iota_i", [P, E], I32)
        iota = sb("iota", [P, E])
        token = sb("token", [P, TPC], I32)
        before_f = sb("before_f", [P, P])
        before = sb("before", [P, P], BF16)
        ones = sb("ones", [P, P], BF16)
        zeros = sb("zeros", [P, SLOTS // P], I32)
        oT_raw = sb("oT_raw", [P, KT, CH])
        oT = [sb("oT_hi", [P, KT, CH], F32R), sb("oT_lo", [P, KT, CH], F32R)]
        x_raw = sb("x_raw", [P, TPC, D])
        xb = sb("xb", [P, TPC, D])
        x1 = sb("x1", [P, TPC, D])
        stats = sb("stats", [P, TPC, 6])
        mv = sb("mv", [P, TPC, 2])
        std = sb("std", [P, TPC])
        rstd = sb("rstd", [P, TPC])
        xn = sb("xn", [P, TPC, D])
        xnT = sb("xnT", [P, KT, CH])
        logits = sb("logits", [P, TPC, E])
        best = sb("best", [P, TPC, 8])
        best_at = sb("best_at", [P, TPC, 8], U32)
        expert = sb("expert", [P, TPC, TOP])
        picked = sb("picked", [P, TPC, TOP, E])
        chosen = sb("chosen", [P, TPC, E], BF16)
        chunk_sum = sb("chunk_sum", [P, E])
        run = sb("run", [P, E])
        run_b = sb("run_b", [P, E], BF16)
        at = sb("at", [P, TPC, TOP, E])
        place = sb("place", [P, TPC, TOP])
        slot = sb("slot", [P, TPC, TOP])
        far = sb("far", [P, TPC, TOP])
        target = sb("target", [P, TPC, TOP], I32)
        value = sb("value", [P, NCH, TPC, TOP])
        kept = sb("kept", [P, NCH, TPC, TOP])
        row_f = sb("row_f", [P, TPC, TOP])
        w_tmp = [sb(f"w_tmp{i}", [P, NCH, TPC]) for i in range(5)]
        w_gk = sb("w_gk", [P, NCH, TPC, TOP])
        y_ps = ctx.enter_context(nc.psum_tensor("rt_y_ps", [P, TPC, 512], F32))
        turned = ctx.enter_context(nc.psum_tensor("rt_turned", [P, 2, 512], F32))
        logit_ps = ctx.enter_context(nc.psum_tensor("rt_logit_ps", [P, 512], F32))
        place_ps = ctx.enter_context(nc.psum_tensor("rt_place_ps", [P, 512], F32))
        logit_v = logit_ps[:, 0:TPC * E].rearrange("p (t e) -> p t e", e=E)
        place_v = place_ps[:, 0:TPC * E].rearrange("p (t e) -> p t e", e=E)

        dve_passed, pool_passed = sem("dve_passed"), sem("pool_passed")
        wo_loaded, small_loaded = sem("wo_loaded"), sem("small_loaded")
        o_loaded, x_loaded = sem("o_loaded"), sem("x_loaded")
        pool_const, dve_const, tanh_ready = sem("pool_const"), sem("dve_const"), sem("tanh_ready")
        table_zeroed = sem("table_zeroed")
        wo_turned, wo_hi, wo_lo = sem("wo_turned"), sem("wo_hi"), sem("wo_lo")
        o_hi, o_lo = sem("o_hi"), sem("o_lo")
        y_done, x1_ready, stats_done = sem("y_done"), sem("x1_ready"), sem("stats_done")
        var_ready, std_ready, rstd_ready = sem("var_ready"), sem("std_ready"), sem("rstd_ready")
        xb_ready, xn_ready = sem("xb_ready"), sem("xn_ready")
        x1_stored, xn_stored = sem("x1_stored"), sem("xn_stored")
        xn_turned, xnT_ready, logits_done = sem("xn_turned"), sem("xnT_ready"), sem("logits_done")
        pick, chosen_ready = sem("pick"), sem("chosen_ready")
        place_done, placed = sem("place_done"), sem("placed")
        scattered, token_next, weigh, exp_ready = sem("scattered"), sem("token_next"), sem("weigh"), sem("exp_ready")

        WU = KT + 1
        PICK, PLACE = 12, 11

        with nc.Block() as block:
            @block.sync
            def _(sp):
                def load(dst, src, c, done):
                    sp.dma_start(dst[:, :, :], src[ds(c * CH, CH), :].rearrange("(t p) c -> p t c", p=P)).then_inc(done, 16)

                def load_o(c):
                    sp.dma_start(oT_raw[:, :, :], scr["o"][:, ds(c * CH, CH)].rearrange("(k p) n -> p k n", p=P)).then_inc(o_loaded, 16)

                def store(dst, src, c, done):
                    sp.dma_start(dst[ds(c * CH, CH), :].rearrange("(t p) c -> p t c", p=P), src[:, :, :]).then_inc(done, 16)

                sp.dma_start(wo_raw[:, :, :], a["Wo"].rearrange("(m p) c -> p m c", p=P)).then_inc(wo_loaded, 16)
                load_o(0)
                load(x_raw, a["x"], 0, x_loaded)
                for dst, src, n in ((rb, "router_b", E), (bo, "bo", D)):
                    sp.dma_start(dst[:, :], a[src].rearrange("(o c) -> o c", o=1).to_broadcast([P, n])).then_inc(small_loaded, 16)
                for i, src in enumerate(("g_xattn", "g_ffn")):
                    sp.dma_start(gate[:, i:i + 1], a[src].rearrange("(o c) -> o c", o=1).to_broadcast([P, 1])).then_inc(small_loaded, 16)
                sp.dma_start(rw[:, :], a["router_w"]).then_inc(small_loaded, 16)
                sp.wait_ge(pool_const, 8)
                sp.dma_start(scr["token_of"].rearrange("(p n) o -> p (n o)", p=P), zeros[:, :]).then_inc(table_zeroed, 16)

                def step(c, more):
                    if more:
                        sp.wait_ge(o_lo, c + 1)
                        load_o(c + 1)
                        sp.wait_ge(xb_ready, TPC * (c + 1))
                        load(x_raw, a["x"], c + 1, x_loaded)
                    sp.wait_ge(x1_ready, TPC * (c + 1))
                    store(scr["x1"], x1, c, x1_stored)
                    sp.wait_ge(xn_ready, TPC * (c + 1))
                    store(scr["xn"], xn, c, xn_stored)

                with sp.Fori(0, NCH - 1) as c:
                    step(c, True)
                step(NCH - 1, False)
                sp.wait_ge(x1_stored, 16 * NCH)
                sp.wait_ge(xn_stored, 16 * NCH)

            @block.gpsimd
            def _(pool):
                pool.memset(eps[:, :], EPS)
                pool.memset(zeros[:, :], 0)
                pool.memset(ones[:, :], 1.0)
                pool.memset(before_f[:, :], 1.0)
                pool.memset(ident[:, :], 0.0)
                pool.iota(iota_i[:, :], [[1, E]], base=0, channel_multiplier=0)
                pool.iota(token[:, :], [[P, TPC]], base=0, channel_multiplier=1).then_inc(pool_const, 6)
                pool.wait_ge(pool_const, 6)
                pool.affine_select(out=ident[:, :], in_=ident[:, :], compare_op=ALU.not_equal, fill=1.0, base=0,
                                   pattern=[[-1, P]], channel_multiplier=1).then_inc(pool_const, 1)
                pool.affine_select(out=before_f[:, :], in_=before_f[:, :], compare_op=ALU.is_gt, fill=0.0, base=0,
                                   pattern=[[1, P]], channel_multiplier=-1).then_inc(pool_const, 1)

                def add_bias(c, first=False):
                    pool.wait_ge(x_loaded, 16 * (c + 1))
                    for t in range(TPC):
                        if not first:
                            pool.wait_ge(x1_ready, TPC * (c - 1) + t + 1)
                            pool.wait_ge(xb_ready, TPC * c + t)
                        elif t:
                            pool.wait_ge(xb_ready, t)
                        pool.tensor_tensor(xb[:, t, :], x_raw[:, t, :], tanh_bo[:, :], ALU.add).then_inc(xb_ready, 1)

                def scatter(c):
                    pool.wait_ge(placed, PLACE * (c + 1))
                    pool.wait_ge(token_next, c)
                    settle(pool, pool_passed)
                    for i in range(PICKS):
                        t, k = i // TOP, i % TOP
                        pool.indirect_dma_start(scr["token_of"], bass.IndirectOffsetOnAxis(target[:, t, k:k + 1], 0),
                                                token[:, t:t + 1], None, bounds_check=SLOTS - 1,
                                                oob_is_err=False).then_inc(scattered, 16)
                    pool.wait_ge(scattered, 16 * PICKS * (c + 1))
                    settle(pool, pool_passed)
                    pool.tensor_scalar(token[:, :], token[:, :], CH, None, ALU.add).then_inc(token_next, 1)

                pool.wait_ge(dve_const, 2)
                add_bias(0, True)
                add_bias(1)
                pool.wait_ge(table_zeroed, 16)
                with pool.Fori(1, NCH - 1) as c:
                    add_bias(c + 1)
                    scatter(c - 1)
                scatter(NCH - 2)
                scatter(NCH - 1)

            @block.scalar
            def _(act):
                act.wait_ge(small_loaded, 80)
                act.activation(tanh_g[:, :], gate[:, :], ACT.Tanh).then_inc(tanh_ready, 1)
                for u in range(KT):
                    act.wait_ge(wo_turned, u + 1)
                    act.activation(woT[0][:, u, :], turned[:, u % 2, :], ACT.Copy).then_inc(wo_hi, 1)
                act.wait_ge(pool_const, 8)

                def split_o(c, first=False):
                    act.wait_ge(o_loaded, 16 * (c + 1))
                    if not first:
                        act.wait_ge(y_done, TPC * c)
                    act.activation(oT[0][:, :, :], oT_raw[:, :, :], ACT.Copy).then_inc(o_hi, 1)

                def std_of(c):
                    act.wait_ge(var_ready, c + 1)
                    act.activation(std[:, :], mv[:, :, 1], ACT.Sqrt, bias=eps[:, 0:1]).then_inc(std_ready, 1)

                def copy_turned(c, first=False):
                    if not first:
                        act.wait_ge(logits_done, c)
                    for t in range(TPC):
                        act.wait_ge(xn_turned, TPC * c + t + 1)
                        act.activation(xnT[:, :, t * P:(t + 1) * P],
                                       turned[:, t % 2, :].rearrange("p (k n) -> p k n", n=P), ACT.Copy).then_inc(xnT_ready, 1)

                split_o(0, True)
                std_of(0)
                split_o(1)
                std_of(1)
                split_o(2)
                copy_turned(0, True)
                with act.Fori(1, NCH - 2) as c:
                    std_of(c + 1)
                    split_o(c + 2)
                    copy_turned(c)
                std_of(NCH - 1)
                copy_turned(NCH - 2)
                copy_turned(NCH - 1)
                act.wait_ge(weigh, 1)
                act.activation(w_tmp[1][:, :, :], w_tmp[0][:, :, :], ACT.Exp).then_inc(exp_ready, 1)

            @block.vector
            def _(dve):
                dve.memset(run[:, :], 0.0)
                dve.memset(run_b[:, :], 0.0)
                dve.wait_ge(tanh_ready, 1)
                dve.tensor_scalar(tanh_bo[:, :], bo[:, :], tanh_g[:, 0:1], None, ALU.mult).then_inc(dve_const, 2)
                dve.wait_ge(pool_const, 8)
                dve.tensor_copy(iota[:, :], iota_i[:, :]).then_inc(dve_const, 1)
                dve.tensor_copy(before[:, :], before_f[:, :]).then_inc(dve_const, 1)
                for u in range(KT):
                    dve.wait_ge(wo_hi, u + 1)
                    dve.tensor_tensor(woT[1][:, u, :], turned[:, u % 2, :], woT[0][:, u, :].bitcast(F32),
                                      ALU.subtract).then_inc(wo_lo, 1)
                dve.wait_ge(wo_turned, WU)
                dve.tensor_copy(rwT[:, :, :], turned[:, KT % 2, 0:KT * E].rearrange("p (k e) -> p k e", e=E)).then_inc(wo_lo, 1)
                dve.wait_ge(dve_const, 4)

                def split_o(c):
                    dve.wait_ge(o_hi, c + 1)
                    dve.tensor_tensor(oT[1][:, :, :], oT_raw[:, :, :], oT[0][:, :, :].bitcast(F32),
                                      ALU.subtract).then_inc(o_lo, 1)

                def normalise(c, first=False):
                    def residual(t):
                        dve.wait_ge(y_done, TPC * c + t + 1)
                        dve.wait_ge(xb_ready, TPC * c + t + 1)
                        dve.scalar_tensor_tensor(out=x1[:, t, :], in0=y_ps[:, t, :], scalar=tanh_g[:, 0:1], in1=xb[:, t, :],
                                                 op0=ALU.mult, op1=ALU.add).then_inc(x1_ready, 1)

                    def statistics(t):
                        dve.wait_ge(x1_ready, TPC * c + t + 1)
                        dve.bn_stats(stats[:, t, :], x1[:, t, :]).then_inc(stats_done, 1)

                    dve.wait_ge(x1_stored, 16 * c)
                    residual(0)
                    for t in range(1, TPC):
                        residual(t)
                        statistics(t - 1)
                    statistics(TPC - 1)
                    dve.wait_ge(stats_done, TPC * (c + 1))
                    settle(dve, dve_passed)
                    for t in range(TPC):
                        last = dve.bn_aggr(mv[:, t, :], stats[:, t, :])
                    last.then_inc(var_ready, 1)
                    dve.wait_ge(std_ready, c + 1)
                    dve.reciprocal(rstd[:, :], std[:, :]).then_inc(rstd_ready, 1)
                    dve.wait_ge(rstd_ready, c + 1)
                    dve.wait_ge(xn_stored, 16 * c)
                    if not first:
                        dve.wait_ge(xn_turned, TPC * c)
                    for t in range(TPC):
                        dve.tensor_scalar(xn[:, t, :], x1[:, t, :], mv[:, t, 0:1], rstd[:, t:t + 1],
                                          ALU.subtract, ALU.mult).then_inc(xn_ready, 1)

                def choose(c):
                    n = PICK * c
                    dve.wait_ge(logits_done, c + 1)
                    dve.tensor_tensor(logits[:, :, :], logit_v, rb[:, :].unsqueeze(1).to_broadcast([P, TPC, E]),
                                      ALU.add).then_inc(pick, 1)
                    dve.wait_ge(pick, n + 1)
                    settle(dve, dve_passed)
                    for t in range(TPC):
                        dve.max(best[:, t, :], logits[:, t, :]).then_inc(pick, 1)
                    for t in range(TPC):
                        dve.wait_ge(pick, n + 2 + t)
                        settle(dve, dve_passed)
                        dve.max_index(best_at[:, t, :], best[:, t, :], logits[:, t, :]).then_inc(pick, 1)
                    dve.wait_ge(pick, n + 9)
                    dve.tensor_copy(value[:, ds(c, 1), :, :].rearrange("p o t k -> p (o t) k"), best[:, :, 0:TOP])
                    dve.tensor_copy(expert[:, :, :], best_at[:, :, 0:TOP]).then_inc(pick, 1)
                    dve.wait_ge(pick, n + 10)
                    dve.tensor_tensor(picked[:, :, :, :].rearrange("p t k e -> p (t k) e"),
                                      iota[:, :].unsqueeze(1).to_broadcast([P, PICKS, E]),
                                      expert[:, :, :].rearrange("p t k -> p (t k)").unsqueeze(2).to_broadcast([P, PICKS, E]),
                                      ALU.is_equal).then_inc(pick, 1)
                    dve.wait_ge(pick, n + 11)
                    dve.tensor_tensor(chosen[:, :, :], picked[:, :, 0, :], picked[:, :, 1, :], ALU.add).then_inc(pick, 1)

                def assign(c):
                    n = PLACE * c
                    dve.wait_ge(place_done, c + 1)
                    dve.tensor_reduce(chunk_sum[:, :], chosen[:, :, :].rearrange("p t e -> p e t"), AX_X, ALU.add).then_inc(placed, 1)
                    for k in range(TOP):
                        dve.tensor_tensor(at[:, :, k, :], picked[:, :, k, :], place_v, ALU.mult).then_inc(placed, 1)
                    dve.wait_ge(placed, n + 1)
                    dve.tensor_tensor(run[:, :], run[:, :], chunk_sum[:, :], ALU.add).then_inc(placed, 1)
                    dve.wait_ge(placed, n + 3)
                    dve.tensor_reduce(place[:, :, :].rearrange("p t k -> p (t k)"),
                                      at[:, :, :, :].rearrange("p t k e -> p (t k) e"), AX_X, ALU.add).then_inc(placed, 1)
                    dve.wait_ge(placed, n + 4)
                    dve.tensor_copy(run_b[:, :], run[:, :]).then_inc(placed, 1)
                    dve.wait_ge(placed, n + 5)
                    dve.scalar_tensor_tensor(out=slot[:, :, :], in0=expert[:, :, :], scalar=float(CAP), in1=place[:, :, :],
                                             op0=ALU.mult, op1=ALU.add).then_inc(placed, 1)
                    dve.tensor_scalar(far[:, :, :], place[:, :, :], float(CAP), FAR, ALU.is_ge, ALU.mult).then_inc(placed, 1)
                    dve.tensor_scalar(kept[:, ds(c, 1), :, :].rearrange("p o t k -> p (o t) k"), place[:, :, :], float(CAP), None,
                                      ALU.is_lt).then_inc(placed, 1)
                    dve.wait_ge(scattered, 16 * PICKS * c)
                    dve.wait_ge(placed, n + 8)
                    dve.tensor_tensor(target[:, :, :], slot[:, :, :], far[:, :, :], ALU.add).then_inc(placed, 1)
                    dve.tensor_scalar(keep["row"][:, ds(c, 1), :, :].rearrange("p o t k -> p (o t) k"), slot[:, :, :],
                                      float(SLOTS - 1), None, ALU.min).then_inc(placed, 1)

                split_o(0)
                normalise(0, True)
                split_o(1)
                normalise(1)
                split_o(2)
                choose(0)
                with dve.Fori(1, NCH - 2) as c:
                    assign(c - 1)
                    normalise(c + 1)
                    split_o(c + 2)
                    choose(c)
                assign(NCH - 3)
                normalise(NCH - 1)
                choose(NCH - 2)
                assign(NCH - 2)
                choose(NCH - 1)
                assign(NCH - 1)

                diff, ex, total, inv, den = w_tmp
                v0, v1 = value[:, :, :, 0], value[:, :, :, 1]
                dve.wait_ge(placed, PLACE * NCH)
                dve.tensor_tensor(diff[:, :, :], v1, v0, ALU.subtract).then_inc(weigh, 1)
                dve.wait_ge(exp_ready, 1)
                dve.tensor_scalar(total[:, :, :], ex[:, :, :], 1.0, None, ALU.add).then_inc(weigh, 1)
                dve.wait_ge(weigh, 2)
                dve.reciprocal(inv[:, :, :], total[:, :, :]).then_inc(weigh, 1)
                dve.wait_ge(weigh, 3)
                dve.tensor_tensor(w_gk[:, :, :, 0], inv[:, :, :], kept[:, :, :, 0], ALU.mult).then_inc(weigh, 1)
                dve.tensor_tensor(total[:, :, :], ex[:, :, :], inv[:, :, :], ALU.mult).then_inc(weigh, 1)
                dve.wait_ge(weigh, 5)
                dve.tensor_tensor(w_gk[:, :, :, 1], total[:, :, :], kept[:, :, :, 1], ALU.mult).then_inc(weigh, 1)
                dve.wait_ge(weigh, 6)
                dve.scalar_tensor_tensor(out=den[:, :, :], in0=w_gk[:, :, :, 0], scalar=1e-9, in1=w_gk[:, :, :, 1],
                                         op0=ALU.add, op1=ALU.add).then_inc(weigh, 1)
                dve.wait_ge(weigh, 7)
                dve.reciprocal(inv[:, :, :], den[:, :, :]).then_inc(weigh, 1)
                dve.wait_ge(weigh, 8)
                for k in range(TOP):
                    dve.scalar_tensor_tensor(out=keep["weight"][:, :, :, k], in0=w_gk[:, :, :, k], scalar=tanh_g[:, 1:2],
                                             in1=inv[:, :, :], op0=ALU.mult, op1=ALU.mult).then_inc(weigh, 1)

            @block.tensor
            def _(pe):
                pe.wait_ge(pool_const, 8)
                pe.wait_ge(wo_loaded, 16)
                for u in range(KT):
                    if u >= 2:
                        pe.wait_ge(wo_lo, u - 1)
                    for m in range(KT):
                        last = pe.transpose(turned[:, u % 2, m * P:(m + 1) * P], wo_raw[:, m, u * P:(u + 1) * P], ident[:, :])
                    last.then_inc(wo_turned, 1)
                pe.wait_ge(wo_lo, KT - 1)
                pe.wait_ge(small_loaded, 80)
                for k in range(KT):
                    last = pe.transpose(turned[:, KT % 2, k * E:(k + 1) * E], rw[:, k * P:(k + 1) * P], ident[0:E, 0:E])
                last.then_inc(wo_turned, 1)
                pe.wait_ge(wo_lo, WU)
                pe.wait_ge(dve_const, 4)

                def product(c, first=False):
                    pe.wait_ge(o_lo, c + 1)
                    for t in range(TPC):
                        if not first:
                            pe.wait_ge(x1_ready, TPC * (c - 1) + t + 1)
                        for k in range(KT):
                            last = split_matmul(pe, y_ps[:, t, :], oT[0][:, k, t * P:(t + 1) * P], oT[1][:, k, t * P:(t + 1) * P],
                                                woT[0][:, k, :], woT[1][:, k, :], k == 0, k == KT - 1)
                        last.then_inc(y_done, 1)

                def turn_and_score(c, first=False):
                    for t in range(TPC):
                        pe.wait_ge(xn_ready, TPC * c + t + 1)
                        if not first or t >= 2:
                            pe.wait_ge(xnT_ready, TPC * c + t - 1)
                        for k in range(KT):
                            last = pe.transpose(turned[:, t % 2, k * P:(k + 1) * P], xn[:, t, k * P:(k + 1) * P], ident[:, :])
                        last.then_inc(xn_turned, 1)
                    if not first:
                        pe.wait_ge(pick, PICK * (c - 1) + 1)
                    for t in range(TPC):
                        pe.wait_ge(xnT_ready, TPC * c + t + 1)
                        for k in range(KT):
                            last = pe.matmul(logit_ps[:, t * E:(t + 1) * E], xnT[:, k, t * P:(t + 1) * P], rwT[:, k, :],
                                             start=(k == 0), stop=(k == KT - 1))
                    last.then_inc(logits_done, 1)

                def places(c):
                    pe.wait_ge(pick, PICK * (c + 1))
                    if not isinstance(c, int) or c > 0:
                        pe.wait_ge(placed, PLACE * c)
                    for t in range(TPC):
                        out = place_ps[:, t * E:(t + 1) * E]
                        pe.matmul(out, before[:, :], chosen[:, t, :], start=True, stop=False)
                        for s in range(t):
                            pe.matmul(out, ones[:, :], chosen[:, s, :], start=False, stop=False)
                        last = pe.matmul(out, ones[:, :], run_b[:, :], start=False, stop=True)
                    last.then_inc(place_done, 1)

                product(0, True)
                product(1)
                turn_and_score(0, True)
                with pe.Fori(1, NCH - 1) as c:
                    places(c - 1)
                    product(c + 1)
                    turn_and_score(c)
                places(NCH - 2)
                turn_and_score(NCH - 1)
                places(NCH - 1)


def run_experts(nc, z, a, scr):
    KT, D, E, CAP, F = z.KT, z.D, z.E, z.CAP, z.F
    FT = F // P
    ST = CAP // P
    HALF = CAP // 2
    WC = 4
    NC = FT // WC
    RING = 4
    AHEAD = 3
    X_STEPS = tuple(range(3, 3 + 2 * ST, 2))
    PAIRS = E // 2
    with ExitStack() as ctx:
        def sb(name, shape, dt=F32):
            return ctx.enter_context(nc.sbuf_tensor("ex_" + name, shape, dt))

        def sem(name):
            return ctx.enter_context(nc.semaphore("ex_" + name))

        ident = sb("ident", [P, P])
        b1_raw = sb("b1_raw", [P, 2, P])
        b1T = sb("b1T", [P, E * FT])
        index = [sb(f"index{i}", [P, ST], I32) for i in range(2)]
        rows = [sb(f"rows{i}", [P, ST, D]) for i in range(2)]
        xT_hi = [sb(f"xT_hi{i}", [P, KT, CAP], F32R) for i in range(2)]
        xT_lo = [sb(f"xT_lo{i}", [P, KT, CAP], F32R) for i in range(2)]
        w1_raw = [sb(f"w1_raw{i}", [P, KT, WC * P]) for i in range(NC)]
        w2_raw = [sb(f"w2_raw{i}", [P, WC, D]) for i in range(NC)]
        w1_hi = [sb(f"w1_hi{i}", [P, KT, P], F32R) for i in range(RING)]
        w1_lo = [sb(f"w1_lo{i}", [P, KT, P], F32R) for i in range(RING)]
        w2_hi = [sb(f"w2_hi{i}", [P, D], F32R) for i in range(RING)]
        w2_lo = [sb(f"w2_lo{i}", [P, D], F32R) for i in range(RING)]
        hid = [sb(f"hid{i}", [P, CAP]) for i in range(2)]
        hid_hi = [sb(f"hid_hi{i}", [P, CAP], F32R) for i in range(2)]
        hid_lo = [sb(f"hid_lo{i}", [P, CAP], F32R) for i in range(2)]
        b2 = [sb(f"b2_{i}", [P, D]) for i in range(2)]
        result = sb("result", [P, ST, D])
        acc = ctx.enter_context(nc.psum_tensor("ex_acc", [P, ST, 512], F32))
        first_ps = [ctx.enter_context(nc.psum_tensor(f"ex_first{i}", [P, 512], F32)) for i in range(2)]
        turned = ctx.enter_context(nc.psum_tensor("ex_turned", [P, 512], F32))

        act_passed, pool_passed = sem("act_passed"), sem("pool_passed")
        ident_ready, b1_loaded, b1_turned, b1_ready = sem("ident_ready"), sem("b1_loaded"), sem("b1_turned"), sem("b1_ready")
        w1_loaded = [sem(f"w1_loaded{i}") for i in range(NC)]
        w2_loaded = [sem(f"w2_loaded{i}") for i in range(NC)]
        w_hi, w_lo = sem("w_hi"), sem("w_lo")
        w_free = sem("w_free")
        index_loaded = [sem(f"index_loaded{i}") for i in range(2)]
        gathered = [sem(f"gathered{i}") for i in range(2)]
        x_turned, x_hi, x_lo = sem("x_turned"), sem("x_hi"), sem("x_lo")
        first_done = sem("first_done")
        first_free = sem("first_free")
        hid_free = sem("hid_free")
        hid_hi_done, hid_ready = sem("hid_hi_done"), sem("hid_ready")
        acc_done = sem("acc_done")
        acc_free = sem("acc_free")
        b2_loaded = [sem(f"b2_loaded{i}") for i in range(2)]
        stored = sem("stored")

        with nc.Block() as block:
            @block.sync
            def _(sp):
                w1_v = a["w1"].rearrange("e (k p) f -> p (e k) f", p=P)
                w2_v = a["w2"].rearrange("e (t p) d -> p (e t) d", p=P)

                def load(e, c):
                    sp.dma_start(w1_raw[c][:, :, :], w1_v[:, ds(KT * e, KT), c * WC * P:(c + 1) * WC * P]).then_inc(w1_loaded[c], 16)
                    sp.dma_start(w2_raw[c][:, :, :], w2_v[:, ds(FT * e + WC * c, WC), :]).then_inc(w2_loaded[c], 16)

                def store(e):
                    sp.wait_ge(acc_free, ST * (e + 2))
                    sp.dma_start(scr["eout"][ds(CAP * e, CAP), :].rearrange("(s p) c -> p s c", p=P),
                                 result[:, :, :]).then_inc(stored, 16)

                sp.dma_start(b1_raw[:, :, :], a["b1"].rearrange("(h e) (t p) -> (e t) h p", h=2, p=P)).then_inc(b1_loaded, 16)
                for c in range(NC):
                    load(0, c)

                def step(e, first=False):
                    for c in range(NC):
                        sp.wait_ge(w_lo, FT * (e - 1) + WC * (c + 1))
                        load(e, c)
                        if c == 0 and not first:
                            store(e - 2)

                step(1, True)
                with sp.Fori(2, E) as e:
                    step(e)
                store(E - 2)
                store(E - 1)
                sp.wait_ge(stored, 16 * E)

            @block.gpsimd
            def _(pool):
                make_identity(nc, pool, ident, ident_ready)

                def gather(e, i, use):
                    pool.dma_start(index[i][:, :], scr["token_of"][ds(CAP * e, CAP), :].rearrange("(s p) o -> p (s o)", p=P)
                                   ).then_inc(index_loaded[i], 16)
                    pool.wait_ge(index_loaded[i], 16 * (use + 1))
                    settle(pool, pool_passed)
                    for s in range(ST):
                        pool.indirect_dma_start(rows[i][:, s, :], None, scr["xn"],
                                                bass.IndirectOffsetOnAxis(index[i][:, s:s + 1], 0),
                                                bounds_check=z.TOK - 1, oob_is_err=False).then_inc(gathered[i], 16)

                def load_b2(e, i):
                    pool.dma_start(b2[i][:, :], a["b2"][ds(e, 1), :].to_broadcast([P, D])).then_inc(b2_loaded[i], 16)

                with nc.allow_non_contiguous_dma(reason="640 slot numbers"):
                    for i in range(2):
                        gather(i, i, 0)
                        load_b2(i, i)
                    with pool.Fori(1, PAIRS) as j:
                        for i in range(2):
                            e = 2 * j + i
                            pool.wait_ge(gathered[i], 16 * ST * j)
                            pool.wait_ge(x_turned, ST * (e - 1))
                            gather(e, i, j)
                            pool.wait_ge(acc_free, ST * e)
                            load_b2(e, i)

            @block.scalar
            def _(act):
                def split_w(e, f):
                    c, r = f // WC, f % RING
                    if f % WC == 0:
                        act.wait_ge(w1_loaded[c], 16 * (e + 1))
                        act.wait_ge(w2_loaded[c], 16 * (e + 1))
                    act.wait_ge(w_free, FT * e + f + 1)
                    act.activation(w1_hi[r][:, :, :], w1_raw[c][:, :, (f % WC) * P:(f % WC + 1) * P], ACT.Copy)
                    act.activation(w2_hi[r][:, :], w2_raw[c][:, f % WC, :], ACT.Copy).then_inc(w_hi, 1)

                def split_x(e, i, s):
                    act.wait_ge(x_turned, ST * e + s + 1)
                    act.activation(xT_hi[i][:, :, s * P:(s + 1) * P], turned[:, :].rearrange("p (k n) -> p k n", n=P),
                                   ACT.Copy).then_inc(x_hi, 1)

                def gelu(e, f):
                    act.wait_ge(hid_free, FT * e + f + 1)
                    for h in range(2):
                        act.wait_ge(first_done, 2 * (FT * e + f) + h + 1)
                        settle(act, act_passed)
                        act.activation(hid[f % 2][:, h * HALF:(h + 1) * HALF], first_ps[h][:, 0:HALF], ACT.Gelu,
                                       bias=b1T[:, ds(FT * e + f, 1)]).then_inc(first_free, 1)

                def expert(e, i, last):
                    for f in range(FT):
                        if not (last and f + AHEAD >= FT):
                            split_w(e + (f + AHEAD) // FT, (f + AHEAD) % FT)
                        if not (last and f + 1 >= FT):
                            gelu(e + (f + 1) // FT, (f + 1) % FT)
                        if f in X_STEPS and not last:
                            split_x(e + 1, 1 - i, X_STEPS.index(f))

                for s in range(ST):
                    split_x(0, 0, s)
                for f in range(AHEAD):
                    split_w(0, f)
                act.wait_ge(b1_ready, 1)
                gelu(0, 0)
                with act.Fori(0, PAIRS - 1) as j:
                    for i in range(2):
                        expert(2 * j + i, i, False)
                expert(E - 2, 0, False)
                expert(E - 1, 1, True)

            @block.vector
            def _(dve):
                def split_w(e, f):
                    c, r = f // WC, f % RING
                    dve.wait_ge(w_hi, FT * e + f + 1)
                    dve.tensor_tensor(w1_lo[r][:, :, :], w1_raw[c][:, :, (f % WC) * P:(f % WC + 1) * P],
                                      w1_hi[r][:, :, :].bitcast(F32), ALU.subtract)
                    dve.tensor_tensor(w2_lo[r][:, :], w2_raw[c][:, f % WC, :], w2_hi[r][:, :].bitcast(F32),
                                      ALU.subtract).then_inc(w_lo, 1)

                def split_x(e, i, s):
                    dve.wait_ge(x_hi, ST * e + s + 1)
                    dve.tensor_tensor(xT_lo[i][:, :, s * P:(s + 1) * P], turned[:, :].rearrange("p (k n) -> p k n", n=P),
                                      xT_hi[i][:, :, s * P:(s + 1) * P].bitcast(F32), ALU.subtract).then_inc(x_lo, 1)

                def split_hid(e, f):
                    n, r = FT * e + f, f % 2
                    dve.wait_ge(first_free, 2 * n + 4)
                    dve.wait_ge(w_free, n + RING - 1)
                    dve.tensor_copy(hid_hi[r][:, :], hid[r][:, :]).then_inc(hid_hi_done, 1)
                    dve.wait_ge(hid_hi_done, n + 1)
                    dve.tensor_tensor(hid_lo[r][:, :], hid[r][:, :], hid_hi[r][:, :].bitcast(F32), ALU.subtract).then_inc(hid_free, 1)

                def finish(e, i, use):
                    dve.wait_ge(b2_loaded[i], 16 * (use + 1))
                    dve.wait_ge(stored, 16 * e)
                    for s in range(ST):
                        if s < ST - 1:
                            dve.wait_ge(acc_done, (ST - 1) * e + s + 1)
                        else:
                            dve.wait_ge(w_free, RING + FT * (e + 1))
                        dve.tensor_tensor(result[:, s, :], acc[:, s, :], b2[i][:, :], ALU.add).then_inc(acc_free, 1)

                def expert(e, i, j, first, last):
                    for f in range(FT):
                        if f == 0 and not first:
                            finish(e - 1, 1 - i, j - 1 + i)
                        if not (last and f + AHEAD >= FT):
                            split_w(e + (f + AHEAD) // FT, (f + AHEAD) % FT)
                        if not (last and f + 1 >= FT):
                            split_hid(e + (f + 1) // FT, (f + 1) % FT)
                        if f in X_STEPS and not last:
                            split_x(e + 1, 1 - i, X_STEPS.index(f))

                dve.memset(result[:, 0, 0:1], 0.0).then_inc(acc_free, ST)
                dve.memset(result[:, 0, 1:2], 0.0).then_inc(first_free, 2)
                dve.memset(result[:, 0, 2:3], 0.0).then_inc(hid_free, 2)
                dve.memset(result[:, 0, 3:4], 0.0).then_inc(w_free, RING)
                dve.wait_ge(b1_turned, 1)
                dve.tensor_copy(b1T[:, :], turned[:, 0:2 * P]).then_inc(b1_ready, 1)
                for s in range(ST):
                    split_x(0, 0, s)
                for f in range(AHEAD):
                    split_w(0, f)
                split_hid(0, 0)
                expert(0, 0, 0, True, False)
                expert(1, 1, 0, False, False)
                with dve.Fori(1, PAIRS - 1) as j:
                    for i in range(2):
                        expert(2 * j + i, i, j, False, False)
                expert(E - 2, 0, PAIRS - 1, False, False)
                expert(E - 1, 1, PAIRS - 1, False, True)
                finish(E - 1, 1, PAIRS - 1)

            @block.tensor
            def _(pe):
                def turn(e, i, s, use):
                    if s == 0:
                        pe.wait_ge(gathered[i], 16 * ST * (use + 1))
                    pe.wait_ge(x_lo, ST * e + s)
                    for k in range(KT):
                        last = pe.transpose(turned[:, k * P:(k + 1) * P], rows[i][:, s, k * P:(k + 1) * P], ident[:, :])
                    last.then_inc(x_turned, 1)

                def first(e, i, f):
                    n, r = FT * e + f, f % RING
                    pe.wait_ge(w_lo, n + 1)
                    if f == 0:
                        pe.wait_ge(x_lo, ST * (e + 1))
                    for h in range(2):
                        pe.wait_ge(first_free, 2 * n + h + 1)
                        sl = slice(h * HALF, (h + 1) * HALF)
                        for k in range(KT):
                            last = split_matmul(pe, first_ps[h][:, 0:HALF], w1_hi[r][:, k, :], w1_lo[r][:, k, :],
                                                xT_hi[i][:, k, sl], xT_lo[i][:, k, sl], k == 0, k == KT - 1)
                        last.then_inc(first_done, 1)

                def second(e, f):
                    n, r = FT * e + f, f % RING
                    pe.wait_ge(hid_free, n + 3)
                    for s in range(ST):
                        if f == 0:
                            pe.wait_ge(acc_free, ST * e + s + 1)
                        sl = slice(s * P, (s + 1) * P)
                        last = split_matmul(pe, acc[:, s, :], hid_hi[f % 2][:, sl], hid_lo[f % 2][:, sl],
                                            w2_hi[r][:, :], w2_lo[r][:, :], f == 0, f == FT - 1)
                        if f == FT - 1 and s < ST - 1:
                            last.then_inc(acc_done, 1)
                    last.then_inc(w_free, 1)

                def expert(e, i, j, last):
                    for f in range(FT):
                        if not (last and f + 1 >= FT):
                            first(e + (f + 1) // FT, (i + (f + 1) // FT) % 2, (f + 1) % FT)
                        if f in X_STEPS and not last:
                            turn(e + 1, 1 - i, X_STEPS.index(f), j + i)
                        second(e, f)

                pe.wait_ge(ident_ready, 2)
                pe.wait_ge(b1_loaded, 16)
                for h in range(2):
                    last = pe.transpose(turned[:, h * P:(h + 1) * P], b1_raw[:, h, :], ident[:, :])
                last.then_inc(b1_turned, 1)
                pe.wait_ge(b1_ready, 1)
                for s in range(ST):
                    turn(0, 0, s, 0)
                first(0, 0, 0)
                with pe.Fori(0, PAIRS - 1) as j:
                    for i in range(2):
                        expert(2 * j + i, i, j, False)
                expert(E - 2, 0, PAIRS - 1, False)
                expert(E - 1, 1, PAIRS - 1, True)


def combine(nc, z, out, scr, keep):
    CH, TPC, NCH, D, TOP = z.CH, z.TPC, z.NCH, z.D, z.TOP
    PICKS = TPC * TOP
    with ExitStack() as ctx:
        def sb(name, shape, dt=F32):
            return [ctx.enter_context(nc.sbuf_tensor(f"cb_{name}{i}", shape, dt)) for i in range(2)]

        def sem(name):
            return ctx.enter_context(nc.semaphore("cb_" + name))

        row = sb("row", [P, TPC, TOP], I32)
        weight = sb("weight", [P, TPC, TOP])
        rows = sb("rows", [P, PICKS, D])
        x1 = sb("x1", [P, TPC, D])
        part = sb("part", [P, TPC, D])
        result = sb("result", [P, TPC, D])

        pool_passed = sem("pool_passed")
        copied = sem("copied")
        gathered = [sem("gathered0"), sem("gathered1")]
        x1_loaded = [sem("x1_loaded0"), sem("x1_loaded1")]
        first_added, second_added = sem("first_added"), sem("second_added")
        stored = [sem("stored0"), sem("stored1")]

        with nc.Block() as block:
            @block.sync
            def _(sp):
                def load(c, i):
                    sp.dma_start(x1[i][:, :, :], scr["x1"][ds(c * CH, CH), :].rearrange("(t p) c -> p t c", p=P)).then_inc(x1_loaded[i], 16)

                def store(c, i):
                    sp.wait_ge(second_added, TPC * (c + 1))
                    sp.dma_start(out[ds(c * CH, CH), :].rearrange("(t p) c -> p t c", p=P), result[i][:, :, :]).then_inc(stored[i], 16)

                for i in range(2):
                    load(i, i)
                with sp.Fori(1, NCH // 2) as j:
                    for i in range(2):
                        c = 2 * j + i
                        store(c - 2, i)
                        load(c, i)
                for i in range(2):
                    store(NCH - 2 + i, i)
                for i in range(2):
                    sp.wait_ge(stored[i], 16 * NCH // 2)

            @block.gpsimd
            def _(pool):
                def gather(c, i, first=False):
                    pool.wait_ge(copied, 2 * (c + 1))
                    for n in range(PICKS):
                        t, k = n // TOP, n % TOP
                        if not first:
                            pool.wait_ge(second_added, TPC * (c - 2) + t + 1)
                            settle(pool, pool_passed)
                        pool.indirect_dma_start(rows[i][:, n, :], None, scr["eout"],
                                                bass.IndirectOffsetOnAxis(row[i][:, t, k:k + 1], 0),
                                                bounds_check=z.E * z.CAP - 1, oob_is_err=False).then_inc(gathered[i], 16)

                gather(0, 0, True)
                gather(1, 1, True)
                with pool.Fori(1, NCH // 2) as j:
                    for i in range(2):
                        gather(2 * j + i, i)

            @block.vector
            def _(dve):
                def copy(c, i):
                    dve.tensor_copy(row[i][:, :, :], keep["row"][:, ds(c, 1), :, :].rearrange("p o t k -> p (o t) k")).then_inc(copied, 1)
                    dve.tensor_copy(weight[i][:, :, :], keep["weight"][:, ds(c, 1), :, :].rearrange("p o t k -> p (o t) k")).then_inc(copied, 1)

                def add(c, i, use):
                    dve.wait_ge(gathered[i], 16 * PICKS * (use + 1))
                    dve.wait_ge(x1_loaded[i], 16 * (use + 1))
                    dve.wait_ge(stored[i], 16 * use)
                    dve.wait_ge(copied, 2 * (c + 1))
                    for t in range(TPC):
                        dve.scalar_tensor_tensor(out=part[i][:, t, :], in0=rows[i][:, TOP * t, :], scalar=weight[i][:, t, 0:1],
                                                 in1=x1[i][:, t, :], op0=ALU.mult, op1=ALU.add).then_inc(first_added, 1)
                        if t:
                            second(c, i, t - 1)
                    second(c, i, TPC - 1)

                def second(c, i, t):
                    dve.wait_ge(first_added, TPC * c + t + 1)
                    dve.scalar_tensor_tensor(out=result[i][:, t, :], in0=rows[i][:, TOP * t + 1, :], scalar=weight[i][:, t, 1:2],
                                             in1=part[i][:, t, :], op0=ALU.mult, op1=ALU.add).then_inc(second_added, 1)

                for i in range(2):
                    copy(i, i)
                with dve.Fori(0, NCH // 2 - 1) as j:
                    for i in range(2):
                        c = 2 * j + i
                        add(c, i, j)
                        dve.wait_ge(second_added, TPC * (c + 1))
                        copy(c + 2, i)
                for i in range(2):
                    add(NCH - 2 + i, i, NCH // 2 - 1)


INPUTS = ("x", "ctx_1024", "g_xattn", "g_ffn", "L0_xattn_Wq", "L0_xattn_bq", "L0_xattn_Wk", "L0_xattn_bk",
          "L0_xattn_Wv", "L0_xattn_bv", "L0_xattn_Wo", "L0_xattn_bo", "L0_ffn_router_w", "L0_ffn_router_b",
          "L0_ffn_w1", "L0_ffn_b1", "L0_ffn_w2", "L0_ffn_b2")


def gated_attention_and_experts(nc, z, a, out):
    def dram(name, shape, dt=F32):
        return nc.dram_tensor(name, shape, dt).ap()

    scr = dict(qk=dram("scr_qk", [2, 2, z.KT, P, z.TOK]),
               v=dram("scr_v", [z.TOK, z.D]),
               o=dram("scr_o", [z.D, z.TOK]),
               x1=dram("scr_x1", [z.TOK, z.D]),
               xn=dram("scr_xn", [z.TOK, z.D]),
               token_of=dram("scr_token_of", [z.E * z.CAP, 1], I32),
               eout=dram("scr_eout", [z.E * z.CAP, z.D]))
    project_inputs(nc, z, a, scr)
    attend(nc, z, scr)
    with nc.sbuf_tensor("keep_row", [P, z.NCH, z.TPC, z.TOP], I32) as row, \
            nc.sbuf_tensor("keep_weight", [P, z.NCH, z.TPC, z.TOP], F32) as weight:
        keep = dict(row=row, weight=weight)
        route(nc, z, a, scr, keep)
        run_experts(nc, z, a, scr)
        combine(nc, z, out, scr, keep)


def kernel(**inputs):
    import numpy as np
    from concourse import bacc
    from concourse.bass_utils import run_bass_kernel_spmd

    nc = bacc.Bacc("TRN2", target_bir_lowering=False, num_devices=1)
    z = Shapes(inputs["x"], inputs["L0_ffn_w1"])
    arrays, a = {}, {}
    for name in INPUTS:
        v = np.ascontiguousarray(inputs[name])
        if name in ("x", "ctx_1024"):
            v = v.reshape(z.TOK, z.D)
        arrays[name] = v
        short = {"ctx_1024": "ctx"}.get(name, name.removeprefix("L0_xattn_").removeprefix("L0_ffn_"))
        a[short] = nc.dram_tensor(name, v.shape, mybir.dt.from_np(v.dtype), kind="ExternalInput").ap()
    out = nc.dram_tensor("out", (z.TOK, z.D), F32, kind="ExternalOutput").ap()
    gated_attention_and_experts(nc, z, a, out)
    result = run_bass_kernel_spmd(nc, [arrays], core_ids=[0])
    return result.results[0]["out"].reshape(z.B, z.S, z.D)
```

```python
from contextlib import ExitStack

import concourse.bass as bass
from concourse import mybir

F32 = mybir.dt.float32
F32R = mybir.dt.float32r
BF16 = mybir.dt.bfloat16
I32 = mybir.dt.int32
U32 = mybir.dt.uint32
ALU = mybir.AluOpType
ACT = mybir.ActivationFunctionType
AX_X = mybir.AxisListType.X
ds = bass.ds

P = 128
EPS = 1e-5


class Shapes:

    def __init__(self, x, w1):
        self.B, self.S, self.D = x.shape
        self.E, _, self.F = w1.shape
        self.H = 16
        self.HD = self.D // self.H
        self.TOP = 2
        self.TOK = self.B * self.S
        self.CAP = -(-5 * self.TOK * self.TOP // (4 * self.E))
        self.KT = self.D // P
        self.CH = 512
        self.NCH = self.TOK // self.CH
        self.TPC = self.CH // P
        self.NT = self.TOK // P


def split_matmul(pe, out, w_hi, w_lo, m_hi, m_lo, first, last):
    pe.matmul(out, w_hi, m_hi, start=first, stop=False)
    pe.matmul(out, w_hi, m_lo, start=False, stop=False)
    return pe.matmul(out, w_lo, m_hi, start=False, stop=last)


def settle(engine, passed):
    engine.sem_inc(passed, 1)


def make_identity(nc, pool, ident, ready):
    pool.memset(ident[:, :], 0.0).then_inc(ready, 1)
    pool.wait_ge(ready, 1)
    pool.affine_select(out=ident[:, :], in_=ident[:, :], compare_op=ALU.not_equal, fill=1.0, base=0,
                       pattern=[[-1, P]], channel_multiplier=1).then_inc(ready, 1)


def project_inputs(nc, z, a, scr):
    KT, CH, TPC, NCH, D = z.KT, z.CH, z.TPC, z.NCH, z.D
    with ExitStack() as ctx:
        def sb(name, shape, dt=F32):
            return ctx.enter_context(nc.sbuf_tensor(name, shape, dt))

        def sem(name):
            return ctx.enter_context(nc.semaphore(name))

        ident = sb("pi_ident", [P, P])
        eps = sb("pi_eps", [P, 1])
        w_raw = sb("pi_w_raw", [P, 3, KT, D])
        wT_hi = sb("pi_wT_hi", [P, 3, KT, D], F32R)
        wT_lo = sb("pi_wT_lo", [P, 3, KT, D], F32R)
        b_qk = sb("pi_b_qk", [P, 2, KT])
        b_v = sb("pi_b_v", [P, D])
        x_raw = sb("pi_x_raw", [P, TPC, D])
        c_raw = sb("pi_c_raw", [P, TPC, D])
        xn = sb("pi_xn", [P, TPC, D])
        stats = sb("pi_stats", [P, TPC, 6])
        mv = sb("pi_mv", [P, TPC, 2])
        std = sb("pi_std", [P, TPC])
        rstd = sb("pi_rstd", [P, TPC])
        xT = [sb("pi_xT_hi", [P, KT, CH], F32R), sb("pi_xT_lo", [P, KT, CH], F32R)]
        cT = [sb("pi_cT_hi", [P, KT, CH], F32R), sb("pi_cT_lo", [P, KT, CH], F32R)]
        qk_out = sb("pi_qk_out", [P, 2, 2, KT, CH], F32R)
        v_out = sb("pi_v_out", [P, TPC, D])
        turned = ctx.enter_context(nc.psum_tensor("pi_turned", [P, 4, 512], F32))
        projected = ctx.enter_context(nc.psum_tensor("pi_projected", [P, 4, 512], F32))

        dve_passed = sem("pi_dve_passed")
        ident_ready, eps_ready = sem("pi_ident_ready"), sem("pi_eps_ready")
        w_loaded, b_loaded = sem("pi_w_loaded"), sem("pi_b_loaded")
        x_loaded, c_loaded = sem("pi_x_loaded"), sem("pi_c_loaded")
        var_ready, std_ready, rstd_ready = sem("pi_var_ready"), sem("pi_std_ready"), sem("pi_rstd_ready")
        xn_ready = sem("pi_xn_ready")
        turn_done, hi_done, lo_done = sem("pi_turn_done"), sem("pi_hi_done"), sem("pi_lo_done")
        proj_done = sem("pi_proj_done")
        qk_hi_done, proj_read = sem("pi_qk_hi_done"), sem("pi_proj_read")
        stored = [sem(f"pi_stored{i}") for i in range(5)]

        WU = 3 * KT

        def x_units(n):
            return WU + TPC + 2 * TPC * n

        def c_units(n):
            return x_units(n) + TPC

        with nc.Block() as block:
            @block.sync
            def _(sp):
                for i, w in enumerate(("Wq", "Wk", "Wv")):
                    sp.dma_start(w_raw[:, i], a[w].rearrange("(m p) c -> p m c", p=P)).then_inc(w_loaded, 16)
                with nc.allow_non_contiguous_dma(reason="512 elements each"):
                    sp.dma_start(b_qk[:, 0, :], a["bq"].rearrange("(m p) -> p m", p=P)).then_inc(b_loaded, 16)
                    sp.dma_start(b_qk[:, 1, :], a["bk"].rearrange("(m p) -> p m", p=P)).then_inc(b_loaded, 16)
                sp.dma_start(b_v[:, :], a["bv"].rearrange("(o c) -> o c", o=1).to_broadcast([P, D])).then_inc(b_loaded, 16)

                def load(dst, src, n, done):
                    sp.dma_start(dst[:, :, :], src[ds(n * CH, CH), :].rearrange("(t p) c -> p t c", p=P)).then_inc(done, 16)

                load(x_raw, a["x"], 0, x_loaded)
                load(c_raw, a["ctx"], 0, c_loaded)
                sp.wait_ge(xn_ready, TPC)
                load(x_raw, a["x"], 1, x_loaded)
                with sp.Fori(0, NCH - 2) as n:
                    sp.wait_ge(turn_done, c_units(n))
                    load(c_raw, a["ctx"], n + 1, c_loaded)
                    sp.wait_ge(xn_ready, TPC * (n + 2))
                    load(x_raw, a["x"], n + 2, x_loaded)
                sp.wait_ge(turn_done, c_units(NCH - 2))
                load(c_raw, a["ctx"], NCH - 1, c_loaded)

            @block.gpsimd
            def _(pool):
                pool.memset(eps[:, :], EPS).then_inc(eps_ready, 1)
                make_identity(nc, pool, ident, ident_ready)
                with pool.Fori(0, NCH) as n:
                    for i in range(4):
                        t, part = i // 2, i % 2
                        if part == 0:
                            pool.wait_ge(qk_hi_done, 2 * KT * n + KT * (t + 1))
                        else:
                            pool.wait_ge(proj_read, 3 * KT * n + KT * (t + 1))
                        pool.dma_start(scr["qk"][t, part].rearrange("g p n -> p g n")[:, :, ds(n * CH, CH)],
                                       qk_out[:, t, part].bitcast(F32)).then_inc(stored[i], 16)
                    pool.wait_ge(proj_read, 3 * KT * n + 3 * KT)
                    pool.dma_start(scr["v"][ds(n * CH, CH), :].rearrange("(t p) c -> p t c", p=P),
                                   v_out[:, :, :]).then_inc(stored[4], 16)
                for i in range(5):
                    pool.wait_ge(stored[i], 16 * NCH)

            def unit_hi(u, bank, dst):
                nc.scalar.wait_ge(turn_done, u + 1)
                nc.scalar.activation(dst, turned[:, bank, :].rearrange("p (k t) -> p k t", t=P), ACT.Copy).then_inc(hi_done, 1)

            def unit_lo(u, bank, dst, hi):
                nc.vector.wait_ge(hi_done, u + 1)
                nc.vector.tensor_tensor(dst, turned[:, bank, :].rearrange("p (k t) -> p k t", t=P), hi.bitcast(F32),
                                        ALU.subtract).then_inc(lo_done, 1)

            def w_part(w, k):
                return w[:, k // KT, k % KT, :].rearrange("p (k t) -> p k t", t=P)

            @block.scalar
            def _(act):
                def std_of(n):
                    act.wait_ge(var_ready, n + 1)
                    act.activation(std[:, :], mv[:, :, 1], ACT.Sqrt, bias=eps[:, 0:1]).then_inc(std_ready, 1)

                def qk_hi(n, t):
                    if not isinstance(n, int) or n > 0:
                        act.wait_ge(stored[2 * t], 16 * n)
                    for m in range(KT):
                        o = 3 * KT * n + KT * t + m
                        act.wait_ge(proj_done, o + 1)
                        act.activation(qk_out[:, t, 0, m, :], projected[:, m, :], ACT.Identity,
                                       bias=b_qk[:, t, m:m + 1]).then_inc(qk_hi_done, 1)

                act.wait_ge(eps_ready, 1)
                act.wait_ge(b_loaded, 48)
                for k in range(WU):
                    unit_hi(k, k % 4, w_part(wT_hi, k))
                std_of(0)
                for t in range(TPC):
                    unit_hi(WU + t, t, xT[0][:, :, t * P:(t + 1) * P])

                def chunk(n, last):
                    if not last:
                        std_of(n + 1)
                    for t in range(TPC):
                        unit_hi(x_units(n) + t, t, cT[0][:, :, t * P:(t + 1) * P])
                    qk_hi(n, 0)
                    if not last:
                        for t in range(TPC):
                            unit_hi(c_units(n) + t, t, xT[0][:, :, t * P:(t + 1) * P])
                    qk_hi(n, 1)

                chunk(0, False)
                with act.Fori(1, NCH - 1) as n:
                    chunk(n, False)
                chunk(NCH - 1, True)

            @block.vector
            def _(dve):
                def normalise(n):
                    dve.wait_ge(x_loaded, 16 * (n + 1))
                    for t in range(TPC):
                        last = dve.bn_stats(stats[:, t, :], x_raw[:, t, :])
                    last.then_inc(rstd_ready, 1)
                    dve.wait_ge(rstd_ready, 2 * n + 1)
                    settle(dve, dve_passed)
                    for t in range(TPC):
                        last = dve.bn_aggr(mv[:, t, :], stats[:, t, :])
                    last.then_inc(var_ready, 1)
                    dve.wait_ge(std_ready, n + 1)
                    dve.reciprocal(rstd[:, :], std[:, :]).then_inc(rstd_ready, 1)
                    dve.wait_ge(rstd_ready, 2 * n + 2)
                    if not isinstance(n, int) or n > 0:
                        dve.wait_ge(turn_done, x_units(n) - 2 * TPC)
                    for t in range(TPC):
                        dve.tensor_scalar(xn[:, t, :], x_raw[:, t, :], mv[:, t, 0:1], rstd[:, t:t + 1],
                                          ALU.subtract, ALU.mult).then_inc(xn_ready, 1)

                def qk_lo(n, t):
                    if not isinstance(n, int) or n > 0:
                        dve.wait_ge(stored[2 * t + 1], 16 * n)
                    for m in range(KT):
                        dve.wait_ge(qk_hi_done, 2 * KT * n + KT * t + m + 1)
                        dve.scalar_tensor_tensor(out=qk_out[:, t, 1, m, :], in0=projected[:, m, :],
                                                 scalar=b_qk[:, t, m:m + 1], in1=qk_out[:, t, 0, m, :].bitcast(F32),
                                                 op0=ALU.add, op1=ALU.subtract).then_inc(proj_read, 1)

                dve.wait_ge(b_loaded, 48)
                for k in range(WU):
                    unit_lo(k, k % 4, w_part(wT_lo, k), w_part(wT_hi, k))
                normalise(0)
                for t in range(TPC):
                    sl = slice(t * P, (t + 1) * P)
                    unit_lo(WU + t, t, xT[1][:, :, sl], xT[0][:, :, sl])

                def chunk(n, last):
                    if not last:
                        normalise(n + 1)
                    for t in range(TPC):
                        sl = slice(t * P, (t + 1) * P)
                        unit_lo(x_units(n) + t, t, cT[1][:, :, sl], cT[0][:, :, sl])
                    qk_lo(n, 0)
                    if not last:
                        for t in range(TPC):
                            sl = slice(t * P, (t + 1) * P)
                            unit_lo(c_units(n) + t, t, xT[1][:, :, sl], xT[0][:, :, sl])
                    qk_lo(n, 1)
                    if not isinstance(n, int) or n > 0:
                        dve.wait_ge(stored[4], 16 * n)
                    for t in range(TPC):
                        dve.wait_ge(proj_done, 3 * KT * n + 2 * KT + t + 1)
                        dve.tensor_tensor(v_out[:, t, :], projected[:, t, :], b_v[:, :], ALU.add).then_inc(proj_read, 1)

                chunk(0, False)
                with dve.Fori(1, NCH - 1) as n:
                    chunk(n, False)
                chunk(NCH - 1, True)

            @block.tensor
            def _(pe):
                def turn(u, bank, src, free):
                    if free:
                        pe.wait_ge(lo_done, u - 3)
                    for k in range(KT):
                        last = pe.transpose(turned[:, bank, k * P:(k + 1) * P], src(k), ident[:, :])
                    last.then_inc(turn_done, 1)

                def turn_x(n):
                    for t in range(TPC):
                        pe.wait_ge(xn_ready, TPC * n + t + 1)
                        turn(x_units(n) - TPC + t, t, lambda k: xn[:, t, k * P:(k + 1) * P], True)

                def project_qk(n, t, src, ready):
                    pe.wait_ge(lo_done, ready)
                    for m in range(KT):
                        if t or not isinstance(n, int) or n > 0:
                            pe.wait_ge(proj_read, 3 * KT * n + KT * t + m + 1 - 4)
                        for k in range(KT):
                            last = split_matmul(pe, projected[:, m, :], wT_hi[:, t, k, m * P:(m + 1) * P],
                                                wT_lo[:, t, k, m * P:(m + 1) * P], src[0][:, k, :], src[1][:, k, :],
                                                k == 0, k == KT - 1)
                        last.then_inc(proj_done, 1)

                pe.wait_ge(ident_ready, 2)
                pe.wait_ge(w_loaded, 48)
                for k in range(WU):
                    turn(k, k % 4, lambda m: w_raw[:, k // KT, m, (k % KT) * P:(k % KT + 1) * P], k >= 4)
                turn_x(0)

                def chunk(n, first, last):
                    pe.wait_ge(c_loaded, 16 * (n + 1))
                    for t in range(TPC):
                        turn(x_units(n) + t, t, lambda k: c_raw[:, t, k * P:(k + 1) * P], True)
                    project_qk(n, 0, xT, x_units(n))
                    if not last:
                        turn_x(n + 1)
                    project_qk(n, 1, cT, c_units(n))
                    for t in range(TPC):
                        pe.wait_ge(proj_read, 3 * KT * n + 2 * KT + t + 1 - 4)
                        for k in range(KT):
                            last_mm = split_matmul(pe, projected[:, t, :], cT[0][:, k, t * P:(t + 1) * P],
                                                   cT[1][:, k, t * P:(t + 1) * P], wT_hi[:, 2, k, :], wT_lo[:, 2, k, :],
                                                   k == 0, k == KT - 1)
                        last_mm.then_inc(proj_done, 1)

                chunk(0, True, False)
                with pe.Fori(1, NCH - 1) as n:
                    chunk(n, False, False)
                chunk(NCH - 1, False, True)


def attend(nc, z, scr):
    B, S, HD, KT = z.B, z.S, z.HD, z.KT
    HPG = P // HD
    G_ALL = B * z.H // HPG
    PAIRS = G_ALL // 2
    QT = S // P
    QH = S // 512
    STEPS = QT * QH
    UNITS = HPG * QT
    ROWS = 3 * HD
    SCALE = float(HD) ** -0.5
    RING = 8
    HP = HPG - 1
    STACKS = 3
    TURN_STEP = STEPS - 3
    LEAD = UNITS - 2 * TURN_STEP
    UNITS_AT = [[(1, LEAD + 2 * T + i) if T < TURN_STEP else (2, 2 * (T - TURN_STEP) + i) for i in range(2)]
                for T in range(STEPS)]
    assert HPG == 4 and QH == 2

    with ExitStack() as ctx:
        def sb(name, shape, dt=F32):
            return ctx.enter_context(nc.sbuf_tensor(name, shape, dt))

        def ps(name, shape):
            return ctx.enter_context(nc.psum_tensor(name, shape, F32))

        def sem(name):
            return ctx.enter_context(nc.semaphore(name))

        ident = sb("at_ident", [P, P])
        ones = sb("at_ones", [P, HD])
        q_st = [sb(f"at_q{w}", [P, HPG, S], F32R) for w in range(STACKS)]
        k_st = [sb(f"at_k{w}", [P, HPG, S], F32R) for w in range(STACKS)]
        v_sb = [sb(f"at_v{e}", [P, QT, P]) for e in range(2)]
        maxima = [sb(f"at_max{e}", [P, P]) for e in range(2)]
        neg_max = [sb(f"at_negmax{e}", [UNITS, P], F32R) for e in range(2)]
        probs = [sb(f"at_probs{r}", [P, HPG, 512]) for r in range(RING)]
        psum_k = [sb(f"at_keysum{h}", [P, HPG, 512]) for h in range(QH)]
        o_raw = [sb(f"at_o_raw{h}", [P, 512]) for h in range(QH)]
        den_t = sb("at_den_t", [P, 512])
        recip_t = sb("at_recip_t", [P, 512 // 32])
        recip = sb("at_recip", [P, 512])
        o_out = [sb(f"at_o_out{h}", [P, 512]) for h in range(QH)]
        unit_ps = [ps(f"at_unit_ps{i}", [P, 2, 512]) for i in range(2)]
        score_ps = [ps(f"at_score_ps{i}", [P, 512]) for i in range(2)]
        pv_ps = ps("at_pv_ps", [P, 512])
        den_ps = ps("at_den_ps", [P, 512])

        const_ready = sem("at_const_ready")
        ident_ready = sem("at_ident_ready")
        qk_loaded = [[sem(f"at_qk_loaded{w}{j}") for j in range(HPG)] for w in range(STACKS)]
        v_loaded = [sem(f"at_v_loaded{e}") for e in range(2)]
        max_loaded = [sem(f"at_max_loaded{e}") for e in range(2)]
        unit_done, unit_read = sem("at_unit_done"), sem("at_unit_read")
        score_done, exp_done = sem("at_score_done"), sem("at_exp_done")
        pv_done, pv_read = sem("at_pv_done"), sem("at_pv_read")
        added = sem("at_added")
        added_last = sem("at_added_last")
        den_done, recip_done, o_done = sem("at_den_done"), sem("at_recip_done"), sem("at_o_done")
        o_stored = [sem(f"at_o_stored{h}") for h in range(QH)]

        def whole(G):
            return isinstance(G, int)

        ROUND = 2 * STACKS

        def number(r, d):
            return ROUND * r + d

        def over_groups(engine, group):
            group(0, 0)
            group(0, 1)
            with engine.Fori(0, (G_ALL - 4) // ROUND) as r:
                for d in range(2, 2 + ROUND):
                    group(r, d)
            group(0, G_ALL - 2)
            group(0, G_ALL - 1)

        with nc.Block() as block:
            @block.sync
            def _(sp):
                def load_stacks(r, d):
                    G, w = number(r, d), d % STACKS
                    b, g = G // 4, G % 4
                    if not (whole(G) and G < STACKS):
                        sp.wait_ge(score_done, HPG * STEPS * (G - STACKS + 1))
                    for j in range(HPG):
                        for dst, t, parts in ((q_st[w], 0, (0, 1, 0)), (k_st[w], 1, (0, 0, 1))):
                            for i, part in enumerate(parts):
                                src = scr["qk"][t, part].rearrange("g p n -> (g p) n")
                                sp.dma_start(dst[i * HD:(i + 1) * HD, j, :].bitcast(F32),
                                             src[ds(g * P + j * HD, HD), ds(b * S, S)]).then_inc(qk_loaded[w][j], 16)

                def load_v(r, d):
                    G, e = number(r, d), d % 2
                    b, g = G // 4, G % 4
                    if not (whole(G) and G < 2):
                        sp.wait_ge(pv_done, STEPS * (G - 1))
                    sp.dma_start(v_sb[e][:, :, :], scr["v"][ds(b * S, S), ds(g * P, P)]
                                 .rearrange("(k p) c -> p k c", p=P)).then_inc(v_loaded[e], 16)

                def store(r, d, h):
                    G = number(r, d)
                    b, g = G // 4, G % 4
                    sp.wait_ge(o_done, QH * G + h + 1)
                    sp.dma_start(scr["o"][ds(g * P, P), ds(b * S + h * 512, 512)], o_out[h][:, :]).then_inc(o_stored[h], 16)

                def load_max(r, d):
                    G, e, w = number(r, d), d % 2, d % STACKS
                    sp.wait_ge(unit_read, (UNITS + 1) * (G + 1))
                    sp.dma_start(q_st[w][ROWS:ROWS + 1, :, :].bitcast(F32).rearrange("o j (t n) -> o (j t) n", n=P),
                                 neg_max[e][:, :].bitcast(F32)).then_inc(max_loaded[e], 16)

                def group(r, d):
                    if not (whole(r) and d + 1 >= G_ALL):
                        load_v(r, d + 1)
                    if not (whole(r) and d + 2 >= G_ALL):
                        load_stacks(r, d + 2)
                    if not (whole(r) and d == 0):
                        store(r, d - 1, 1)
                    if not (whole(r) and d + 1 >= G_ALL):
                        load_max(r, d + 1)
                    store(r, d, 0)

                load_stacks(0, 0)
                load_v(0, 0)
                load_stacks(0, 1)
                load_max(0, 0)
                over_groups(sp, group)
                store(0, G_ALL - 1, 1)
                for h in range(QH):
                    sp.wait_ge(o_stored[h], 16 * G_ALL)

            @block.gpsimd
            def _(pool):
                make_identity(nc, pool, ident, ident_ready)

                def group(G, first):
                    for h in range(QH):
                        for k in range(1, QT):
                            T = QT * h + k
                            pool.wait_ge(exp_done, HPG * (STEPS * G + T + 1))
                            if k == 1 and not first:
                                pool.wait_ge(den_done, QH * (G - 1) + h + 1)
                            if k > 1 or h > 0 or not first:
                                pool.wait_ge(added, (QT - 1) * (QH * G + h) + k - 1)
                            before = probs[(T - 1) % RING] if k == 1 else psum_k[h]
                            pool.tensor_tensor(psum_k[h][:, 0:HP, :], probs[T % RING][:, 0:HP, :], before[:, 0:HP, :],
                                               ALU.add).then_inc(added, 1)

                group(0, True)
                with pool.Fori(1, G_ALL) as G:
                    group(G, False)

            @block.scalar
            def _(act):
                def exps(G, T, first):
                    for j in range(HPG):
                        n = HPG * (STEPS * G + T) + j
                        if j == 0:
                            if T >= RING:
                                k = T - RING
                                act.wait_ge(pv_done, STEPS * G + k + 1)
                                for add in (added, added_last):
                                    act.wait_ge(add, (QT - 1) * (QH * G + k // QT) + max(k % QT, 1))
                            elif not first:
                                k = STEPS + T - RING
                                act.wait_ge(pv_done, STEPS * (G - 1) + k + 1)
                                for add in (added, added_last):
                                    act.wait_ge(add, (QT - 1) * (QH * (G - 1) + 1) + max(k % QT, 1))
                        act.wait_ge(score_done, n + 1)
                        act.activation(probs[T % RING][:, j, :], score_ps[j % 2][:, :], ACT.Exp,
                                       scale=SCALE).then_inc(exp_done, 1)

                def read_pv(G, h, first=False):
                    act.wait_ge(pv_done, STEPS * G + QT * (h + 1))
                    if not first:
                        act.wait_ge(o_done, QH * (G - 1) + h + 1)
                    act.activation(o_raw[h][:, :], pv_ps[:, :], ACT.Copy).then_inc(pv_read, 1)

                def group(G, first):
                    for T in range(STEPS):
                        exps(G, T, first)
                        if T == 0 and not first:
                            read_pv(G - 1, 1, whole(G) and G == 1)
                        if T == QT:
                            read_pv(G, 0, first)

                group(0, True)
                group(1, False)
                with act.Fori(2, G_ALL) as G:
                    group(G, False)
                read_pv(G_ALL - 1, 1)

            @block.vector
            def _(dve):
                dve.memset(ones[:, :], 1.0)
                for w in range(STACKS):
                    dve.memset(k_st[w][ROWS:ROWS + 1, :, :].bitcast(F32), 1.0)
                for e in range(2):
                    last = dve.memset(maxima[e][:, :], 0.0)
                last.then_inc(const_ready, 1)
                dve.wait_ge(const_ready, 1)

                def unit(G, e, u):
                    dve.wait_ge(unit_done, (UNITS + 1) * G + u + 1)
                    dve.tensor_reduce(maxima[e][:, u:u + 1], unit_ps[(e + u) % 2][:, :, :].rearrange("p a b -> p (a b)"),
                                      AX_X, ALU.max).then_inc(unit_read, 1)

                def read_turn(G, e, use):
                    dve.wait_ge(unit_done, (UNITS + 1) * (G + 1))
                    dve.wait_ge(max_loaded[e], 16 * use)
                    dve.tensor_scalar(neg_max[e][:, :], unit_ps[(e + UNITS) % 2][0:UNITS, 0, 0:P], -1.0, None,
                                      ALU.mult).then_inc(unit_read, 1)

                def invert(G, h, stage):
                    if stage == 0:
                        dve.wait_ge(den_done, QH * G + h + 1)
                        dve.transpose(den_t[:, :], den_ps[:, :]).then_inc(recip_done, 1)
                    elif stage == 1:
                        dve.wait_ge(recip_done, 3 * (QH * G + h) + 1)
                        dve.reciprocal(recip_t[:, :], den_t[:, :].rearrange("p (b c) -> p b c", c=32)[:, :, 0]).then_inc(recip_done, 1)
                    else:
                        dve.wait_ge(recip_done, 3 * (QH * G + h) + 2)
                        dve.transpose(recip[:, :], recip_t[:, :].unsqueeze(2).to_broadcast([P, 512 // 32, 32])).then_inc(recip_done, 1)

                def normalise(G, h):
                    dve.wait_ge(recip_done, 3 * (QH * G + h) + 3)
                    dve.wait_ge(pv_read, QH * G + h + 1)
                    dve.wait_ge(o_stored[h], 16 * G)
                    dve.tensor_tensor(o_out[h][:, :], o_raw[h][:, :], recip[:, :], ALU.mult).then_inc(o_done, 1)

                def add_keys(G, T, first):
                    h, k = T // QT, T % QT
                    if k == 0:
                        return
                    dve.wait_ge(exp_done, HPG * (STEPS * G + T + 1))
                    if k == 1 and not first:
                        dve.wait_ge(den_done, QH * (G - 1) + h + 1)
                    if k > 1 or h > 0 or not first:
                        dve.wait_ge(added_last, (QT - 1) * (QH * G + h) + k - 1)
                    before = probs[(T - 1) % RING] if k == 1 else psum_k[h]
                    dve.tensor_tensor(psum_k[h][:, HP, :], probs[T % RING][:, HP, :], before[:, HP, :],
                                      ALU.add).then_inc(added_last, 1)

                def results(G, T, first):
                    for Gh, h, T0 in ((G - 1, 1, 3), (G, 0, QT + 3)):
                        if T in (T0, T0 + 1) and not (first and h == 1):
                            if T == T0:
                                invert(Gh, h, 0)
                                yield
                                invert(Gh, h, 1)
                            else:
                                invert(Gh, h, 2)
                                yield
                                normalise(Gh, h)

                def group(G, e, i, first=False, left=2):
                    for T in range(STEPS):
                        if T == TURN_STEP and left:
                            read_turn(G + 1, 1 - e, i + e)
                        stages = results(G, T, first)
                        for ahead, u in UNITS_AT[T]:
                            if ahead <= left:
                                unit(G + ahead, (e + ahead) % 2, u)
                            next(stages, None)
                        add_keys(G, T, first)
                        for _ in stages:
                            pass

                for u in range(UNITS):
                    unit(0, 0, u)
                read_turn(0, 0, 0)
                for u in range(LEAD):
                    unit(1, 1, u)
                group(0, 0, 0, first=True)
                group(1, 1, 0)
                with dve.Fori(1, PAIRS - 1) as i:
                    for e in range(2):
                        group(2 * i + e, e, i)
                group(G_ALL - 2, 0, PAIRS - 1, left=1)
                group(G_ALL - 1, 1, PAIRS - 1, left=0)
                for stage in range(3):
                    invert(G_ALL - 1, 1, stage)
                normalise(G_ALL - 1, 1)

            @block.tensor
            def _(pe):
                def unit(r, d, u):
                    G, e, w = number(r, d), d % 2, d % STACKS
                    n = (UNITS + 1) * G + u
                    j, qt = u // QT, u % QT
                    if qt == 0:
                        pe.wait_ge(qk_loaded[w][j], 96 * (2 * r + d // 3 + 1))
                    if not (whole(n) and n < 2):
                        pe.wait_ge(unit_read, n - 1)
                    out = unit_ps[(e + u) % 2]
                    for h in range(2):
                        last = pe.matmul(out[:, h, :], q_st[w][0:ROWS, j, qt * P:(qt + 1) * P],
                                         k_st[w][0:ROWS, j, h * 512:(h + 1) * 512], start=True, stop=True)
                    last.then_inc(unit_done, 1)

                def turn(r, d):
                    G, e = number(r, d), d % 2
                    pe.wait_ge(unit_read, (UNITS + 1) * G + UNITS)
                    pe.transpose(unit_ps[(e + UNITS) % 2][:, 0, 0:P], maxima[e][:, :], ident[:, :]).then_inc(unit_done, 1)

                def score(r, d, T, j):
                    G, e, w = number(r, d), d % 2, d % STACKS
                    h, k = T // QT, T % QT
                    n = HPG * (STEPS * G + T) + j
                    if T == 0 and j == 0:
                        pe.wait_ge(max_loaded[e], 16 * (3 * r + d // 2 + 1))
                    if not (whole(n) and n < 2):
                        pe.wait_ge(exp_done, n - 1)
                    pe.matmul(score_ps[j % 2][:, :], k_st[w][0:ROWS + 1, j, k * P:(k + 1) * P],
                              q_st[w][0:ROWS + 1, j, h * 512:(h + 1) * 512], start=True, stop=True).then_inc(score_done, 1)

                def times_v(G, e, T):
                    h, k = T // QT, T % QT
                    if k == 0 and not (whole(G) and G == 0 and h == 0):
                        pe.wait_ge(pv_read, QH * G + h)
                    pe.wait_ge(exp_done, HPG * (STEPS * G + T + 1))
                    for j in range(HPG):
                        last = pe.matmul(pv_ps[j * HD:(j + 1) * HD, :], v_sb[e][:, k, j * HD:(j + 1) * HD],
                                         probs[T % RING][:, j, :], start=(k == 0), stop=(k == QT - 1),
                                         tile_position=(0, j * HD))
                    last.then_inc(pv_done, 1)

                def denominators(G, h):
                    pe.wait_ge(added, (QT - 1) * (QH * G + h + 1))
                    pe.wait_ge(added_last, (QT - 1) * (QH * G + h + 1))
                    if not (whole(G) and G == 0 and h == 0):
                        pe.wait_ge(recip_done, 3 * (QH * G + h - 1) + 1)
                    for j in range(HPG):
                        last = pe.matmul(den_ps[j * HD:(j + 1) * HD, :], ones[:, :], psum_k[h][:, j, :],
                                         start=True, stop=True, tile_position=(0, j * HD))
                    last.then_inc(den_done, 1)

                def group(r, d):
                    G, e = number(r, d), d % 2
                    left = G_ALL - 1 - d if whole(r) else 2
                    for T in range(STEPS):
                        if T == 0:
                            pe.wait_ge(v_loaded[e], 16 * (3 * r + d // 2 + 1))
                        units = [(r, d + ahead, u) for ahead, u in UNITS_AT[T] if ahead <= left]
                        nxt = (r, d, T + 1) if T + 1 < STEPS else (r, d + 1, 0)
                        go = T + 1 < STEPS or left
                        for j in range(HPG):
                            if go:
                                score(*nxt, j)
                            if j == 1:
                                times_v(G, e, T)
                                if T == TURN_STEP and left:
                                    turn(r, d + 1)
                            if j % 2 and units:
                                unit(*units.pop(0))
                        if T == 2 and not (whole(r) and d == 0):
                            denominators(G - 1, 1)
                        if T == QT + 2:
                            denominators(G, 0)

                pe.wait_ge(const_ready, 1)
                pe.wait_ge(ident_ready, 2)
                for u in range(UNITS):
                    unit(0, 0, u)
                turn(0, 0)
                for j in range(2):
                    unit(0, 1, j)
                for j in range(HPG):
                    score(0, 0, 0, j)
                for u in range(2, LEAD):
                    unit(0, 1, u)
                over_groups(pe, group)
                denominators(G_ALL - 1, 1)


def route(nc, z, a, scr, weights):
    KT, CH, TPC, NCH, D, E, CAP, TOP = z.KT, z.CH, z.TPC, z.NCH, z.D, z.E, z.CAP, z.TOP
    SLOTS = E * CAP
    TOK = z.TOK
    FAR = 100000.0
    PICKS = TPC * TOP
    with ExitStack() as ctx:
        def sb(name, shape, dt=F32):
            return ctx.enter_context(nc.sbuf_tensor("rt_" + name, shape, dt))

        def sem(name):
            return ctx.enter_context(nc.semaphore("rt_" + name))

        ident = sb("ident", [P, P])
        eps = sb("eps", [P, 1])
        wo_raw = sb("wo_raw", [P, KT, D])
        woT = [sb("woT_hi", [P, KT, D], F32R), sb("woT_lo", [P, KT, D], F32R)]
        rw = sb("rw", [E, D])
        rwT = sb("rwT", [P, KT, E])
        rb = sb("rb", [P, E])
        bo = sb("bo", [P, D])
        gate = sb("gate", [P, 2])
        tanh_g = sb("tanh_g", [P, 2])
        tanh_bo = sb("tanh_bo", [P, D])
        iota_i = sb("iota_i", [P, E], I32)
        iota = sb("iota", [P, E])
        user = sb("user", [P, TPC, TOP, 2], I32)
        spare = sb("spare", [E, CAP, 2], I32)
        zero_row = sb("zero_row", [P, D])
        before_f = sb("before_f", [P, P])
        before = sb("before", [P, P], BF16)
        ones = sb("ones", [P, P], BF16)
        oT_raw = sb("oT_raw", [P, KT, CH])
        oT = [sb("oT_hi", [P, KT, CH], F32R), sb("oT_lo", [P, KT, CH], F32R)]
        x_raw = sb("x_raw", [P, TPC, D])
        xb = sb("xb", [P, TPC, D])
        x1 = sb("x1", [P, TPC, D])
        stats = sb("stats", [P, TPC, 6])
        mv = sb("mv", [P, TPC, 2])
        std = sb("std", [P, TPC])
        rstd = sb("rstd", [P, TPC])
        xn = sb("xn", [P, TPC, D])
        xnT = sb("xnT", [P, KT, CH])
        logits = sb("logits", [P, TPC, E])
        best = sb("best", [P, TPC, 8])
        best_at = sb("best_at", [P, TPC, 8], U32)
        expert = sb("expert", [P, TPC, TOP])
        picked = sb("picked", [P, TPC, TOP, E])
        chosen = sb("chosen", [P, TPC, E], BF16)
        chunk_sum = sb("chunk_sum", [P, E])
        run = sb("run", [P, E])
        run_b = sb("run_b", [P, E], BF16)
        at = sb("at", [P, TPC, TOP, E])
        place = sb("place", [P, TPC, TOP])
        slot = sb("slot", [P, TPC, TOP])
        far = sb("far", [P, TPC, TOP])
        target = sb("target", [P, TPC, TOP], I32)
        value = sb("value", [P, NCH, TPC, TOP])
        kept = sb("kept", [P, NCH, TPC, TOP])
        w_tmp = [sb(f"w_tmp{i}", [P, NCH, TPC]) for i in range(5)]
        w_gk = sb("w_gk", [P, NCH, TPC, TOP])
        weight = sb("weight", [P, TOP, NCH, TPC])
        y_ps = ctx.enter_context(nc.psum_tensor("rt_y_ps", [P, TPC, 512], F32))
        turned = ctx.enter_context(nc.psum_tensor("rt_turned", [P, 2, 512], F32))
        logit_ps = ctx.enter_context(nc.psum_tensor("rt_logit_ps", [P, 512], F32))
        place_ps = ctx.enter_context(nc.psum_tensor("rt_place_ps", [P, 512], F32))
        logit_v = logit_ps[:, 0:TPC * E].rearrange("p (t e) -> p t e", e=E)
        place_v = place_ps[:, 0:TPC * E].rearrange("p (t e) -> p t e", e=E)

        dve_passed, pool_passed = sem("dve_passed"), sem("pool_passed")
        wo_loaded, small_loaded = sem("wo_loaded"), sem("small_loaded")
        o_loaded, x_loaded = sem("o_loaded"), sem("x_loaded")
        pool_const, dve_const, tanh_ready = sem("pool_const"), sem("dve_const"), sem("tanh_ready")
        spares_stored = sem("spares_stored")
        wo_turned, wo_hi, wo_lo = sem("wo_turned"), sem("wo_hi"), sem("wo_lo")
        o_hi, o_lo = sem("o_hi"), sem("o_lo")
        y_done, x1_ready, stats_done = sem("y_done"), sem("x1_ready"), sem("stats_done")
        var_ready, std_ready, rstd_ready = sem("var_ready"), sem("std_ready"), sem("rstd_ready")
        xb_ready, xn_ready = sem("xb_ready"), sem("xn_ready")
        x1_stored, xn_stored = sem("x1_stored"), sem("xn_stored")
        xn_turned, xnT_ready, logits_done = sem("xn_turned"), sem("xnT_ready"), sem("logits_done")
        pick, chosen_ready = sem("pick"), sem("chosen_ready")
        place_done, placed = sem("place_done"), sem("placed")
        scattered = sem("scattered")
        user_next = sem("user_next")
        weigh, exp_ready, weight_stored = sem("weigh"), sem("exp_ready"), sem("weight_stored")

        WU = KT + 1
        PICK, PLACE = 12, 10

        with nc.Block() as block:
            @block.sync
            def _(sp):
                def load(dst, src, c, done):
                    sp.dma_start(dst[:, :, :], src[ds(c * CH, CH), :].rearrange("(t p) c -> p t c", p=P)).then_inc(done, 16)

                def load_o(c):
                    sp.dma_start(oT_raw[:, :, :], scr["o"][:, ds(c * CH, CH)].rearrange("(k p) n -> p k n", p=P)).then_inc(o_loaded, 16)

                def store(dst, src, c, done):
                    sp.dma_start(dst[ds(c * CH, CH), :].rearrange("(t p) c -> p t c", p=P), src[:, :, :]).then_inc(done, 16)

                sp.dma_start(wo_raw[:, :, :], a["Wo"].rearrange("(m p) c -> p m c", p=P)).then_inc(wo_loaded, 16)
                load_o(0)
                load(x_raw, a["x"], 0, x_loaded)
                for dst, src, n in ((rb, "router_b", E), (bo, "bo", D)):
                    sp.dma_start(dst[:, :], a[src].rearrange("(o c) -> o c", o=1).to_broadcast([P, n])).then_inc(small_loaded, 16)
                for i, src in enumerate(("g_xattn", "g_ffn")):
                    sp.dma_start(gate[:, i:i + 1], a[src].rearrange("(o c) -> o c", o=1).to_broadcast([P, 1])).then_inc(small_loaded, 16)
                sp.dma_start(rw[:, :], a["router_w"]).then_inc(small_loaded, 16)
                sp.wait_ge(pool_const, 9)
                sp.dma_start(scr["user_of"].rearrange("(e s) o -> e s o", e=E), spare[:, :, :]).then_inc(spares_stored, 16)
                for i in range(CAP // P):
                    for dst in ("xn", "out"):
                        sp.dma_start(scr[dst][TOK + i * P:TOK + (i + 1) * P, :], zero_row[:, :]).then_inc(spares_stored, 16)
                sp.dma_start(scr["weight"][TOK:TOK + CAP, :].rearrange("(p n) o -> p (n o)", p=P),
                             zero_row[:, 0:CAP // P]).then_inc(spares_stored, 16)
                weights.load(sp, 0, 0)

                def step(c, more):
                    if more:
                        sp.wait_ge(o_lo, c + 1)
                        load_o(c + 1)
                        sp.wait_ge(xb_ready, TPC * (c + 1))
                        load(x_raw, a["x"], c + 1, x_loaded)
                    sp.wait_ge(x1_ready, TPC * (c + 1))
                    store(scr["out"], x1, c, x1_stored)
                    sp.wait_ge(xn_ready, TPC * (c + 1))
                    store(scr["xn"], xn, c, xn_stored)

                step(0, True)
                for c in range(1, weights.LOADS):
                    weights.load(sp, 0, c)
                with sp.Fori(1, NCH - 1) as c:
                    step(c, True)
                step(NCH - 1, False)
                sp.wait_ge(weigh, 10)
                with nc.allow_non_contiguous_dma(reason="4096 weights each"):
                    for k in range(TOP):
                        sp.dma_start(scr["weight"][k * (TOK + CAP):k * (TOK + CAP) + TOK, :].rearrange("(n p) o -> p (n o)", p=P),
                                     weight[:, k, :, :].rearrange("p c t -> p (c t)")).then_inc(weight_stored, 16)
                sp.wait_ge(x1_stored, 16 * NCH)
                sp.wait_ge(xn_stored, 16 * NCH)
                sp.wait_ge(weight_stored, 16 * TOP)

            @block.gpsimd
            def _(pool):
                pool.memset(eps[:, :], EPS)
                pool.memset(zero_row[:, :], 0.0)
                pool.memset(ones[:, :], 1.0)
                pool.memset(before_f[:, :], 1.0)
                pool.memset(ident[:, :], 0.0)
                pool.iota(iota_i[:, :], [[1, E]], base=0, channel_multiplier=0)
                for i in range(2):
                    pool.iota(spare[:, :, i], [[1, CAP]], base=TOK, channel_multiplier=0)
                    for k in range(TOP):
                        last = pool.iota(user[:, :, k, i], [[P, TPC]], base=k * i * (TOK + CAP), channel_multiplier=1)
                last.then_inc(pool_const, 7)
                pool.wait_ge(pool_const, 7)
                pool.affine_select(out=ident[:, :], in_=ident[:, :], compare_op=ALU.not_equal, fill=1.0, base=0,
                                   pattern=[[-1, P]], channel_multiplier=1).then_inc(pool_const, 1)
                pool.affine_select(out=before_f[:, :], in_=before_f[:, :], compare_op=ALU.is_gt, fill=0.0, base=0,
                                   pattern=[[1, P]], channel_multiplier=-1).then_inc(pool_const, 1)

                def add_bias(c, first=False):
                    pool.wait_ge(x_loaded, 16 * (c + 1))
                    for t in range(TPC):
                        if not first:
                            pool.wait_ge(x1_ready, TPC * (c - 1) + t + 1)
                            pool.wait_ge(xb_ready, TPC * c + t)
                        elif t:
                            pool.wait_ge(xb_ready, t)
                        pool.tensor_tensor(xb[:, t, :], x_raw[:, t, :], tanh_bo[:, :], ALU.add).then_inc(xb_ready, 1)

                def scatter(c):
                    pool.wait_ge(placed, PLACE * (c + 2))
                    settle(pool, pool_passed)
                    for i in range(PICKS):
                        t, k = i // TOP, i % TOP
                        pool.indirect_dma_start(scr["user_of"], bass.IndirectOffsetOnAxis(target[:, t, k:k + 1], 0),
                                                user[:, t, k, :], None, bounds_check=SLOTS - 1,
                                                oob_is_err=False).then_inc(scattered, 16)

                pool.wait_ge(dve_const, 2)
                add_bias(0, True)
                add_bias(1)
                pool.wait_ge(spares_stored, 16 * (2 + 2 * (CAP // P)))
                with pool.Fori(1, NCH - 1) as c:
                    add_bias(c + 1)
                    scatter(c - 1)
                scatter(NCH - 2)
                scatter(NCH - 1)
                pool.wait_ge(scattered, 16 * PICKS * NCH)

            @block.scalar
            def _(act):
                act.wait_ge(small_loaded, 80)
                act.activation(tanh_g[:, :], gate[:, :], ACT.Tanh).then_inc(tanh_ready, 1)
                for u in range(KT):
                    act.wait_ge(wo_turned, u + 1)
                    act.activation(woT[0][:, u, :], turned[:, u % 2, :], ACT.Copy).then_inc(wo_hi, 1)
                act.wait_ge(pool_const, 9)

                def split_o(c, first=False):
                    act.wait_ge(o_loaded, 16 * (c + 1))
                    if not first:
                        act.wait_ge(y_done, TPC * c)
                    act.activation(oT[0][:, :, :], oT_raw[:, :, :], ACT.Copy).then_inc(o_hi, 1)

                def std_of(c):
                    act.wait_ge(var_ready, c + 1)
                    act.activation(std[:, :], mv[:, :, 1], ACT.Sqrt, bias=eps[:, 0:1]).then_inc(std_ready, 1)

                def copy_turned(c, first=False):
                    if not first:
                        act.wait_ge(logits_done, c)
                    for t in range(TPC):
                        act.wait_ge(xn_turned, TPC * c + t + 1)
                        act.activation(xnT[:, :, t * P:(t + 1) * P],
                                       turned[:, t % 2, :].rearrange("p (k n) -> p k n", n=P), ACT.Copy).then_inc(xnT_ready, 1)

                split_o(0, True)
                std_of(0)
                split_o(1)
                std_of(1)
                split_o(2)
                copy_turned(0, True)
                with act.Fori(1, NCH - 2) as c:
                    std_of(c + 1)
                    split_o(c + 2)
                    copy_turned(c)
                std_of(NCH - 1)
                copy_turned(NCH - 2)
                copy_turned(NCH - 1)
                act.wait_ge(weigh, 1)
                act.activation(w_tmp[1][:, :, :], w_tmp[0][:, :, :], ACT.Exp).then_inc(exp_ready, 1)

            @block.vector
            def _(dve):
                dve.memset(run[:, :], 0.0)
                dve.memset(run_b[:, :], 0.0).then_inc(placed, PLACE)
                dve.sem_inc(user_next, 1)
                dve.wait_ge(tanh_ready, 1)
                dve.tensor_scalar(tanh_bo[:, :], bo[:, :], tanh_g[:, 0:1], None, ALU.mult).then_inc(dve_const, 2)
                dve.wait_ge(pool_const, 9)
                dve.tensor_copy(iota[:, :], iota_i[:, :]).then_inc(dve_const, 1)
                dve.tensor_copy(before[:, :], before_f[:, :]).then_inc(dve_const, 1)
                for u in range(KT):
                    dve.wait_ge(wo_hi, u + 1)
                    dve.tensor_tensor(woT[1][:, u, :], turned[:, u % 2, :], woT[0][:, u, :].bitcast(F32),
                                      ALU.subtract).then_inc(wo_lo, 1)
                dve.wait_ge(wo_turned, WU)
                dve.tensor_copy(rwT[:, :, :], turned[:, KT % 2, 0:KT * E].rearrange("p (k e) -> p k e", e=E)).then_inc(wo_lo, 1)
                dve.wait_ge(dve_const, 4)

                def split_o(c):
                    dve.wait_ge(o_hi, c + 1)
                    dve.tensor_tensor(oT[1][:, :, :], oT_raw[:, :, :], oT[0][:, :, :].bitcast(F32),
                                      ALU.subtract).then_inc(o_lo, 1)

                def normalise(c, first=False):
                    def residual(t):
                        dve.wait_ge(y_done, TPC * c + t + 1)
                        dve.wait_ge(xb_ready, TPC * c + t + 1)
                        dve.scalar_tensor_tensor(out=x1[:, t, :], in0=y_ps[:, t, :], scalar=tanh_g[:, 0:1], in1=xb[:, t, :],
                                                 op0=ALU.mult, op1=ALU.add).then_inc(x1_ready, 1)

                    def statistics(t):
                        dve.wait_ge(x1_ready, TPC * c + t + 1)
                        dve.bn_stats(stats[:, t, :], x1[:, t, :]).then_inc(stats_done, 1)

                    dve.wait_ge(x1_stored, 16 * c)
                    residual(0)
                    for t in range(1, TPC):
                        residual(t)
                        statistics(t - 1)
                    statistics(TPC - 1)
                    dve.wait_ge(stats_done, TPC * (c + 1))
                    settle(dve, dve_passed)
                    for t in range(TPC):
                        last = dve.bn_aggr(mv[:, t, :], stats[:, t, :])
                    last.then_inc(var_ready, 1)
                    dve.wait_ge(std_ready, c + 1)
                    dve.reciprocal(rstd[:, :], std[:, :]).then_inc(rstd_ready, 1)
                    dve.wait_ge(rstd_ready, c + 1)
                    dve.wait_ge(xn_stored, 16 * c)
                    if not first:
                        dve.wait_ge(xn_turned, TPC * c)
                    for t in range(TPC):
                        dve.tensor_scalar(xn[:, t, :], x1[:, t, :], mv[:, t, 0:1], rstd[:, t:t + 1],
                                          ALU.subtract, ALU.mult).then_inc(xn_ready, 1)

                def choose(c):
                    n = PICK * c
                    dve.wait_ge(logits_done, c + 1)
                    dve.tensor_tensor(logits[:, :, :], logit_v, rb[:, :].unsqueeze(1).to_broadcast([P, TPC, E]),
                                      ALU.add).then_inc(pick, 1)
                    dve.wait_ge(pick, n + 1)
                    settle(dve, dve_passed)
                    for t in range(TPC):
                        dve.max(best[:, t, :], logits[:, t, :]).then_inc(pick, 1)
                    for t in range(TPC):
                        dve.wait_ge(pick, n + 2 + t)
                        settle(dve, dve_passed)
                        dve.max_index(best_at[:, t, :], best[:, t, :], logits[:, t, :]).then_inc(pick, 1)
                    dve.wait_ge(pick, n + 9)
                    dve.tensor_copy(value[:, ds(c, 1), :, :].rearrange("p o t k -> p (o t) k"), best[:, :, 0:TOP])
                    dve.tensor_copy(expert[:, :, :], best_at[:, :, 0:TOP]).then_inc(pick, 1)
                    dve.wait_ge(pick, n + 10)
                    dve.tensor_tensor(picked[:, :, :, :].rearrange("p t k e -> p (t k) e"),
                                      iota[:, :].unsqueeze(1).to_broadcast([P, PICKS, E]),
                                      expert[:, :, :].rearrange("p t k -> p (t k)").unsqueeze(2).to_broadcast([P, PICKS, E]),
                                      ALU.is_equal).then_inc(pick, 1)
                    dve.wait_ge(pick, n + 11)
                    dve.tensor_tensor(chosen[:, :, :], picked[:, :, 0, :], picked[:, :, 1, :], ALU.add).then_inc(pick, 1)

                def assign(c):
                    n = PLACE * (c + 1)
                    dve.wait_ge(place_done, c + 1)
                    dve.tensor_reduce(chunk_sum[:, :], chosen[:, :, :].rearrange("p t e -> p e t"), AX_X, ALU.add).then_inc(placed, 1)
                    for k in range(TOP):
                        dve.tensor_tensor(at[:, :, k, :], picked[:, :, k, :], place_v, ALU.mult).then_inc(placed, 1)
                    dve.wait_ge(placed, n + 1)
                    dve.tensor_tensor(run[:, :], run[:, :], chunk_sum[:, :], ALU.add).then_inc(placed, 1)
                    dve.wait_ge(placed, n + 3)
                    dve.tensor_reduce(place[:, :, :].rearrange("p t k -> p (t k)"),
                                      at[:, :, :, :].rearrange("p t k e -> p (t k) e"), AX_X, ALU.add).then_inc(placed, 1)
                    dve.wait_ge(placed, n + 4)
                    dve.tensor_copy(run_b[:, :], run[:, :]).then_inc(placed, 1)
                    dve.wait_ge(placed, n + 5)
                    dve.scalar_tensor_tensor(out=slot[:, :, :], in0=expert[:, :, :], scalar=float(CAP), in1=place[:, :, :],
                                             op0=ALU.mult, op1=ALU.add).then_inc(placed, 1)
                    dve.tensor_scalar(far[:, :, :], place[:, :, :], float(CAP), FAR, ALU.is_ge, ALU.mult).then_inc(placed, 1)
                    dve.tensor_scalar(kept[:, ds(c, 1), :, :].rearrange("p o t k -> p (o t) k"), place[:, :, :], float(CAP), None,
                                      ALU.is_lt).then_inc(placed, 1)
                    dve.wait_ge(placed, n + 8)
                    if not isinstance(c, int) or c > 0:
                        dve.wait_ge(scattered, 16 * PICKS * c)
                        dve.wait_ge(user_next, c)
                        dve.tensor_scalar(user[:, :, :, :], user[:, :, :, :], CH, None, ALU.add).then_inc(user_next, 1)
                        dve.wait_ge(user_next, c + 1)
                    dve.tensor_tensor(target[:, :, :], slot[:, :, :], far[:, :, :], ALU.add).then_inc(placed, 1)

                split_o(0)
                normalise(0, True)
                split_o(1)
                normalise(1)
                split_o(2)
                choose(0)

                def step(c):
                    assign(c - 1)
                    normalise(c + 1)
                    split_o(c + 2)
                    choose(c)

                step(1)
                with dve.Fori(2, NCH - 2) as c:
                    step(c)
                assign(NCH - 3)
                normalise(NCH - 1)
                choose(NCH - 2)
                assign(NCH - 2)
                choose(NCH - 1)
                assign(NCH - 1)

                diff, ex, total, inv, den = w_tmp
                v0, v1 = value[:, :, :, 0], value[:, :, :, 1]
                dve.wait_ge(placed, PLACE * (NCH + 1))
                dve.tensor_tensor(diff[:, :, :], v1, v0, ALU.subtract).then_inc(weigh, 1)
                dve.wait_ge(exp_ready, 1)
                dve.tensor_scalar(total[:, :, :], ex[:, :, :], 1.0, None, ALU.add).then_inc(weigh, 1)
                dve.wait_ge(weigh, 2)
                dve.reciprocal(inv[:, :, :], total[:, :, :]).then_inc(weigh, 1)
                dve.wait_ge(weigh, 3)
                dve.tensor_tensor(w_gk[:, :, :, 0], inv[:, :, :], kept[:, :, :, 0], ALU.mult).then_inc(weigh, 1)
                dve.tensor_tensor(total[:, :, :], ex[:, :, :], inv[:, :, :], ALU.mult).then_inc(weigh, 1)
                dve.wait_ge(weigh, 5)
                dve.tensor_tensor(w_gk[:, :, :, 1], total[:, :, :], kept[:, :, :, 1], ALU.mult).then_inc(weigh, 1)
                dve.wait_ge(weigh, 6)
                dve.scalar_tensor_tensor(out=den[:, :, :], in0=w_gk[:, :, :, 0], scalar=1e-9, in1=w_gk[:, :, :, 1],
                                         op0=ALU.add, op1=ALU.add).then_inc(weigh, 1)
                dve.wait_ge(weigh, 7)
                dve.reciprocal(inv[:, :, :], den[:, :, :]).then_inc(weigh, 1)
                dve.wait_ge(weigh, 8)
                for k in range(TOP):
                    dve.scalar_tensor_tensor(out=weight[:, k, :, :], in0=w_gk[:, :, :, k], scalar=tanh_g[:, 1:2],
                                             in1=inv[:, :, :], op0=ALU.mult, op1=ALU.mult).then_inc(weigh, 1)

            @block.tensor
            def _(pe):
                pe.wait_ge(pool_const, 9)
                pe.wait_ge(wo_loaded, 16)
                for u in range(KT):
                    if u >= 2:
                        pe.wait_ge(wo_lo, u - 1)
                    for m in range(KT):
                        last = pe.transpose(turned[:, u % 2, m * P:(m + 1) * P], wo_raw[:, m, u * P:(u + 1) * P], ident[:, :])
                    last.then_inc(wo_turned, 1)
                pe.wait_ge(wo_lo, KT - 1)
                pe.wait_ge(small_loaded, 80)
                for k in range(KT):
                    last = pe.transpose(turned[:, KT % 2, k * E:(k + 1) * E], rw[:, k * P:(k + 1) * P], ident[0:E, 0:E])
                last.then_inc(wo_turned, 1)
                pe.wait_ge(wo_lo, WU)
                pe.wait_ge(dve_const, 4)

                def product(c, first=False):
                    pe.wait_ge(o_lo, c + 1)
                    for t in range(TPC):
                        if not first:
                            pe.wait_ge(x1_ready, TPC * (c - 1) + t + 1)
                        for k in range(KT):
                            last = split_matmul(pe, y_ps[:, t, :], oT[0][:, k, t * P:(t + 1) * P], oT[1][:, k, t * P:(t + 1) * P],
                                                woT[0][:, k, :], woT[1][:, k, :], k == 0, k == KT - 1)
                        last.then_inc(y_done, 1)

                def turn_and_score(c, first=False):
                    for t in range(TPC):
                        pe.wait_ge(xn_ready, TPC * c + t + 1)
                        if not first or t >= 2:
                            pe.wait_ge(xnT_ready, TPC * c + t - 1)
                        for k in range(KT):
                            last = pe.transpose(turned[:, t % 2, k * P:(k + 1) * P], xn[:, t, k * P:(k + 1) * P], ident[:, :])
                        last.then_inc(xn_turned, 1)
                    if not first:
                        pe.wait_ge(pick, PICK * (c - 1) + 1)
                    for t in range(TPC):
                        pe.wait_ge(xnT_ready, TPC * c + t + 1)
                        for k in range(KT):
                            last = pe.matmul(logit_ps[:, t * E:(t + 1) * E], xnT[:, k, t * P:(t + 1) * P], rwT[:, k, :],
                                             start=(k == 0), stop=(k == KT - 1))
                    last.then_inc(logits_done, 1)

                def places(c):
                    pe.wait_ge(pick, PICK * (c + 1))
                    pe.wait_ge(placed, PLACE * (c + 1))
                    for t in range(TPC):
                        out = place_ps[:, t * E:(t + 1) * E]
                        pe.matmul(out, before[:, :], chosen[:, t, :], start=True, stop=False)
                        for s in range(t):
                            pe.matmul(out, ones[:, :], chosen[:, s, :], start=False, stop=False)
                        last = pe.matmul(out, ones[:, :], run_b[:, :], start=False, stop=True)
                    last.then_inc(place_done, 1)

                product(0, True)
                product(1)
                turn_and_score(0, True)
                with pe.Fori(1, NCH - 1) as c:
                    places(c - 1)
                    product(c + 1)
                    turn_and_score(c)
                places(NCH - 2)
                turn_and_score(NCH - 1)
                places(NCH - 1)


class ExpertWeights:

    WC = 4

    def __init__(self, nc, ctx, z, a):
        self.LOADS = z.F // P // self.WC
        self.KT, self.FT = z.KT, z.F // P
        n = range(self.LOADS)
        self.w1 = [ctx.enter_context(nc.sbuf_tensor(f"w1_raw{c}", [P, z.KT, self.WC * P], F32)) for c in n]
        self.w2 = [ctx.enter_context(nc.sbuf_tensor(f"w2_raw{c}", [P, self.WC, z.D], F32)) for c in n]
        self.w1_loaded = [ctx.enter_context(nc.semaphore(f"w1_loaded{c}")) for c in n]
        self.w2_loaded = [ctx.enter_context(nc.semaphore(f"w2_loaded{c}")) for c in n]
        self.w1_dram = a["w1"].rearrange("e (k p) f -> p (e k) f", p=P)
        self.w2_dram = a["w2"].rearrange("e (t p) d -> p (e t) d", p=P)

    def load(self, sp, e, c):
        WC = self.WC
        sp.dma_start(self.w1[c][:, :, :], self.w1_dram[:, ds(self.KT * e, self.KT), c * WC * P:(c + 1) * WC * P]
                     ).then_inc(self.w1_loaded[c], 16)
        sp.dma_start(self.w2[c][:, :, :], self.w2_dram[:, ds(self.FT * e + WC * c, WC), :]).then_inc(self.w2_loaded[c], 16)


def run_experts(nc, z, a, scr, weights):
    KT, D, E, CAP, F = z.KT, z.D, z.E, z.CAP, z.F
    FT = F // P
    ST = CAP // P
    HALF = CAP // 2
    WC, NC = weights.WC, weights.LOADS
    RING = 4
    AHEAD = 3
    X_STEPS = tuple(range(5, 5 + 2 * ST, 2))
    PAIRS = E // 2
    with ExitStack() as ctx:
        def sb(name, shape, dt=F32):
            return ctx.enter_context(nc.sbuf_tensor("ex_" + name, shape, dt))

        def sem(name):
            return ctx.enter_context(nc.semaphore("ex_" + name))

        ident = sb("ident", [P, P])
        b1_raw = sb("b1_raw", [P, 2, P])
        b1T = sb("b1T", [P, E * FT])
        user = [sb(f"user{i}", [P, ST, 2], I32) for i in range(2)]
        rows = sb("rows", [P, ST, D])
        slot_weight = [sb(f"slot_weight{i}", [P, ST]) for i in range(2)]
        xT_hi = [sb(f"xT_hi{i}", [P, KT, CAP], F32R) for i in range(2)]
        xT_lo = [sb(f"xT_lo{i}", [P, KT, CAP], F32R) for i in range(2)]
        w1_raw, w2_raw = weights.w1, weights.w2
        w1_hi = [sb(f"w1_hi{i}", [P, KT, P], F32R) for i in range(RING)]
        w1_lo = [sb(f"w1_lo{i}", [P, KT, P], F32R) for i in range(RING)]
        w2_hi = [sb(f"w2_hi{i}", [P, D], F32R) for i in range(RING)]
        w2_lo = [sb(f"w2_lo{i}", [P, D], F32R) for i in range(RING)]
        hid = [sb(f"hid{i}", [P, CAP]) for i in range(2)]
        hid_hi = [sb(f"hid_hi{i}", [P, CAP], F32R) for i in range(2)]
        hid_lo = [sb(f"hid_lo{i}", [P, CAP], F32R) for i in range(2)]
        b2 = [sb(f"b2_{i}", [P, D]) for i in range(2)]
        total = sb("total", [P, ST, D])
        result = sb("result", [P, ST, D])
        acc = ctx.enter_context(nc.psum_tensor("ex_acc", [P, ST, 512], F32))
        first_ps = [ctx.enter_context(nc.psum_tensor(f"ex_first{i}", [P, 512], F32)) for i in range(2)]
        turned = ctx.enter_context(nc.psum_tensor("ex_turned", [P, 512], F32))

        act_passed, pool_passed = sem("act_passed"), sem("pool_passed")
        ident_ready, b1_loaded, b1_turned, b1_ready = sem("ident_ready"), sem("b1_loaded"), sem("b1_turned"), sem("b1_ready")
        w1_loaded, w2_loaded = weights.w1_loaded, weights.w2_loaded
        w_hi, w_lo = sem("w_hi"), sem("w_lo")
        w_free = sem("w_free")
        user_loaded = [sem(f"user_loaded{i}") for i in range(2)]
        gathered = sem("gathered")
        weight_gathered = [sem(f"weight_gathered{i}") for i in range(2)]
        x_turned, x_hi, x_lo = sem("x_turned"), sem("x_hi"), sem("x_lo")
        first_done = sem("first_done")
        first_free = sem("first_free")
        hid_free = sem("hid_free")
        hid_hi_done, hid_ready = sem("hid_hi_done"), sem("hid_ready")
        acc_done = sem("acc_done")
        acc_free = sem("acc_free")
        b2_loaded = [sem(f"b2_loaded{i}") for i in range(2)]
        weighted = sem("weighted")
        added = sem("added")

        with nc.Block() as block:
            @block.sync
            def _(sp):
                sp.dma_start(b1_raw[:, :, :], a["b1"].rearrange("(h e) (t p) -> (e t) h p", h=2, p=P)).then_inc(b1_loaded, 16)
                with sp.Fori(1, E) as e:
                    for c in range(NC):
                        sp.wait_ge(w_lo, FT * (e - 1) + WC * (c + 1))
                        weights.load(sp, e, c)

            @block.gpsimd
            def _(pool):
                make_identity(nc, pool, ident, ident_ready)

                def load_b2(e, i):
                    pool.dma_start(b2[i][:, :], a["b2"][ds(e, 1), :].to_broadcast([P, D])).then_inc(b2_loaded[i], 16)

                def gather(e, i, use):
                    pool.dma_start(user[i][:, :, :], scr["user_of"][ds(CAP * e, CAP), :].rearrange("(s p) o -> p s o", p=P)
                                   ).then_inc(user_loaded[i], 16)
                    pool.wait_ge(user_loaded[i], 16 * (use + 1))
                    settle(pool, pool_passed)
                    for s in range(ST):
                        pool.indirect_dma_start(rows[:, s, :], None, scr["xn"],
                                                bass.IndirectOffsetOnAxis(user[i][:, s, 0:1], 0),
                                                bounds_check=z.TOK + CAP - 1, oob_is_err=False).then_inc(gathered, 16)
                    for s in range(ST):
                        pool.indirect_dma_start(slot_weight[i][:, s:s + 1], None, scr["weight"],
                                                bass.IndirectOffsetOnAxis(user[i][:, s, 1:2], 0),
                                                bounds_check=2 * z.TOK + CAP - 1, oob_is_err=False).then_inc(weight_gathered[i], 16)

                def add_results(e, i):
                    for s in range(ST):
                        pool.wait_ge(weighted, ST * e + s + 1)
                        settle(pool, pool_passed)
                        pool.indirect_dma_start(scr["out"], bass.IndirectOffsetOnAxis(user[i][:, s, 0:1], 0),
                                                result[:, s, :], None, bounds_check=z.TOK + CAP - 1,
                                                compute_op=ALU.add).then_inc(added, 16)
                    pool.wait_ge(added, 16 * ST * (e + 1))
                    settle(pool, pool_passed)

                with nc.allow_non_contiguous_dma(reason="640 slots' users, 8 bytes each"):
                    gather(0, 0, 0)
                    load_b2(0, 0)
                    load_b2(1, 1)
                    pool.wait_ge(x_turned, ST)
                    gather(1, 1, 0)
                    with pool.Fori(0, PAIRS - 1) as j:
                        for i in range(2):
                            e = 2 * j + i
                            add_results(e, i)
                            load_b2(e + 2, i)
                            pool.wait_ge(x_turned, ST * (e + 2))
                            gather(e + 2, i, j + 1)
                    for i in range(2):
                        add_results(E - 2 + i, i)

            @block.scalar
            def _(act):
                def split_w(e, f):
                    c, r = f // WC, f % RING
                    if f % WC == 0:
                        act.wait_ge(w1_loaded[c], 16 * (e + 1))
                        act.wait_ge(w2_loaded[c], 16 * (e + 1))
                    act.wait_ge(w_free, FT * e + f + 1)
                    act.activation(w1_hi[r][:, :, :], w1_raw[c][:, :, (f % WC) * P:(f % WC + 1) * P], ACT.Copy)
                    act.activation(w2_hi[r][:, :], w2_raw[c][:, f % WC, :], ACT.Copy).then_inc(w_hi, 1)

                def split_x(e, i, s):
                    act.wait_ge(x_turned, ST * e + s + 1)
                    act.activation(xT_hi[i][:, :, s * P:(s + 1) * P], turned[:, :].rearrange("p (k n) -> p k n", n=P),
                                   ACT.Copy).then_inc(x_hi, 1)

                def gelu(e, f):
                    act.wait_ge(hid_free, FT * e + f + 1)
                    for h in range(2):
                        act.wait_ge(first_done, 2 * (FT * e + f) + h + 1)
                        settle(act, act_passed)
                        act.activation(hid[f % 2][:, h * HALF:(h + 1) * HALF], first_ps[h][:, 0:HALF], ACT.Gelu,
                                       bias=b1T[:, ds(FT * e + f, 1)]).then_inc(first_free, 1)

                def weigh(e, i, use):
                    act.wait_ge(weight_gathered[i], 16 * ST * (use + 1))
                    if not isinstance(e, int) or e > 0:
                        act.wait_ge(added, 16 * ST * e)
                    for s in range(ST):
                        act.wait_ge(acc_free, ST * (e + 1) + s + 1)
                        act.activation(result[:, s, :], total[:, s, :], ACT.Identity,
                                       scale=slot_weight[i][:, s:s + 1]).then_inc(weighted, 1)

                def expert(e, i, use, first=False, last=False):
                    for f in range(FT):
                        if not (last and f + AHEAD >= FT):
                            split_w(e + (f + AHEAD) // FT, (f + AHEAD) % FT)
                        if not (last and f + 1 >= FT):
                            gelu(e + (f + 1) // FT, (f + 1) % FT)
                        if f == 0 and not first:
                            weigh(e - 1, 1 - i, use - 1 + i)
                        if f in X_STEPS and not last:
                            split_x(e + 1, 1 - i, X_STEPS.index(f))

                for s in range(ST):
                    split_x(0, 0, s)
                for f in range(AHEAD):
                    split_w(0, f)
                act.wait_ge(b1_ready, 1)
                gelu(0, 0)
                expert(0, 0, 0, first=True)
                expert(1, 1, 0)
                with act.Fori(1, PAIRS - 1) as j:
                    for i in range(2):
                        expert(2 * j + i, i, j)
                expert(E - 2, 0, PAIRS - 1)
                expert(E - 1, 1, PAIRS - 1, last=True)
                weigh(E - 1, 1, PAIRS - 1)

            @block.vector
            def _(dve):
                def split_w(e, f):
                    c, r = f // WC, f % RING
                    dve.wait_ge(w_hi, FT * e + f + 1)
                    dve.tensor_tensor(w1_lo[r][:, :, :], w1_raw[c][:, :, (f % WC) * P:(f % WC + 1) * P],
                                      w1_hi[r][:, :, :].bitcast(F32), ALU.subtract)
                    dve.tensor_tensor(w2_lo[r][:, :], w2_raw[c][:, f % WC, :], w2_hi[r][:, :].bitcast(F32),
                                      ALU.subtract).then_inc(w_lo, 1)

                def split_x(e, i, s):
                    dve.wait_ge(x_hi, ST * e + s + 1)
                    dve.tensor_tensor(xT_lo[i][:, :, s * P:(s + 1) * P], turned[:, :].rearrange("p (k n) -> p k n", n=P),
                                      xT_hi[i][:, :, s * P:(s + 1) * P].bitcast(F32), ALU.subtract).then_inc(x_lo, 1)

                def split_hid(e, f):
                    n, r = FT * e + f, f % 2
                    dve.wait_ge(first_free, 2 * n + 4)
                    dve.wait_ge(w_free, n + RING - 1)
                    dve.tensor_copy(hid_hi[r][:, :], hid[r][:, :]).then_inc(hid_hi_done, 1)
                    dve.wait_ge(hid_hi_done, n + 1)
                    dve.tensor_tensor(hid_lo[r][:, :], hid[r][:, :], hid_hi[r][:, :].bitcast(F32), ALU.subtract).then_inc(hid_free, 1)

                def finish(e, i, use):
                    dve.wait_ge(b2_loaded[i], 16 * (use + 1))
                    if not isinstance(e, int) or e > 0:
                        dve.wait_ge(weighted, ST * e)
                    for s in range(ST):
                        if s < ST - 1:
                            dve.wait_ge(acc_done, (ST - 1) * e + s + 1)
                        else:
                            dve.wait_ge(w_free, RING + FT * (e + 1))
                        dve.tensor_tensor(total[:, s, :], acc[:, s, :], b2[i][:, :], ALU.add).then_inc(acc_free, 1)

                def expert(e, i, j, first, last):
                    for f in range(FT):
                        if f == 0 and not first:
                            finish(e - 1, 1 - i, j - 1 + i)
                        if not (last and f + AHEAD >= FT):
                            split_w(e + (f + AHEAD) // FT, (f + AHEAD) % FT)
                        if not (last and f + 1 >= FT):
                            split_hid(e + (f + 1) // FT, (f + 1) % FT)
                        if f in X_STEPS and not last:
                            split_x(e + 1, 1 - i, X_STEPS.index(f))

                dve.sem_inc(acc_free, ST)
                dve.sem_inc(first_free, 2)
                dve.sem_inc(hid_free, 2)
                dve.sem_inc(w_free, RING)
                dve.wait_ge(b1_turned, 1)
                dve.tensor_copy(b1T[:, :], turned[:, 0:2 * P]).then_inc(b1_ready, 1)
                for s in range(ST):
                    split_x(0, 0, s)
                for f in range(AHEAD):
                    split_w(0, f)
                split_hid(0, 0)
                expert(0, 0, 0, True, False)
                expert(1, 1, 0, False, False)
                with dve.Fori(1, PAIRS - 1) as j:
                    for i in range(2):
                        expert(2 * j + i, i, j, False, False)
                expert(E - 2, 0, PAIRS - 1, False, False)
                expert(E - 1, 1, PAIRS - 1, False, True)
                finish(E - 1, 1, PAIRS - 1)

            @block.tensor
            def _(pe):
                def turn(e, s):
                    if s == 0:
                        pe.wait_ge(gathered, 16 * ST * (e + 1))
                    if s or not isinstance(e, int) or e > 0:
                        pe.wait_ge(x_lo, ST * e + s)
                    for k in range(KT):
                        last = pe.transpose(turned[:, k * P:(k + 1) * P], rows[:, s, k * P:(k + 1) * P], ident[:, :])
                    last.then_inc(x_turned, 1)

                def first(e, i, f):
                    n, r = FT * e + f, f % RING
                    pe.wait_ge(w_lo, n + 1)
                    if f == 0:
                        pe.wait_ge(x_lo, ST * (e + 1))
                    for h in range(2):
                        pe.wait_ge(first_free, 2 * n + h + 1)
                        sl = slice(h * HALF, (h + 1) * HALF)
                        for k in range(KT):
                            last = split_matmul(pe, first_ps[h][:, 0:HALF], w1_hi[r][:, k, :], w1_lo[r][:, k, :],
                                                xT_hi[i][:, k, sl], xT_lo[i][:, k, sl], k == 0, k == KT - 1)
                        last.then_inc(first_done, 1)

                def second(e, f):
                    n, r = FT * e + f, f % RING
                    pe.wait_ge(hid_free, n + 3)
                    for s in range(ST):
                        if f == 0:
                            pe.wait_ge(acc_free, ST * e + s + 1)
                        sl = slice(s * P, (s + 1) * P)
                        last = split_matmul(pe, acc[:, s, :], hid_hi[f % 2][:, sl], hid_lo[f % 2][:, sl],
                                            w2_hi[r][:, :], w2_lo[r][:, :], f == 0, f == FT - 1)
                        if f == FT - 1 and s < ST - 1:
                            last.then_inc(acc_done, 1)
                    last.then_inc(w_free, 1)

                def expert(e, i, j, last):
                    for f in range(FT):
                        if not (last and f + 1 >= FT):
                            first(e + (f + 1) // FT, (i + (f + 1) // FT) % 2, (f + 1) % FT)
                        if f in X_STEPS and not last:
                            turn(e + 1, X_STEPS.index(f))
                        second(e, f)

                pe.wait_ge(ident_ready, 2)
                pe.wait_ge(b1_loaded, 16)
                for h in range(2):
                    last = pe.transpose(turned[:, h * P:(h + 1) * P], b1_raw[:, h, :], ident[:, :])
                last.then_inc(b1_turned, 1)
                pe.wait_ge(b1_ready, 1)
                for s in range(ST):
                    turn(0, s)
                first(0, 0, 0)
                with pe.Fori(0, PAIRS - 1) as j:
                    for i in range(2):
                        expert(2 * j + i, i, j, False)
                expert(E - 2, 0, PAIRS - 1, False)
                expert(E - 1, 1, PAIRS - 1, True)


INPUTS = ("x", "ctx_1024", "g_xattn", "g_ffn", "L0_xattn_Wq", "L0_xattn_bq", "L0_xattn_Wk", "L0_xattn_bk",
          "L0_xattn_Wv", "L0_xattn_bv", "L0_xattn_Wo", "L0_xattn_bo", "L0_ffn_router_w", "L0_ffn_router_b",
          "L0_ffn_w1", "L0_ffn_b1", "L0_ffn_w2", "L0_ffn_b2")


def gated_attention_and_experts(nc, z, a, out):
    def dram(name, shape, dt=F32):
        return nc.dram_tensor(name, shape, dt).ap()

    scr = dict(qk=dram("scr_qk", [2, 2, z.KT, P, z.TOK]),
               v=dram("scr_v", [z.TOK, z.D]),
               o=dram("scr_o", [z.D, z.TOK]),
               xn=dram("scr_xn", [z.TOK + z.CAP, z.D]),
               weight=dram("scr_weight", [2 * z.TOK + z.CAP, 1]),
               user_of=dram("scr_user_of", [z.E * z.CAP, 2], I32),
               out=out)
    project_inputs(nc, z, a, scr)
    attend(nc, z, scr)
    with ExitStack() as ctx:
        weights = ExpertWeights(nc, ctx, z, a)
        route(nc, z, a, scr, weights)
        run_experts(nc, z, a, scr, weights)


def kernel(**inputs):
    import numpy as np
    from concourse import bacc
    from concourse.bass_utils import run_bass_kernel_spmd

    nc = bacc.Bacc("TRN2", target_bir_lowering=False, num_devices=1)
    z = Shapes(inputs["x"], inputs["L0_ffn_w1"])
    arrays, a = {}, {}
    for name in INPUTS:
        v = np.ascontiguousarray(inputs[name])
        if name in ("x", "ctx_1024"):
            v = v.reshape(z.TOK, z.D)
        arrays[name] = v
        short = {"ctx_1024": "ctx"}.get(name, name.removeprefix("L0_xattn_").removeprefix("L0_ffn_"))
        a[short] = nc.dram_tensor(name, v.shape, mybir.dt.from_np(v.dtype), kind="ExternalInput").ap()
    out = nc.dram_tensor("out", (z.TOK + z.CAP, z.D), F32, kind="ExternalOutput").ap()
    gated_attention_and_experts(nc, z, a, out)
    result = run_bass_kernel_spmd(nc, [arrays], core_ids=[0])
    return result.results[0]["out"][:z.TOK].reshape(z.B, z.S, z.D)
```

```python
from contextlib import ExitStack

import concourse.bass as bass
from concourse import mybir

F32 = mybir.dt.float32
F32R = mybir.dt.float32r
BF16 = mybir.dt.bfloat16
I32 = mybir.dt.int32
U32 = mybir.dt.uint32
ALU = mybir.AluOpType
ACT = mybir.ActivationFunctionType
AX_X = mybir.AxisListType.X
ds = bass.ds

P = 128
EPS = 1e-5


class Shapes:

    def __init__(self, x, w1):
        self.B, self.S, self.D = x.shape
        self.E, _, self.F = w1.shape
        self.H = 16
        self.HD = self.D // self.H
        self.TOP = 2
        self.TOK = self.B * self.S
        self.CAP = -(-5 * self.TOK * self.TOP // (4 * self.E))
        self.KT = self.D // P
        self.CH = 512
        self.NCH = self.TOK // self.CH
        self.TPC = self.CH // P
        self.NT = self.TOK // P


def split_matmul(pe, out, w_hi, w_lo, m_hi, m_lo, first, last):
    pe.matmul(out, w_hi, m_hi, start=first, stop=False)
    pe.matmul(out, w_hi, m_lo, start=False, stop=False)
    return pe.matmul(out, w_lo, m_hi, start=False, stop=last)


def settle(engine, passed):
    engine.sem_inc(passed, 1)


def make_identity(nc, pool, ident, ready):
    pool.memset(ident[:, :], 0.0).then_inc(ready, 1)
    pool.wait_ge(ready, 1)
    pool.affine_select(out=ident[:, :], in_=ident[:, :], compare_op=ALU.not_equal, fill=1.0, base=0,
                       pattern=[[-1, P]], channel_multiplier=1).then_inc(ready, 1)


class Stacks:

    def __init__(self, nc, ctx, z, w):
        self.z, hpg = z, P // z.HD
        self.q = ctx.enter_context(nc.sbuf_tensor(f"at_q{w}", [P, hpg, z.S], F32R))
        self.k = ctx.enter_context(nc.sbuf_tensor(f"at_k{w}", [P, hpg, z.S], F32R))
        self.loaded = [ctx.enter_context(nc.semaphore(f"at_qk_loaded{w}{j}")) for j in range(hpg)]

    def load(self, sp, scr, b, g):
        HD, S = self.z.HD, self.z.S
        for j, loaded in enumerate(self.loaded):
            for dst, t, parts in ((self.q, 0, (0, 1, 0)), (self.k, 1, (0, 0, 1))):
                for i, part in enumerate(parts):
                    src = scr["qk"][t, part].rearrange("g p n -> (g p) n")
                    sp.dma_start(dst[i * HD:(i + 1) * HD, j, :].bitcast(F32),
                                 src[ds(g * P + j * HD, HD), ds(b * S, S)]).then_inc(loaded, 16)


def project_inputs(nc, z, a, scr, stacks):
    KT, CH, TPC, NCH, D = z.KT, z.CH, z.TPC, z.NCH, z.D
    with ExitStack() as ctx:
        def sb(name, shape, dt=F32):
            return ctx.enter_context(nc.sbuf_tensor(name, shape, dt))

        def sem(name):
            return ctx.enter_context(nc.semaphore(name))

        ident = sb("pi_ident", [P, P])
        eps = sb("pi_eps", [P, 1])
        w_raw = sb("pi_w_raw", [P, 3, KT, D])
        wT_hi = sb("pi_wT_hi", [P, 3, KT, D], F32R)
        wT_lo = sb("pi_wT_lo", [P, 3, KT, D], F32R)
        b_qk = sb("pi_b_qk", [P, 2, KT])
        b_v = sb("pi_b_v", [P, D])
        x_raw = sb("pi_x_raw", [P, TPC, D])
        c_raw = sb("pi_c_raw", [P, TPC, D])
        xn = sb("pi_xn", [P, TPC, D])
        stats = sb("pi_stats", [P, TPC, 6])
        mv = sb("pi_mv", [P, TPC, 2])
        std = sb("pi_std", [P, TPC])
        rstd = sb("pi_rstd", [P, TPC])
        xT = [sb("pi_xT_hi", [P, KT, CH], F32R), sb("pi_xT_lo", [P, KT, CH], F32R)]
        cT = [sb("pi_cT_hi", [P, KT, CH], F32R), sb("pi_cT_lo", [P, KT, CH], F32R)]
        qk_out = sb("pi_qk_out", [P, 2, 2, KT, CH], F32R)
        v_out = sb("pi_v_out", [P, TPC, D])
        turned = ctx.enter_context(nc.psum_tensor("pi_turned", [P, 4, 512], F32))
        projected = ctx.enter_context(nc.psum_tensor("pi_projected", [P, 4, 512], F32))

        dve_passed = sem("pi_dve_passed")
        ident_ready, eps_ready = sem("pi_ident_ready"), sem("pi_eps_ready")
        w_loaded, b_loaded = [sem(f"pi_w_loaded{i}") for i in range(3)], sem("pi_b_loaded")
        x_loaded, c_loaded = sem("pi_x_loaded"), sem("pi_c_loaded")
        var_ready, std_ready, rstd_ready = sem("pi_var_ready"), sem("pi_std_ready"), sem("pi_rstd_ready")
        xn_ready = sem("pi_xn_ready")
        turn_done, hi_done, lo_done = sem("pi_turn_done"), sem("pi_hi_done"), sem("pi_lo_done")
        proj_done = sem("pi_proj_done")
        qk_hi_done, proj_read = sem("pi_qk_hi_done"), sem("pi_proj_read")
        stored = [sem(f"pi_stored{i}") for i in range(5)]

        WU = 3 * KT

        def x_units(n):
            return WU + TPC + 2 * TPC * n

        def c_units(n):
            return x_units(n) + TPC

        with nc.Block() as block:
            @block.sync
            def _(sp):
                def load(dst, src, n, done):
                    sp.dma_start(dst[:, :, :], src[ds(n * CH, CH), :].rearrange("(t p) c -> p t c", p=P)).then_inc(done, 16)

                for i, w in enumerate(("Wq", "Wk", "Wv")):
                    sp.dma_start(w_raw[:, i], a[w].rearrange("(m p) c -> p m c", p=P)).then_inc(w_loaded[i], 16)
                    if i == 0:
                        load(x_raw, a["x"], 0, x_loaded)
                with nc.allow_non_contiguous_dma(reason="512 elements each"):
                    sp.dma_start(b_qk[:, 0, :], a["bq"].rearrange("(m p) -> p m", p=P)).then_inc(b_loaded, 16)
                    sp.dma_start(b_qk[:, 1, :], a["bk"].rearrange("(m p) -> p m", p=P)).then_inc(b_loaded, 16)
                sp.dma_start(b_v[:, :], a["bv"].rearrange("(o c) -> o c", o=1).to_broadcast([P, D])).then_inc(b_loaded, 16)

                load(c_raw, a["ctx"], 0, c_loaded)
                sp.wait_ge(xn_ready, TPC)
                load(x_raw, a["x"], 1, x_loaded)
                with sp.Fori(0, NCH - 2) as n:
                    sp.wait_ge(turn_done, c_units(n))
                    load(c_raw, a["ctx"], n + 1, c_loaded)
                    sp.wait_ge(xn_ready, TPC * (n + 2))
                    load(x_raw, a["x"], n + 2, x_loaded)
                sp.wait_ge(turn_done, c_units(NCH - 2))
                load(c_raw, a["ctx"], NCH - 1, c_loaded)
                for i in range(4):
                    sp.wait_ge(stored[i], 16 * (z.S // CH))
                stacks.load(sp, scr, 0, 0)

            @block.gpsimd
            def _(pool):
                pool.memset(eps[:, :], EPS).then_inc(eps_ready, 1)
                make_identity(nc, pool, ident, ident_ready)
                with pool.Fori(0, NCH) as n:
                    for i in range(4):
                        t, part = i // 2, i % 2
                        if part == 0:
                            pool.wait_ge(qk_hi_done, 2 * KT * n + KT * (t + 1))
                        else:
                            pool.wait_ge(proj_read, 3 * KT * n + KT * (t + 1))
                        pool.dma_start(scr["qk"][t, part].rearrange("g p n -> p g n")[:, :, ds(n * CH, CH)],
                                       qk_out[:, t, part].bitcast(F32)).then_inc(stored[i], 16)
                    pool.wait_ge(proj_read, 3 * KT * n + 3 * KT)
                    pool.dma_start(scr["v"][ds(n * CH, CH), :].rearrange("(t p) c -> p t c", p=P),
                                   v_out[:, :, :]).then_inc(stored[4], 16)
                for i in range(5):
                    pool.wait_ge(stored[i], 16 * NCH)

            def unit_hi(u, bank, dst):
                nc.scalar.wait_ge(turn_done, u + 1)
                nc.scalar.activation(dst, turned[:, bank, :].rearrange("p (k t) -> p k t", t=P), ACT.Copy).then_inc(hi_done, 1)

            def unit_lo(u, bank, dst, hi):
                nc.vector.wait_ge(hi_done, u + 1)
                nc.vector.tensor_tensor(dst, turned[:, bank, :].rearrange("p (k t) -> p k t", t=P), hi.bitcast(F32),
                                        ALU.subtract).then_inc(lo_done, 1)

            def w_part(w, k):
                return w[:, k // KT, k % KT, :].rearrange("p (k t) -> p k t", t=P)

            @block.scalar
            def _(act):
                def std_of(n):
                    act.wait_ge(var_ready, n + 1)
                    act.activation(std[:, :], mv[:, :, 1], ACT.Sqrt, bias=eps[:, 0:1]).then_inc(std_ready, 1)

                def qk_hi(n, t):
                    if not isinstance(n, int) or n > 0:
                        act.wait_ge(stored[2 * t], 16 * n)
                    for m in range(KT):
                        o = 3 * KT * n + KT * t + m
                        act.wait_ge(proj_done, o + 1)
                        act.activation(qk_out[:, t, 0, m, :], projected[:, m, :], ACT.Identity,
                                       bias=b_qk[:, t, m:m + 1]).then_inc(qk_hi_done, 1)

                act.wait_ge(eps_ready, 1)
                for k in range(WU):
                    unit_hi(k, k % 4, w_part(wT_hi, k))
                    if k == KT - 1:
                        std_of(0)
                act.wait_ge(b_loaded, 48)
                for t in range(TPC):
                    unit_hi(WU + t, t, xT[0][:, :, t * P:(t + 1) * P])

                def chunk(n, last):
                    if not last:
                        std_of(n + 1)
                    for t in range(TPC):
                        unit_hi(x_units(n) + t, t, cT[0][:, :, t * P:(t + 1) * P])
                    qk_hi(n, 0)
                    if not last:
                        for t in range(TPC):
                            unit_hi(c_units(n) + t, t, xT[0][:, :, t * P:(t + 1) * P])
                    qk_hi(n, 1)

                chunk(0, False)
                with act.Fori(1, NCH - 1) as n:
                    chunk(n, False)
                chunk(NCH - 1, True)

            @block.vector
            def _(dve):
                def normalise(n):
                    dve.wait_ge(x_loaded, 16 * (n + 1))
                    for t in range(TPC):
                        last = dve.bn_stats(stats[:, t, :], x_raw[:, t, :])
                    last.then_inc(rstd_ready, 1)
                    dve.wait_ge(rstd_ready, 2 * n + 1)
                    settle(dve, dve_passed)
                    for t in range(TPC):
                        last = dve.bn_aggr(mv[:, t, :], stats[:, t, :])
                    last.then_inc(var_ready, 1)
                    dve.wait_ge(std_ready, n + 1)
                    dve.reciprocal(rstd[:, :], std[:, :]).then_inc(rstd_ready, 1)
                    dve.wait_ge(rstd_ready, 2 * n + 2)
                    if not isinstance(n, int) or n > 0:
                        dve.wait_ge(turn_done, x_units(n) - 2 * TPC)
                    for t in range(TPC):
                        dve.tensor_scalar(xn[:, t, :], x_raw[:, t, :], mv[:, t, 0:1], rstd[:, t:t + 1],
                                          ALU.subtract, ALU.mult).then_inc(xn_ready, 1)

                def qk_lo(n, t):
                    if not isinstance(n, int) or n > 0:
                        dve.wait_ge(stored[2 * t + 1], 16 * n)
                    for m in range(KT):
                        dve.wait_ge(qk_hi_done, 2 * KT * n + KT * t + m + 1)
                        dve.scalar_tensor_tensor(out=qk_out[:, t, 1, m, :], in0=projected[:, m, :],
                                                 scalar=b_qk[:, t, m:m + 1], in1=qk_out[:, t, 0, m, :].bitcast(F32),
                                                 op0=ALU.add, op1=ALU.subtract).then_inc(proj_read, 1)

                for k in range(WU):
                    unit_lo(k, k % 4, w_part(wT_lo, k), w_part(wT_hi, k))
                    if k == KT - 1:
                        normalise(0)
                dve.wait_ge(b_loaded, 48)
                for t in range(TPC):
                    sl = slice(t * P, (t + 1) * P)
                    unit_lo(WU + t, t, xT[1][:, :, sl], xT[0][:, :, sl])

                def chunk(n, last):
                    if not last:
                        normalise(n + 1)
                    for t in range(TPC):
                        sl = slice(t * P, (t + 1) * P)
                        unit_lo(x_units(n) + t, t, cT[1][:, :, sl], cT[0][:, :, sl])
                    qk_lo(n, 0)
                    if not last:
                        for t in range(TPC):
                            sl = slice(t * P, (t + 1) * P)
                            unit_lo(c_units(n) + t, t, xT[1][:, :, sl], xT[0][:, :, sl])
                    qk_lo(n, 1)
                    if not isinstance(n, int) or n > 0:
                        dve.wait_ge(stored[4], 16 * n)
                    for t in range(TPC):
                        dve.wait_ge(proj_done, 3 * KT * n + 2 * KT + t + 1)
                        dve.tensor_tensor(v_out[:, t, :], projected[:, t, :], b_v[:, :], ALU.add).then_inc(proj_read, 1)

                chunk(0, False)
                with dve.Fori(1, NCH - 1) as n:
                    chunk(n, False)
                chunk(NCH - 1, True)

            @block.tensor
            def _(pe):
                def turn(u, bank, src, free):
                    if free:
                        pe.wait_ge(lo_done, u - 3)
                    for k in range(KT):
                        last = pe.transpose(turned[:, bank, k * P:(k + 1) * P], src(k), ident[:, :])
                    last.then_inc(turn_done, 1)

                def turn_x(n):
                    for t in range(TPC):
                        pe.wait_ge(xn_ready, TPC * n + t + 1)
                        turn(x_units(n) - TPC + t, t, lambda k: xn[:, t, k * P:(k + 1) * P], True)

                def project_qk(n, t, src, ready):
                    pe.wait_ge(lo_done, ready)
                    for m in range(KT):
                        if t or not isinstance(n, int) or n > 0:
                            pe.wait_ge(proj_read, 3 * KT * n + KT * t + m + 1 - 4)
                        for k in range(KT):
                            last = split_matmul(pe, projected[:, m, :], wT_hi[:, t, k, m * P:(m + 1) * P],
                                                wT_lo[:, t, k, m * P:(m + 1) * P], src[0][:, k, :], src[1][:, k, :],
                                                k == 0, k == KT - 1)
                        last.then_inc(proj_done, 1)

                pe.wait_ge(ident_ready, 2)
                for k in range(WU):
                    if k % KT == 0:
                        pe.wait_ge(w_loaded[k // KT], 16)
                    turn(k, k % 4, lambda m: w_raw[:, k // KT, m, (k % KT) * P:(k % KT + 1) * P], k >= 4)
                turn_x(0)

                def chunk(n, first, last):
                    pe.wait_ge(c_loaded, 16 * (n + 1))
                    for t in range(TPC):
                        turn(x_units(n) + t, t, lambda k: c_raw[:, t, k * P:(k + 1) * P], True)
                    project_qk(n, 0, xT, x_units(n))
                    if not last:
                        turn_x(n + 1)
                    project_qk(n, 1, cT, c_units(n))
                    for t in range(TPC):
                        pe.wait_ge(proj_read, 3 * KT * n + 2 * KT + t + 1 - 4)
                        for k in range(KT):
                            last_mm = split_matmul(pe, projected[:, t, :], cT[0][:, k, t * P:(t + 1) * P],
                                                   cT[1][:, k, t * P:(t + 1) * P], wT_hi[:, 2, k, :], wT_lo[:, 2, k, :],
                                                   k == 0, k == KT - 1)
                        last_mm.then_inc(proj_done, 1)

                chunk(0, True, False)
                with pe.Fori(1, NCH - 1) as n:
                    chunk(n, False, False)
                chunk(NCH - 1, False, True)


def attend(nc, z, scr, stacks):
    B, S, HD, KT = z.B, z.S, z.HD, z.KT
    HPG = P // HD
    G_ALL = B * z.H // HPG
    PAIRS = G_ALL // 2
    QT = S // P
    QH = S // 512
    STEPS = QT * QH
    UNITS = HPG * QT
    ROWS = 3 * HD
    SCALE = float(HD) ** -0.5
    RING = 8
    HP = HPG - 1
    STACKS = 3
    TURN_STEP = STEPS - 3
    LEAD = UNITS - 2 * TURN_STEP
    UNITS_AT = [[(1, LEAD + 2 * T + i) if T < TURN_STEP else (2, 2 * (T - TURN_STEP) + i) for i in range(2)]
                for T in range(STEPS)]
    assert HPG == 4 and QH == 2

    with ExitStack() as ctx:
        def sb(name, shape, dt=F32):
            return ctx.enter_context(nc.sbuf_tensor(name, shape, dt))

        def ps(name, shape):
            return ctx.enter_context(nc.psum_tensor(name, shape, F32))

        def sem(name):
            return ctx.enter_context(nc.semaphore(name))

        ident = sb("at_ident", [P, P])
        ones = sb("at_ones", [P, HD])
        stacks = [stacks] + [Stacks(nc, ctx, z, w) for w in range(1, STACKS)]
        q_st, k_st, qk_loaded = [st.q for st in stacks], [st.k for st in stacks], [st.loaded for st in stacks]
        v_sb = [sb(f"at_v{e}", [P, QT, P]) for e in range(2)]
        maxima = [sb(f"at_max{e}", [P, P]) for e in range(2)]
        neg_max = [sb(f"at_negmax{e}", [UNITS, P], F32R) for e in range(2)]
        probs = [sb(f"at_probs{r}", [P, HPG, 512]) for r in range(RING)]
        psum_k = [sb(f"at_keysum{h}", [P, HPG, 512]) for h in range(QH)]
        o_raw = [sb(f"at_o_raw{h}", [P, 512]) for h in range(QH)]
        den_t = sb("at_den_t", [P, 512])
        recip_t = sb("at_recip_t", [P, 512 // 32])
        recip = sb("at_recip", [P, 512])
        o_out = [sb(f"at_o_out{h}", [P, 512]) for h in range(QH)]
        unit_ps = [ps(f"at_unit_ps{i}", [P, 2, 512]) for i in range(2)]
        score_ps = [ps(f"at_score_ps{i}", [P, 512]) for i in range(2)]
        pv_ps = ps("at_pv_ps", [P, 512])
        den_ps = ps("at_den_ps", [P, 512])

        const_ready, maxima_zero = sem("at_const_ready"), sem("at_maxima_zero")
        ident_ready = sem("at_ident_ready")
        v_loaded = [sem(f"at_v_loaded{e}") for e in range(2)]
        max_loaded = [sem(f"at_max_loaded{e}") for e in range(2)]
        unit_done, unit_read = sem("at_unit_done"), sem("at_unit_read")
        score_done, exp_done = sem("at_score_done"), sem("at_exp_done")
        pv_done, pv_read = sem("at_pv_done"), sem("at_pv_read")
        added = sem("at_added")
        added_last = sem("at_added_last")
        den_done, recip_done, o_done = sem("at_den_done"), sem("at_recip_done"), sem("at_o_done")
        o_stored = [sem(f"at_o_stored{h}") for h in range(QH)]

        def whole(G):
            return isinstance(G, int)

        ROUND = 2 * STACKS

        def number(r, d):
            return ROUND * r + d

        def over_groups(engine, group):
            group(0, 0)
            group(0, 1)
            with engine.Fori(0, (G_ALL - 4) // ROUND) as r:
                for d in range(2, 2 + ROUND):
                    group(r, d)
            group(0, G_ALL - 2)
            group(0, G_ALL - 1)

        with nc.Block() as block:
            @block.sync
            def _(sp):
                def load_stacks(r, d):
                    G, w = number(r, d), d % STACKS
                    b, g = G // 4, G % 4
                    if not (whole(G) and G < STACKS):
                        sp.wait_ge(score_done, HPG * STEPS * (G - STACKS + 1))
                    stacks[w].load(sp, scr, b, g)

                def load_v(r, d):
                    G, e = number(r, d), d % 2
                    b, g = G // 4, G % 4
                    if not (whole(G) and G < 2):
                        sp.wait_ge(pv_done, STEPS * (G - 1))
                    sp.dma_start(v_sb[e][:, :, :], scr["v"][ds(b * S, S), ds(g * P, P)]
                                 .rearrange("(k p) c -> p k c", p=P)).then_inc(v_loaded[e], 16)

                def store(r, d, h):
                    G = number(r, d)
                    b, g = G // 4, G % 4
                    sp.wait_ge(o_done, QH * G + h + 1)
                    sp.dma_start(scr["o"][ds(g * P, P), ds(b * S + h * 512, 512)], o_out[h][:, :]).then_inc(o_stored[h], 16)

                def load_max(r, d):
                    G, e, w = number(r, d), d % 2, d % STACKS
                    sp.wait_ge(unit_read, (UNITS + 1) * (G + 1))
                    sp.dma_start(q_st[w][ROWS:ROWS + 1, :, :].bitcast(F32).rearrange("o j (t n) -> o (j t) n", n=P),
                                 neg_max[e][:, :].bitcast(F32)).then_inc(max_loaded[e], 16)

                def group(r, d):
                    if not (whole(r) and d + 1 >= G_ALL):
                        load_v(r, d + 1)
                    if not (whole(r) and d + 2 >= G_ALL):
                        load_stacks(r, d + 2)
                    if not (whole(r) and d == 0):
                        store(r, d - 1, 1)
                    if not (whole(r) and d + 1 >= G_ALL):
                        load_max(r, d + 1)
                    store(r, d, 0)

                load_v(0, 0)
                load_stacks(0, 1)
                load_max(0, 0)
                over_groups(sp, group)
                store(0, G_ALL - 1, 1)
                for h in range(QH):
                    sp.wait_ge(o_stored[h], 16 * G_ALL)

            @block.gpsimd
            def _(pool):
                make_identity(nc, pool, ident, ident_ready)
                pool.memset(ones[:, :], 1.0).then_inc(const_ready, 1)
                for w in range(STACKS):
                    pool.wait_ge(const_ready, w + 1)
                    pool.memset(k_st[w][ROWS:ROWS + 1, :, :].bitcast(F32), 1.0).then_inc(const_ready, 1)

                def group(G, first):
                    for h in range(QH):
                        for k in range(1, QT):
                            T = QT * h + k
                            pool.wait_ge(exp_done, HPG * (STEPS * G + T + 1))
                            if k == 1 and not first:
                                pool.wait_ge(den_done, QH * (G - 1) + h + 1)
                            if k > 1 or h > 0 or not first:
                                pool.wait_ge(added, (QT - 1) * (QH * G + h) + k - 1)
                            before = probs[(T - 1) % RING] if k == 1 else psum_k[h]
                            pool.tensor_tensor(psum_k[h][:, 0:HP, :], probs[T % RING][:, 0:HP, :], before[:, 0:HP, :],
                                               ALU.add).then_inc(added, 1)

                group(0, True)
                with pool.Fori(1, G_ALL) as G:
                    group(G, False)

            @block.scalar
            def _(act):
                def exps(G, T, first):
                    for j in range(HPG):
                        n = HPG * (STEPS * G + T) + j
                        if j == 0:
                            if T >= RING:
                                k = T - RING
                                act.wait_ge(pv_done, STEPS * G + k + 1)
                                for add in (added, added_last):
                                    act.wait_ge(add, (QT - 1) * (QH * G + k // QT) + max(k % QT, 1))
                            elif not first:
                                k = STEPS + T - RING
                                act.wait_ge(pv_done, STEPS * (G - 1) + k + 1)
                                for add in (added, added_last):
                                    act.wait_ge(add, (QT - 1) * (QH * (G - 1) + 1) + max(k % QT, 1))
                        act.wait_ge(score_done, n + 1)
                        act.activation(probs[T % RING][:, j, :], score_ps[j % 2][:, :], ACT.Exp,
                                       scale=SCALE).then_inc(exp_done, 1)

                def read_pv(G, h, first=False):
                    act.wait_ge(pv_done, STEPS * G + QT * (h + 1))
                    if not first:
                        act.wait_ge(o_done, QH * (G - 1) + h + 1)
                    act.activation(o_raw[h][:, :], pv_ps[:, :], ACT.Copy).then_inc(pv_read, 1)

                def group(G, first):
                    for T in range(STEPS):
                        exps(G, T, first)
                        if T == 0 and not first:
                            read_pv(G - 1, 1, whole(G) and G == 1)
                        if T == QT:
                            read_pv(G, 0, first)

                group(0, True)
                group(1, False)
                with act.Fori(2, G_ALL) as G:
                    group(G, False)
                read_pv(G_ALL - 1, 1)

            @block.vector
            def _(dve):
                for e in range(2):
                    dve.memset(maxima[e][:, :], 0.0).then_inc(maxima_zero, 1)
                dve.wait_ge(maxima_zero, 2)

                def unit(G, e, u):
                    dve.wait_ge(unit_done, (UNITS + 1) * G + u + 1)
                    dve.tensor_reduce(maxima[e][:, u:u + 1], unit_ps[(e + u) % 2][:, :, :].rearrange("p a b -> p (a b)"),
                                      AX_X, ALU.max).then_inc(unit_read, 1)

                def read_turn(G, e, use):
                    dve.wait_ge(unit_done, (UNITS + 1) * (G + 1))
                    dve.wait_ge(max_loaded[e], 16 * use)
                    dve.tensor_scalar(neg_max[e][:, :], unit_ps[(e + UNITS) % 2][0:UNITS, 0, 0:P], -1.0, None,
                                      ALU.mult).then_inc(unit_read, 1)

                def invert(G, h, stage):
                    if stage == 0:
                        dve.wait_ge(den_done, QH * G + h + 1)
                        dve.transpose(den_t[:, :], den_ps[:, :]).then_inc(recip_done, 1)
                    elif stage == 1:
                        dve.wait_ge(recip_done, 3 * (QH * G + h) + 1)
                        dve.reciprocal(recip_t[:, :], den_t[:, :].rearrange("p (b c) -> p b c", c=32)[:, :, 0]).then_inc(recip_done, 1)
                    else:
                        dve.wait_ge(recip_done, 3 * (QH * G + h) + 2)
                        dve.transpose(recip[:, :], recip_t[:, :].unsqueeze(2).to_broadcast([P, 512 // 32, 32])).then_inc(recip_done, 1)

                def normalise(G, h):
                    dve.wait_ge(recip_done, 3 * (QH * G + h) + 3)
                    dve.wait_ge(pv_read, QH * G + h + 1)
                    dve.wait_ge(o_stored[h], 16 * G)
                    dve.tensor_tensor(o_out[h][:, :], o_raw[h][:, :], recip[:, :], ALU.mult).then_inc(o_done, 1)

                def add_keys(G, T, first):
                    h, k = T // QT, T % QT
                    if k == 0:
                        return
                    dve.wait_ge(exp_done, HPG * (STEPS * G + T + 1))
                    if k == 1 and not first:
                        dve.wait_ge(den_done, QH * (G - 1) + h + 1)
                    if k > 1 or h > 0 or not first:
                        dve.wait_ge(added_last, (QT - 1) * (QH * G + h) + k - 1)
                    before = probs[(T - 1) % RING] if k == 1 else psum_k[h]
                    dve.tensor_tensor(psum_k[h][:, HP, :], probs[T % RING][:, HP, :], before[:, HP, :],
                                      ALU.add).then_inc(added_last, 1)

                def results(G, T, first):
                    for Gh, h, T0 in ((G - 1, 1, 3), (G, 0, QT + 3)):
                        if T in (T0, T0 + 1) and not (first and h == 1):
                            if T == T0:
                                invert(Gh, h, 0)
                                yield
                                invert(Gh, h, 1)
                            else:
                                invert(Gh, h, 2)
                                yield
                                normalise(Gh, h)

                def group(G, e, i, first=False, left=2):
                    for T in range(STEPS):
                        if T == TURN_STEP and left:
                            read_turn(G + 1, 1 - e, i + e)
                        stages = results(G, T, first)
                        for n, (ahead, u) in enumerate(UNITS_AT[T]):
                            if ahead <= left:
                                unit(G + ahead, (e + ahead) % 2, u)
                            if n == 0:
                                add_keys(G, T, first)
                            next(stages, None)
                        for _ in stages:
                            pass

                for u in range(UNITS):
                    unit(0, 0, u)
                read_turn(0, 0, 0)
                for u in range(LEAD):
                    unit(1, 1, u)
                group(0, 0, 0, first=True)
                group(1, 1, 0)
                with dve.Fori(1, PAIRS - 1) as i:
                    for e in range(2):
                        group(2 * i + e, e, i)
                group(G_ALL - 2, 0, PAIRS - 1, left=1)
                group(G_ALL - 1, 1, PAIRS - 1, left=0)
                for stage in range(3):
                    invert(G_ALL - 1, 1, stage)
                normalise(G_ALL - 1, 1)

            @block.tensor
            def _(pe):
                def unit(r, d, u):
                    G, e, w = number(r, d), d % 2, d % STACKS
                    n = (UNITS + 1) * G + u
                    j, qt = u // QT, u % QT
                    if qt == 0:
                        pe.wait_ge(qk_loaded[w][j], 96 * (2 * r + d // 3 + 1))
                    if not (whole(n) and n < 2):
                        pe.wait_ge(unit_read, n - 1)
                    out = unit_ps[(e + u) % 2]
                    for h in range(2):
                        last = pe.matmul(out[:, h, :], q_st[w][0:ROWS, j, qt * P:(qt + 1) * P],
                                         k_st[w][0:ROWS, j, h * 512:(h + 1) * 512], start=True, stop=True)
                    last.then_inc(unit_done, 1)

                def turn(r, d):
                    G, e = number(r, d), d % 2
                    pe.wait_ge(unit_read, (UNITS + 1) * G + UNITS)
                    pe.transpose(unit_ps[(e + UNITS) % 2][:, 0, 0:P], maxima[e][:, :], ident[:, :]).then_inc(unit_done, 1)

                def score(r, d, T, j):
                    G, e, w = number(r, d), d % 2, d % STACKS
                    h, k = T // QT, T % QT
                    n = HPG * (STEPS * G + T) + j
                    if T == 0 and j == 0:
                        pe.wait_ge(max_loaded[e], 16 * (3 * r + d // 2 + 1))
                    if not (whole(n) and n < 2):
                        pe.wait_ge(exp_done, n - 1)
                    pe.matmul(score_ps[j % 2][:, :], k_st[w][0:ROWS + 1, j, k * P:(k + 1) * P],
                              q_st[w][0:ROWS + 1, j, h * 512:(h + 1) * 512], start=True, stop=True).then_inc(score_done, 1)

                def times_v(G, e, T):
                    h, k = T // QT, T % QT
                    if k == 0 and not (whole(G) and G == 0 and h == 0):
                        pe.wait_ge(pv_read, QH * G + h)
                    pe.wait_ge(exp_done, HPG * (STEPS * G + T + 1))
                    for j in range(HPG):
                        last = pe.matmul(pv_ps[j * HD:(j + 1) * HD, :], v_sb[e][:, k, j * HD:(j + 1) * HD],
                                         probs[T % RING][:, j, :], start=(k == 0), stop=(k == QT - 1),
                                         tile_position=(0, j * HD))
                    last.then_inc(pv_done, 1)

                def denominators(G, h):
                    pe.wait_ge(added, (QT - 1) * (QH * G + h + 1))
                    pe.wait_ge(added_last, (QT - 1) * (QH * G + h + 1))
                    if not (whole(G) and G == 0 and h == 0):
                        pe.wait_ge(recip_done, 3 * (QH * G + h - 1) + 1)
                    for j in range(HPG):
                        last = pe.matmul(den_ps[j * HD:(j + 1) * HD, :], ones[:, :], psum_k[h][:, j, :],
                                         start=True, stop=True, tile_position=(0, j * HD))
                    last.then_inc(den_done, 1)

                def group(r, d):
                    G, e = number(r, d), d % 2
                    left = G_ALL - 1 - d if whole(r) else 2
                    for T in range(STEPS):
                        if T == 0:
                            pe.wait_ge(v_loaded[e], 16 * (3 * r + d // 2 + 1))
                        units = [(r, d + ahead, u) for ahead, u in UNITS_AT[T] if ahead <= left]
                        nxt = (r, d, T + 1) if T + 1 < STEPS else (r, d + 1, 0)
                        go = T + 1 < STEPS or left
                        for j in range(HPG):
                            if go:
                                score(*nxt, j)
                            if j == 1:
                                times_v(G, e, T)
                                if T == TURN_STEP and left:
                                    turn(r, d + 1)
                            if units and (j % 2 == (1 if T == TURN_STEP else 0)):
                                unit(*units.pop(0))
                        if T == 2 and not (whole(r) and d == 0):
                            denominators(G - 1, 1)
                        if T == QT + 2:
                            denominators(G, 0)

                for u in range(UNITS):
                    unit(0, 0, u)
                pe.wait_ge(ident_ready, 2)
                turn(0, 0)
                pe.wait_ge(const_ready, 1 + STACKS)
                for j in range(2):
                    unit(0, 1, j)
                for j in range(HPG):
                    score(0, 0, 0, j)
                for u in range(2, LEAD):
                    unit(0, 1, u)
                over_groups(pe, group)
                denominators(G_ALL - 1, 1)


FEWEST = 3


def route(nc, z, a, scr, weights, used):
    KT, CH, TPC, NCH, D, E, CAP, TOP = z.KT, z.CH, z.TPC, z.NCH, z.D, z.E, z.CAP, z.TOP
    SLOTS = E * CAP
    TOK = z.TOK
    FAR = 100000.0
    PICKS = TPC * TOP
    with ExitStack() as ctx:
        def sb(name, shape, dt=F32):
            return ctx.enter_context(nc.sbuf_tensor("rt_" + name, shape, dt))

        def sem(name):
            return ctx.enter_context(nc.semaphore("rt_" + name))

        ident = sb("ident", [P, P])
        eps = sb("eps", [P, 1])
        wo_raw = sb("wo_raw", [P, KT, D])
        woT = [sb("woT_hi", [P, KT, D], F32R), sb("woT_lo", [P, KT, D], F32R)]
        rw = sb("rw", [E, D])
        rwT = sb("rwT", [P, KT, E])
        rb = sb("rb", [P, E])
        bo = sb("bo", [P, D])
        gate = sb("gate", [P, 2])
        tanh_g = sb("tanh_g", [P, 2])
        tanh_bo = sb("tanh_bo", [P, D])
        iota_i = sb("iota_i", [P, E], I32)
        iota = sb("iota", [P, E])
        user = sb("user", [P, TPC, TOP, 2], I32)
        spare = sb("spare", [E, CAP, 2], I32)
        zero_row = sb("zero_row", [P, D])
        before_f = sb("before_f", [P, P])
        before = sb("before", [P, P], BF16)
        ones = sb("ones", [P, P], BF16)
        oT_raw = sb("oT_raw", [P, 2, KT, CH])
        oT = [sb("oT_hi", [P, KT, CH], F32R), sb("oT_lo", [P, KT, CH], F32R)]
        x_raw = sb("x_raw", [P, TPC, D])
        xb = sb("xb", [P, TPC, D])
        x1 = sb("x1", [P, TPC, D])
        stats = sb("stats", [P, TPC, 6])
        mv = sb("mv", [P, TPC, 2])
        std = sb("std", [P, TPC])
        rstd = sb("rstd", [P, TPC])
        xn = sb("xn", [P, TPC, D])
        xnT = sb("xnT", [P, KT, CH])
        logT = sb("logT", [E, CH])
        logits = sb("logits", [P, TPC, E])
        best = sb("best", [P, TPC, 8])
        best_at = sb("best_at", [P, TPC, 8], U32)
        expert = sb("expert", [P, TPC, TOP])
        picked = sb("picked", [P, TPC, TOP, E])
        chosen = sb("chosen", [P, TPC, E], BF16)
        chunk_sum = sb("chunk_sum", [P, E])
        over = [sb(f"over{i}", [P, E]) for i in range(2)]
        run = sb("run", [P, E])
        run_b = sb("run_b", [P, E], BF16)
        at = sb("at", [P, TPC, TOP, E])
        place = sb("place", [P, TPC, TOP])
        slot = sb("slot", [P, TPC, TOP])
        far = sb("far", [P, TPC, TOP])
        target = sb("target", [P, TPC, TOP], I32)
        value = sb("value", [P, NCH, TPC, TOP])
        kept = sb("kept", [P, NCH, TPC, TOP])
        w_tmp = [sb(f"w_tmp{i}", [P, NCH, TPC]) for i in range(5)]
        w_gk = sb("w_gk", [P, NCH, TPC, TOP])
        weight = sb("weight", [P, TOP, NCH, TPC])
        y_ps = ctx.enter_context(nc.psum_tensor("rt_y_ps", [P, TPC, 512], F32))
        turned = ctx.enter_context(nc.psum_tensor("rt_turned", [P, 2, 512], F32))
        logT_ps = ctx.enter_context(nc.psum_tensor("rt_logT_ps", [P, 512], F32))
        place_ps = ctx.enter_context(nc.psum_tensor("rt_place_ps", [P, 512], F32))
        back_v = place_ps[:, TPC * E:2 * TPC * E].rearrange("p (t e) -> p t e", e=E)
        place_v = place_ps[:, 0:TPC * E].rearrange("p (t e) -> p t e", e=E)

        dve_passed, pool_passed, pe_passed = sem("dve_passed"), sem("pool_passed"), sem("pe_passed")
        wo_loaded, small_loaded = sem("wo_loaded"), sem("small_loaded")
        o_loaded, x_loaded = [sem("o_loaded0"), sem("o_loaded1")], sem("x_loaded")
        pool_const, dve_const, tanh_ready = sem("pool_const"), sem("dve_const"), sem("tanh_ready")
        spares_stored = sem("spares_stored")
        wo_turned, wo_hi, wo_lo = sem("wo_turned"), sem("wo_hi"), sem("wo_lo")
        o_hi, o_lo = sem("o_hi"), sem("o_lo")
        y_done, x1_ready, stats_done = sem("y_done"), sem("x1_ready"), sem("stats_done")
        var_ready, std_ready, rstd_ready = sem("var_ready"), sem("std_ready"), sem("rstd_ready")
        xb_ready, xn_ready = sem("xb_ready"), sem("xn_ready")
        x1_stored, xn_stored = sem("x1_stored"), sem("xn_stored")
        xn_turned, xnT_ready, logits_done = sem("xn_turned"), sem("xnT_ready"), sem("logits_done")
        logT_ready, back_done = sem("logT_ready"), sem("back_done")
        used_ready, ident_ready = sem("used_ready"), sem("ident_ready")
        pick, chosen_ready = sem("pick"), sem("chosen_ready")
        place_done, placed = sem("place_done"), sem("placed")
        scattered = sem("scattered")
        user_next = sem("user_next")
        weigh, exp_ready, weight_stored = sem("weigh"), sem("exp_ready"), sem("weight_stored")

        WU = KT + 1
        PICK, PLACE = 12, 10

        with nc.Block() as block:
            @block.sync
            def _(sp):
                def load(dst, src, c, done):
                    sp.dma_start(dst[:, :, :], src[ds(c * CH, CH), :].rearrange("(t p) c -> p t c", p=P)).then_inc(done, 16)

                def load_o(c, i):
                    sp.dma_start(oT_raw[:, i, :, :], scr["o"][:, ds(c * CH, CH)].rearrange("(k p) n -> p k n", p=P)).then_inc(o_loaded[i], 16)

                def store(dst, src, c, done):
                    sp.dma_start(dst[ds(c * CH, CH), :].rearrange("(t p) c -> p t c", p=P), src[:, :, :]).then_inc(done, 16)

                sp.dma_start(wo_raw[:, :, :], a["Wo"].rearrange("(m p) c -> p m c", p=P)).then_inc(wo_loaded, 16)
                for dst, src, n in ((rb, "router_b", E), (bo, "bo", D)):
                    sp.dma_start(dst[:, :], a[src].rearrange("(o c) -> o c", o=1).to_broadcast([P, n])).then_inc(small_loaded, 16)
                for i, src in enumerate(("g_xattn", "g_ffn")):
                    sp.dma_start(gate[:, i:i + 1], a[src].rearrange("(o c) -> o c", o=1).to_broadcast([P, 1])).then_inc(small_loaded, 16)
                sp.dma_start(rw[:, :], a["router_w"]).then_inc(small_loaded, 16)
                load_o(0, 0)
                load(x_raw, a["x"], 0, x_loaded)
                load_o(1, 1)
                sp.wait_ge(pool_const, 9)
                sp.dma_start(scr["user_of"].rearrange("(e s) o -> e s o", e=E), spare[:, :, :]).then_inc(spares_stored, 16)
                for i in range(CAP // P):
                    for dst in ("xn", "out"):
                        sp.dma_start(scr[dst][TOK + i * P:TOK + (i + 1) * P, :], zero_row[:, :]).then_inc(spares_stored, 16)
                sp.dma_start(scr["weight"][TOK:TOK + CAP, :].rearrange("(p n) o -> p (n o)", p=P),
                             zero_row[:, 0:CAP // P]).then_inc(spares_stored, 16)

                def step(c, i, left):
                    if left >= 2:
                        sp.wait_ge(o_lo, TPC * (c + 1))
                        load_o(c + 2, i)
                    if left:
                        sp.wait_ge(xb_ready, TPC * (c + 1))
                        load(x_raw, a["x"], c + 1, x_loaded)
                    sp.wait_ge(x1_ready, TPC * (c + 1))
                    store(scr["out"], x1, c, x1_stored)
                    sp.wait_ge(xn_ready, TPC * (c + 1))
                    store(scr["xn"], xn, c, xn_stored)

                step(0, 0, 2)
                step(1, 1, 2)
                weights.load(sp, 0, 0)
                weights.load(sp, 0, 1)
                with sp.Fori(1, NCH // 2 - 1) as j:
                    for i in range(2):
                        step(2 * j + i, i, 2)
                weights.load(sp, 0, 2)
                step(NCH - 2, 0, 1)
                weights.load(sp, 0, 3)
                step(NCH - 1, 1, 0)
                sp.wait_ge(weigh, 10)
                with nc.allow_non_contiguous_dma(reason="4096 weights each"):
                    for k in range(TOP):
                        sp.dma_start(scr["weight"][k * (TOK + CAP):k * (TOK + CAP) + TOK, :].rearrange("(n p) o -> p (n o)", p=P),
                                     weight[:, k, :, :].rearrange("p c t -> p (c t)")).then_inc(weight_stored, 16)
                sp.wait_ge(x1_stored, 16 * NCH)
                sp.wait_ge(xn_stored, 16 * NCH)
                sp.wait_ge(weight_stored, 16 * TOP)

            @block.gpsimd
            def _(pool):
                make_identity(nc, pool, ident, ident_ready)
                pool.memset(eps[:, :], EPS)
                pool.memset(zero_row[:, :], 0.0)
                pool.memset(ones[:, :], 1.0)
                pool.memset(before_f[:, :], 1.0)
                pool.iota(iota_i[:, :], [[1, E]], base=0, channel_multiplier=0)
                for i in range(2):
                    pool.iota(spare[:, :, i], [[1, CAP]], base=TOK, channel_multiplier=0)
                    for k in range(TOP):
                        last = pool.iota(user[:, :, k, i], [[P, TPC]], base=k * i * (TOK + CAP), channel_multiplier=1)
                last.then_inc(pool_const, 7)
                pool.wait_ge(pool_const, 7)
                pool.affine_select(out=before_f[:, :], in_=before_f[:, :], compare_op=ALU.is_gt, fill=0.0, base=0,
                                   pattern=[[1, P]], channel_multiplier=-1).then_inc(pool_const, 2)

                def add_bias(c, first=False):
                    pool.wait_ge(x_loaded, 16 * (c + 1))
                    for t in range(TPC):
                        if not first:
                            pool.wait_ge(x1_ready, TPC * (c - 1) + t + 1)
                            pool.wait_ge(xb_ready, TPC * c + t)
                        elif t:
                            pool.wait_ge(xb_ready, t)
                        pool.tensor_tensor(xb[:, t, :], x_raw[:, t, :], tanh_bo[:, :], ALU.add).then_inc(xb_ready, 1)

                def scatter(c):
                    pool.wait_ge(placed, PLACE * (c + 2))
                    settle(pool, pool_passed)
                    for i in range(PICKS):
                        t, k = i // TOP, i % TOP
                        pool.indirect_dma_start(scr["user_of"], bass.IndirectOffsetOnAxis(target[:, t, k:k + 1], 0),
                                                user[:, t, k, :], None, bounds_check=SLOTS - 1,
                                                oob_is_err=False).then_inc(scattered, 16)

                pool.wait_ge(dve_const, 2)
                add_bias(0, True)
                add_bias(1)
                pool.wait_ge(spares_stored, 16 * (2 + 2 * (CAP // P)))
                with pool.Fori(0, NCH - 2) as c:
                    add_bias(c + 2)
                    scatter(c)
                scatter(NCH - 2)
                scatter(NCH - 1)
                pool.wait_ge(scattered, 16 * PICKS * NCH)

            @block.scalar
            def _(act):
                act.wait_ge(small_loaded, 80)
                act.activation(tanh_g[:, :], gate[:, :], ACT.Tanh).then_inc(tanh_ready, 1)
                for u in range(KT):
                    act.wait_ge(wo_turned, u + 1)
                    act.activation(woT[0][:, u, :], turned[:, u % 2, :], ACT.Copy).then_inc(wo_hi, 1)
                act.wait_ge(pool_const, 9)

                def split_o(c, t, i):
                    act.wait_ge(o_loaded[i], 16 * ((c - i) // 2 + 1) if isinstance(c, int) else 8 * (c - i) + 16)
                    if not isinstance(c, int) or c > 0:
                        act.wait_ge(y_done, TPC * (c - 1) + t + 1)
                    sl = slice(t * P, (t + 1) * P)
                    act.activation(oT[0][:, :, sl], oT_raw[:, i, :, sl], ACT.Copy).then_inc(o_hi, 1)

                def std_of(c):
                    act.wait_ge(var_ready, c + 1)
                    act.activation(std[:, :], mv[:, :, 1], ACT.Sqrt, bias=eps[:, 0:1]).then_inc(std_ready, 1)

                def copy_turned(c, t):
                    if t == 0 and (not isinstance(c, int) or c > 0):
                        act.wait_ge(logits_done, c)
                    act.wait_ge(xn_turned, TPC * c + t + 1)
                    act.activation(xnT[:, :, t * P:(t + 1) * P],
                                   turned[:, t % 2, :].rearrange("p (k n) -> p k n", n=P), ACT.Copy).then_inc(xnT_ready, 1)

                def copy_logits(c):
                    act.wait_ge(logits_done, c + 1)
                    if not isinstance(c, int) or c > 0:
                        act.wait_ge(back_done, c)
                    act.activation(logT[:, :], logT_ps[0:E, :], ACT.Copy).then_inc(logT_ready, 1)

                def step(c, i, left=2):
                    if left >= 2:
                        split_o(c + 2, 0, i)
                        split_o(c + 2, 1, i)
                    copy_turned(c, 0)
                    copy_turned(c, 1)
                    if left >= 2:
                        split_o(c + 2, 2, i)
                    copy_turned(c, 2)
                    copy_turned(c, 3)
                    if left >= 2:
                        split_o(c + 2, 3, i)
                    if left >= 1:
                        std_of(c + 1)
                    copy_logits(c)

                for i in range(2):
                    for t in range(TPC):
                        split_o(i, t, i)
                std_of(0)
                step(0, 0)
                step(1, 1)
                with act.Fori(1, NCH // 2 - 1) as j:
                    for i in range(2):
                        step(2 * j + i, i)
                step(NCH - 2, 0, 1)
                step(NCH - 1, 1, 0)
                act.wait_ge(weigh, 1)
                act.activation(w_tmp[1][:, :, :], w_tmp[0][:, :, :], ACT.Exp).then_inc(exp_ready, 1)

            @block.vector
            def _(dve):
                dve.memset(run[:, :], 0.0)
                dve.memset(run_b[:, :], 0.0).then_inc(placed, PLACE)
                dve.sem_inc(user_next, 1)
                dve.wait_ge(tanh_ready, 1)
                dve.tensor_scalar(tanh_bo[:, :], bo[:, :], tanh_g[:, 0:1], None, ALU.mult).then_inc(dve_const, 2)
                for u in range(KT):
                    dve.wait_ge(wo_hi, u + 1)
                    dve.tensor_tensor(woT[1][:, u, :], turned[:, u % 2, :], woT[0][:, u, :].bitcast(F32),
                                      ALU.subtract).then_inc(wo_lo, 1)
                dve.wait_ge(wo_turned, WU)
                dve.tensor_copy(rwT[:, :, :], turned[:, KT % 2, 0:KT * E].rearrange("p (k e) -> p k e", e=E)).then_inc(wo_lo, 1)
                dve.wait_ge(pool_const, 9)
                dve.tensor_copy(iota[:, :], iota_i[:, :]).then_inc(dve_const, 1)
                dve.tensor_copy(before[:, :], before_f[:, :]).then_inc(dve_const, 1)
                dve.wait_ge(dve_const, 4)

                def split_o(c, t, i):
                    sl = slice(t * P, (t + 1) * P)
                    dve.wait_ge(o_hi, TPC * c + t + 1)
                    dve.tensor_tensor(oT[1][:, :, sl], oT_raw[:, i, :, sl], oT[0][:, :, sl].bitcast(F32),
                                      ALU.subtract).then_inc(o_lo, 1)

                def residual(c, t):
                    if t == 0 and (not isinstance(c, int) or c > 0):
                        dve.wait_ge(x1_stored, 16 * c)
                    if not isinstance(c, int) or c > 0:
                        dve.wait_ge(xn_ready, TPC * (c - 1) + t + 1)
                    dve.wait_ge(y_done, TPC * c + t + 1)
                    dve.wait_ge(xb_ready, TPC * c + t + 1)
                    dve.scalar_tensor_tensor(out=x1[:, t, :], in0=y_ps[:, t, :], scalar=tanh_g[:, 0:1], in1=xb[:, t, :],
                                             op0=ALU.mult, op1=ALU.add).then_inc(x1_ready, 1)

                def statistics(c, t):
                    dve.wait_ge(x1_ready, TPC * c + t + 1)
                    dve.bn_stats(stats[:, t, :], x1[:, t, :]).then_inc(stats_done, 1)
                    if t == TPC - 1:
                        dve.wait_ge(stats_done, TPC * (c + 1))
                        settle(dve, dve_passed)
                        for k in range(TPC):
                            last = dve.bn_aggr(mv[:, k, :], stats[:, k, :])
                        last.then_inc(var_ready, 1)

                def normalise(c):
                    dve.wait_ge(std_ready, c + 1)
                    dve.reciprocal(rstd[:, :], std[:, :]).then_inc(rstd_ready, 1)
                    dve.wait_ge(rstd_ready, c + 1)
                    if not isinstance(c, int) or c > 0:
                        dve.wait_ge(xn_stored, 16 * c)
                        dve.wait_ge(xn_turned, TPC * c)
                    for t in range(TPC):
                        dve.tensor_scalar(xn[:, t, :], x1[:, t, :], mv[:, t, 0:1], rstd[:, t:t + 1],
                                          ALU.subtract, ALU.mult).then_inc(xn_ready, 1)

                def choose(c):
                    n = PICK * c
                    dve.wait_ge(back_done, c + 1)
                    dve.tensor_tensor(logits[:, :, :], back_v, rb[:, :].unsqueeze(1).to_broadcast([P, TPC, E]),
                                      ALU.add).then_inc(pick, 1)
                    dve.wait_ge(pick, n + 1)
                    settle(dve, dve_passed)
                    for t in range(TPC):
                        dve.max(best[:, t, :], logits[:, t, :]).then_inc(pick, 1)
                    for t in range(TPC):
                        dve.wait_ge(pick, n + 2 + t)
                        settle(dve, dve_passed)
                        dve.max_index(best_at[:, t, :], best[:, t, :], logits[:, t, :]).then_inc(pick, 1)
                    dve.wait_ge(pick, n + 9)
                    dve.tensor_copy(value[:, ds(c, 1), :, :].rearrange("p o t k -> p (o t) k"), best[:, :, 0:TOP])
                    dve.tensor_copy(expert[:, :, :], best_at[:, :, 0:TOP]).then_inc(pick, 1)
                    dve.wait_ge(pick, n + 10)
                    dve.tensor_tensor(picked[:, :, :, :].rearrange("p t k e -> p (t k) e"),
                                      iota[:, :].unsqueeze(1).to_broadcast([P, PICKS, E]),
                                      expert[:, :, :].rearrange("p t k -> p (t k)").unsqueeze(2).to_broadcast([P, PICKS, E]),
                                      ALU.is_equal).then_inc(pick, 1)
                    dve.wait_ge(pick, n + 11)
                    dve.tensor_tensor(chosen[:, :, :], picked[:, :, 0, :], picked[:, :, 1, :], ALU.add).then_inc(pick, 1)

                def assign(c):
                    n = PLACE * (c + 1)
                    dve.wait_ge(place_done, c + 1)
                    dve.tensor_reduce(chunk_sum[:, :], chosen[:, :, :].rearrange("p t e -> p e t"), AX_X, ALU.add).then_inc(placed, 1)
                    for k in range(TOP):
                        dve.tensor_tensor(at[:, :, k, :], picked[:, :, k, :], place_v, ALU.mult).then_inc(placed, 1)
                    dve.wait_ge(placed, n + 1)
                    dve.tensor_tensor(run[:, :], run[:, :], chunk_sum[:, :], ALU.add).then_inc(placed, 1)
                    dve.wait_ge(placed, n + 3)
                    dve.tensor_reduce(place[:, :, :].rearrange("p t k -> p (t k)"),
                                      at[:, :, :, :].rearrange("p t k e -> p (t k) e"), AX_X, ALU.add).then_inc(placed, 1)
                    dve.wait_ge(placed, n + 4)
                    dve.tensor_copy(run_b[:, :], run[:, :]).then_inc(placed, 1)
                    dve.wait_ge(placed, n + 5)
                    dve.scalar_tensor_tensor(out=slot[:, :, :], in0=expert[:, :, :], scalar=float(CAP), in1=place[:, :, :],
                                             op0=ALU.mult, op1=ALU.add).then_inc(placed, 1)
                    dve.tensor_scalar(far[:, :, :], place[:, :, :], float(CAP), FAR, ALU.is_ge, ALU.mult).then_inc(placed, 1)
                    dve.tensor_scalar(kept[:, ds(c, 1), :, :].rearrange("p o t k -> p (o t) k"), place[:, :, :], float(CAP), None,
                                      ALU.is_lt).then_inc(placed, 1)
                    dve.wait_ge(placed, n + 8)
                    if not isinstance(c, int) or c > 0:
                        dve.wait_ge(scattered, 16 * PICKS * c)
                        dve.wait_ge(user_next, c)
                        dve.tensor_scalar(user[:, :, :, :], user[:, :, :, :], CH, None, ALU.add).then_inc(user_next, 1)
                        dve.wait_ge(user_next, c + 1)
                    dve.tensor_tensor(target[:, :, :], slot[:, :, :], far[:, :, :], ALU.add).then_inc(placed, 1)

                def step(c, i, left=2):
                    normalise(c)
                    for t in range(TPC):
                        if left >= 1:
                            residual(c + 1, t)
                        if left >= 2:
                            split_o(c + 2, t, i)
                        if t == 0 and not (isinstance(c, int) and c == 0):
                            choose(c - 1)
                        if t == 2 and not (isinstance(c, int) and c == 0):
                            assign(c - 1)
                        if t and left >= 1:
                            statistics(c + 1, t - 1)
                    if left >= 1:
                        statistics(c + 1, TPC - 1)

                for t in range(TPC):
                    split_o(0, t, 0)
                for t in range(TPC):
                    residual(0, t)
                    split_o(1, t, 1)
                for t in range(TPC):
                    statistics(0, t)
                step(0, 0)
                step(1, 1)
                with dve.Fori(1, NCH // 2 - 1) as j:
                    for i in range(2):
                        step(2 * j + i, i)
                step(NCH - 2, 0, 1)
                step(NCH - 1, 1, 0)
                choose(NCH - 1)
                assign(NCH - 1)

                assert CAP // P == FEWEST + 2
                dve.wait_ge(place_done, NCH + 1)
                for i in range(2):
                    dve.tensor_scalar(over[i][:, :], place_ps[:, 0:E], float((FEWEST + i) * P + 1), float(FEWEST * (1 - i)),
                                      ALU.is_ge, ALU.add).then_inc(used_ready, 1)
                dve.wait_ge(used_ready, 2)
                dve.tensor_tensor(used[:, :], over[0][:, :], over[1][:, :], ALU.add).then_inc(used_ready, 1)

                diff, ex, total, inv, den = w_tmp
                v0, v1 = value[:, :, :, 0], value[:, :, :, 1]
                dve.wait_ge(placed, PLACE * (NCH + 1))
                dve.tensor_tensor(diff[:, :, :], v1, v0, ALU.subtract).then_inc(weigh, 1)
                dve.wait_ge(exp_ready, 1)
                dve.tensor_scalar(total[:, :, :], ex[:, :, :], 1.0, None, ALU.add).then_inc(weigh, 1)
                dve.wait_ge(weigh, 2)
                dve.reciprocal(inv[:, :, :], total[:, :, :]).then_inc(weigh, 1)
                dve.wait_ge(weigh, 3)
                dve.tensor_tensor(w_gk[:, :, :, 0], inv[:, :, :], kept[:, :, :, 0], ALU.mult).then_inc(weigh, 1)
                dve.tensor_tensor(total[:, :, :], ex[:, :, :], inv[:, :, :], ALU.mult).then_inc(weigh, 1)
                dve.wait_ge(weigh, 5)
                dve.tensor_tensor(w_gk[:, :, :, 1], total[:, :, :], kept[:, :, :, 1], ALU.mult).then_inc(weigh, 1)
                dve.wait_ge(weigh, 6)
                dve.scalar_tensor_tensor(out=den[:, :, :], in0=w_gk[:, :, :, 0], scalar=1e-9, in1=w_gk[:, :, :, 1],
                                         op0=ALU.add, op1=ALU.add).then_inc(weigh, 1)
                dve.wait_ge(weigh, 7)
                dve.reciprocal(inv[:, :, :], den[:, :, :]).then_inc(weigh, 1)
                dve.wait_ge(weigh, 8)
                for k in range(TOP):
                    dve.scalar_tensor_tensor(out=weight[:, k, :, :], in0=w_gk[:, :, :, k], scalar=tanh_g[:, 1:2],
                                             in1=inv[:, :, :], op0=ALU.mult, op1=ALU.mult).then_inc(weigh, 1)

            @block.tensor
            def _(pe):
                pe.wait_ge(ident_ready, 2)
                pe.wait_ge(wo_loaded, 16)
                for u in range(KT):
                    if u >= 2:
                        pe.wait_ge(wo_lo, u - 1)
                    for m in range(KT):
                        last = pe.transpose(turned[:, u % 2, m * P:(m + 1) * P], wo_raw[:, m, u * P:(u + 1) * P], ident[:, :])
                    last.then_inc(wo_turned, 1)
                pe.wait_ge(wo_lo, KT - 1)
                pe.wait_ge(small_loaded, 80)
                for k in range(KT):
                    last = pe.transpose(turned[:, KT % 2, k * E:(k + 1) * E], rw[:, k * P:(k + 1) * P], ident[0:E, 0:E])
                last.then_inc(wo_turned, 1)
                pe.wait_ge(wo_lo, WU)

                def product(c, t):
                    pe.wait_ge(o_lo, TPC * c + t + 1)
                    if not isinstance(c, int) or c > 0:
                        pe.wait_ge(x1_ready, TPC * (c - 1) + t + 1)
                    for k in range(KT):
                        last = split_matmul(pe, y_ps[:, t, :], oT[0][:, k, t * P:(t + 1) * P], oT[1][:, k, t * P:(t + 1) * P],
                                            woT[0][:, k, :], woT[1][:, k, :], k == 0, k == KT - 1)
                    last.then_inc(y_done, 1)

                def turn(c, t):
                    pe.wait_ge(xn_ready, TPC * c + t + 1)
                    if t >= 2 or not isinstance(c, int) or c > 0:
                        pe.wait_ge(xnT_ready, TPC * c + t - 1)
                    for k in range(KT):
                        last = pe.transpose(turned[:, t % 2, k * P:(k + 1) * P], xn[:, t, k * P:(k + 1) * P], ident[:, :])
                    last.then_inc(xn_turned, 1)

                def score(c):
                    if not isinstance(c, int) or c > 0:
                        pe.wait_ge(logT_ready, c)
                    pe.wait_ge(xnT_ready, TPC * (c + 1))
                    for k in range(KT):
                        last = pe.matmul(logT_ps[0:E, :], rwT[:, k, :], xnT[:, k, :], start=(k == 0), stop=(k == KT - 1))
                    last.then_inc(logits_done, 1)

                def turn_back(c):
                    pe.wait_ge(logT_ready, c + 1)
                    if not isinstance(c, int) or c > 0:
                        pe.wait_ge(pick, PICK * (c - 1) + 1)
                        pe.wait_ge(placed, PLACE * (c + 1))
                        settle(pe, pe_passed)
                    for t in range(TPC):
                        last = pe.transpose(place_ps[:, (TPC + t) * E:(TPC + t + 1) * E], logT[:, t * P:(t + 1) * P], ident[0:E, 0:E])
                    last.then_inc(back_done, 1)

                def places(c):
                    pe.wait_ge(pick, PICK * (c + 1))
                    pe.wait_ge(placed, PLACE * (c + 1))
                    for t in range(TPC):
                        out = place_ps[:, t * E:(t + 1) * E]
                        pe.matmul(out, before[:, :], chosen[:, t, :], start=True, stop=False)
                        for s in range(t):
                            pe.matmul(out, ones[:, :], chosen[:, s, :], start=False, stop=False)
                        last = pe.matmul(out, ones[:, :], run_b[:, :], start=False, stop=True)
                    last.then_inc(place_done, 1)

                def step(c, more=True):
                    early = isinstance(c, int) and c == 0
                    if more:
                        product(c + 1, 0)
                    if not early:
                        turn_back(c - 1)
                    if more:
                        product(c + 1, 1)
                    turn(c, 0)
                    turn(c, 1)
                    if more:
                        product(c + 1, 2)
                    turn(c, 2)
                    turn(c, 3)
                    if not early:
                        places(c - 1)
                    if more:
                        product(c + 1, 3)
                    score(c)

                for t in range(TPC):
                    product(0, t)
                step(0)
                step(1)
                with pe.Fori(2, NCH - 1) as c:
                    step(c)
                step(NCH - 1, False)
                turn_back(NCH - 1)
                places(NCH - 1)
                pe.wait_ge(placed, PLACE * (NCH + 1))
                pe.matmul(place_ps[:, 0:E], ones[:, :], run_b[:, :], start=True, stop=True).then_inc(place_done, 1)


class ExpertWeights:

    WC = 4

    def __init__(self, nc, ctx, z, a):
        self.LOADS = z.F // P // self.WC
        self.KT, self.FT = z.KT, z.F // P
        n = range(self.LOADS)
        self.w1 = [ctx.enter_context(nc.sbuf_tensor(f"w1_raw{c}", [P, z.KT, self.WC * P], F32)) for c in n]
        self.w2 = [ctx.enter_context(nc.sbuf_tensor(f"w2_raw{c}", [P, self.WC, z.D], F32)) for c in n]
        self.w1_loaded = [ctx.enter_context(nc.semaphore(f"w1_loaded{c}")) for c in n]
        self.w2_loaded = [ctx.enter_context(nc.semaphore(f"w2_loaded{c}")) for c in n]
        self.w1_dram = a["w1"].rearrange("e (k p) f -> p (e k) f", p=P)
        self.w2_dram = a["w2"].rearrange("e (t p) d -> p (e t) d", p=P)

    def load(self, sp, e, c):
        WC = self.WC
        sp.dma_start(self.w1[c][:, :, :], self.w1_dram[:, ds(self.KT * e, self.KT), c * WC * P:(c + 1) * WC * P]
                     ).then_inc(self.w1_loaded[c], 16)
        sp.dma_start(self.w2[c][:, :, :], self.w2_dram[:, ds(self.FT * e + WC * c, WC), :]).then_inc(self.w2_loaded[c], 16)


def run_experts(nc, z, a, scr, weights, used):
    KT, D, E, CAP, F = z.KT, z.D, z.E, z.CAP, z.F
    FT = F // P
    ST = CAP // P
    PARTS = [slice(0, FEWEST * P), slice(FEWEST * P, CAP)]
    ONE_BANK = [slice(0, CAP - P)]
    WC, NC = weights.WC, weights.LOADS
    RING = 4
    AHEAD = 3
    X_STEPS = tuple(range(9, 9 + ST))
    PAIRS = E // 2
    with ExitStack() as ctx:
        def sb(name, shape, dt=F32):
            return ctx.enter_context(nc.sbuf_tensor("ex_" + name, shape, dt))

        def sem(name):
            return ctx.enter_context(nc.semaphore("ex_" + name))

        ident = sb("ident", [P, P])
        b1_raw = sb("b1_raw", [P, 2, P])
        b1T = sb("b1T", [P, E * FT])
        user = [sb(f"user{i}", [P, ST, 2], I32) for i in range(2)]
        rows = sb("rows", [P, ST, D])
        slot_weight = [sb(f"slot_weight{i}", [P, ST]) for i in range(2)]
        xT_hi = [sb(f"xT_hi{i}", [P, KT, CAP], F32R) for i in range(2)]
        xT_lo = [sb(f"xT_lo{i}", [P, KT, CAP], F32R) for i in range(2)]
        w1_raw, w2_raw = weights.w1, weights.w2
        w1_hi = [sb(f"w1_hi{i}", [P, KT, P], F32R) for i in range(RING)]
        w1_lo = [sb(f"w1_lo{i}", [P, KT, P], F32R) for i in range(RING)]
        w2_hi = [sb(f"w2_hi{i}", [P, D], F32R) for i in range(RING)]
        w2_lo = [sb(f"w2_lo{i}", [P, D], F32R) for i in range(RING)]
        hid = [sb(f"hid{i}", [P, CAP]) for i in range(2)]
        hid_hi = [sb(f"hid_hi{i}", [P, CAP], F32R) for i in range(2)]
        hid_lo = [sb(f"hid_lo{i}", [P, CAP], F32R) for i in range(2)]
        b2 = [sb(f"b2_{i}", [P, D]) for i in range(2)]
        total = sb("total", [P, ST, D])
        result = sb("result", [P, ST, D])
        acc = ctx.enter_context(nc.psum_tensor("ex_acc", [P, ST, 512], F32))
        first_ps = [ctx.enter_context(nc.psum_tensor(f"ex_first{i}", [P, 512], F32)) for i in range(2)]
        turned = ctx.enter_context(nc.psum_tensor("ex_turned", [P, 512], F32))

        act_passed, pool_passed = sem("act_passed"), sem("pool_passed")
        ident_ready, b1_loaded, b1_turned, b1_ready = sem("ident_ready"), sem("b1_loaded"), sem("b1_turned"), sem("b1_ready")
        w1_loaded, w2_loaded = weights.w1_loaded, weights.w2_loaded
        w_hi, w_lo = sem("w_hi"), sem("w_lo")
        w_free = sem("w_free")
        user_loaded = [sem(f"user_loaded{i}") for i in range(2)]
        gathered = sem("gathered")
        weight_gathered = [sem(f"weight_gathered{i}") for i in range(2)]
        x_turned, x_hi, x_lo = sem("x_turned"), sem("x_hi"), sem("x_lo")
        first_done = sem("first_done")
        first_free = sem("first_free")
        hid_free = sem("hid_free")
        hid_hi_done, hid_ready = sem("hid_hi_done"), sem("hid_ready")
        acc_done = sem("acc_done")
        acc_free = sem("acc_free")
        b2_loaded = [sem(f"b2_loaded{i}") for i in range(2)]
        weighted = sem("weighted")
        added = sem("added")

        def bank(e, s):
            return (turned, first_ps[0], first_ps[1])[s % 3 if isinstance(e, int) and e == 0 else 0]

        with nc.Block() as block:
            @block.sync
            def _(sp):
                sp.dma_start(b1_raw[:, :, :], a["b1"].rearrange("(h e) (t p) -> (e t) h p", h=2, p=P)).then_inc(b1_loaded, 16)
                with sp.Fori(1, E) as e:
                    for c in range(NC):
                        sp.wait_ge(w_lo, FT * (e - 1) + WC * (c + 1))
                        weights.load(sp, e, c)

            @block.gpsimd
            def _(pool):
                make_identity(nc, pool, ident, ident_ready)

                def load_b2(e, i):
                    pool.dma_start(b2[i][:, :], a["b2"][ds(e, 1), :].to_broadcast([P, D])).then_inc(b2_loaded[i], 16)

                def gather(e, i, use):
                    pool.dma_start(user[i][:, :, :], scr["user_of"][ds(CAP * e, CAP), :].rearrange("(s p) o -> p s o", p=P)
                                   ).then_inc(user_loaded[i], 16)
                    pool.wait_ge(user_loaded[i], 16 * (use + 1))
                    settle(pool, pool_passed)
                    for s in range(ST):
                        pool.indirect_dma_start(rows[:, s, :], None, scr["xn"],
                                                bass.IndirectOffsetOnAxis(user[i][:, s, 0:1], 0),
                                                bounds_check=z.TOK + CAP - 1, oob_is_err=False).then_inc(gathered, 16)
                    for s in range(ST):
                        pool.indirect_dma_start(slot_weight[i][:, s:s + 1], None, scr["weight"],
                                                bass.IndirectOffsetOnAxis(user[i][:, s, 1:2], 0),
                                                bounds_check=2 * z.TOK + CAP - 1, oob_is_err=False).then_inc(weight_gathered[i], 16)

                def add_results(e, i):
                    for s in range(ST):
                        pool.wait_ge(weighted, ST * e + s + 1)
                        settle(pool, pool_passed)
                        pool.indirect_dma_start(scr["out"], bass.IndirectOffsetOnAxis(user[i][:, s, 0:1], 0),
                                                result[:, s, :], None, bounds_check=z.TOK + CAP - 1,
                                                compute_op=ALU.add).then_inc(added, 16)
                    pool.wait_ge(added, 16 * ST * (e + 1))
                    settle(pool, pool_passed)

                with nc.allow_non_contiguous_dma(reason="640 slots' users, 8 bytes each"):
                    gather(0, 0, 0)
                    load_b2(0, 0)
                    load_b2(1, 1)
                    pool.wait_ge(x_turned, ST)
                    gather(1, 1, 0)
                    with pool.Fori(0, PAIRS - 1) as j:
                        for i in range(2):
                            e = 2 * j + i
                            add_results(e, i)
                            load_b2(e + 2, i)
                            pool.wait_ge(x_turned, ST * (e + 2))
                            gather(e + 2, i, j + 1)
                    for i in range(2):
                        add_results(E - 2 + i, i)

            @block.scalar
            def _(act):
                def split_w(e, f):
                    c, r = f // WC, f % RING
                    if f % WC == 0:
                        act.wait_ge(w1_loaded[c], 16 * (e + 1))
                        act.wait_ge(w2_loaded[c], 16 * (e + 1))
                    act.wait_ge(w_free, FT * e + f + 1)
                    act.activation(w1_hi[r][:, :, :], w1_raw[c][:, :, (f % WC) * P:(f % WC + 1) * P], ACT.Copy)
                    act.activation(w2_hi[r][:, :], w2_raw[c][:, f % WC, :], ACT.Copy).then_inc(w_hi, 1)

                def split_x(e, i, s):
                    act.wait_ge(x_turned, ST * e + s + 1)
                    act.activation(xT_hi[i][:, :, s * P:(s + 1) * P], bank(e, s)[:, :].rearrange("p (k n) -> p k n", n=P),
                                   ACT.Copy).then_inc(x_hi, 1)

                def gelu(e, f, parts):
                    act.wait_ge(hid_free, FT * e + f + 1)
                    for h, part in enumerate(parts):
                        act.wait_ge(first_done, 2 * (FT * e + f) + (h + 1) * 2 // len(parts))
                        settle(act, act_passed)
                        act.activation(hid[f % 2][:, part], first_ps[h][:, 0:part.stop - part.start], ACT.Gelu,
                                       bias=b1T[:, ds(FT * e + f, 1)]).then_inc(first_free, 2 // len(parts))

                def weigh(e, i, use):
                    act.wait_ge(weight_gathered[i], 16 * ST * (use + 1))
                    if not isinstance(e, int) or e > 0:
                        act.wait_ge(added, 16 * ST * e)
                    for s in range(ST):
                        act.wait_ge(acc_free, ST * (e + 1) + s + 1)
                        act.activation(result[:, s, :], total[:, s, :], ACT.Identity,
                                       scale=slot_weight[i][:, s:s + 1]).then_inc(weighted, 1)

                def expert(e, i, use, first=False, last=False):
                    in_use = act.value_load(used[0:1, ds(e, 1)], min_val=FEWEST, max_val=ST)
                    with act.If(in_use == ST - 1):
                        steps(e, i, use, first, last, ONE_BANK)
                    with act.If(in_use != ST - 1):
                        steps(e, i, use, first, last, PARTS)

                def steps(e, i, use, first, last, parts):
                    for f in range(FT):
                        if not (last and f + AHEAD >= FT):
                            split_w(e + (f + AHEAD) // FT, (f + AHEAD) % FT)
                        if not (last and f + 1 >= FT):
                            gelu(e + (f + 1) // FT, (f + 1) % FT, parts if f + 1 < FT else PARTS)
                        if f == 0 and not first:
                            weigh(e - 1, 1 - i, use - 1 + i)
                        if f in X_STEPS and not last:
                            split_x(e + 1, 1 - i, X_STEPS.index(f))

                for f in range(AHEAD):
                    split_w(0, f)
                for s in range(ST):
                    split_x(0, 0, s)
                act.wait_ge(b1_ready, 1)
                gelu(0, 0, PARTS)
                expert(0, 0, 0, first=True)
                expert(1, 1, 0)
                with act.Fori(1, PAIRS - 1) as j:
                    for i in range(2):
                        expert(2 * j + i, i, j)
                expert(E - 2, 0, PAIRS - 1)
                expert(E - 1, 1, PAIRS - 1, last=True)
                weigh(E - 1, 1, PAIRS - 1)

            @block.vector
            def _(dve):
                def split_w(e, f):
                    c, r = f // WC, f % RING
                    dve.wait_ge(w_hi, FT * e + f + 1)
                    dve.tensor_tensor(w1_lo[r][:, :, :], w1_raw[c][:, :, (f % WC) * P:(f % WC + 1) * P],
                                      w1_hi[r][:, :, :].bitcast(F32), ALU.subtract)
                    dve.tensor_tensor(w2_lo[r][:, :], w2_raw[c][:, f % WC, :], w2_hi[r][:, :].bitcast(F32),
                                      ALU.subtract).then_inc(w_lo, 1)

                def split_x(e, i, s):
                    dve.wait_ge(x_hi, ST * e + s + 1)
                    dve.tensor_tensor(xT_lo[i][:, :, s * P:(s + 1) * P], bank(e, s)[:, :].rearrange("p (k n) -> p k n", n=P),
                                      xT_hi[i][:, :, s * P:(s + 1) * P].bitcast(F32), ALU.subtract).then_inc(x_lo, 1)

                def split_hid(e, f):
                    n, r = FT * e + f, f % 2
                    dve.wait_ge(first_free, 2 * n + 4)
                    dve.wait_ge(w_free, n + RING - 1)
                    dve.tensor_copy(hid_hi[r][:, :], hid[r][:, :]).then_inc(hid_hi_done, 1)
                    dve.wait_ge(hid_hi_done, n + 1)
                    dve.tensor_tensor(hid_lo[r][:, :], hid[r][:, :], hid_hi[r][:, :].bitcast(F32), ALU.subtract).then_inc(hid_free, 1)

                def finish(e, i, use):
                    dve.wait_ge(b2_loaded[i], 16 * (use + 1))
                    if not isinstance(e, int) or e > 0:
                        dve.wait_ge(weighted, ST * e)
                    for s in range(ST):
                        if s < FEWEST - 1:
                            dve.wait_ge(acc_done, (FEWEST - 1) * e + s + 1)
                        else:
                            dve.wait_ge(w_free, RING + FT * (e + 1))
                        dve.tensor_tensor(total[:, s, :], acc[:, s, :], b2[i][:, :], ALU.add).then_inc(acc_free, 1)

                def expert(e, i, j, first, last):
                    for f in range(FT):
                        if f == 0 and not first:
                            finish(e - 1, 1 - i, j - 1 + i)
                        if not (last and f + AHEAD >= FT):
                            split_w(e + (f + AHEAD) // FT, (f + AHEAD) % FT)
                        if not (last and f + 1 >= FT):
                            split_hid(e + (f + 1) // FT, (f + 1) % FT)
                        if f in X_STEPS and not last:
                            split_x(e + 1, 1 - i, X_STEPS.index(f))

                dve.memset(acc[:, :, :], 0.0).then_inc(acc_free, ST)
                for h in range(2):
                    dve.memset(first_ps[h][:, :], 0.0).then_inc(first_free, 1)
                dve.sem_inc(hid_free, 2)
                dve.sem_inc(w_free, RING)
                dve.wait_ge(b1_turned, 1)
                dve.tensor_copy(b1T[:, :], turned[:, 0:2 * P]).then_inc(b1_ready, 1)
                for f in range(AHEAD):
                    split_w(0, f)
                for s in range(ST):
                    split_x(0, 0, s)
                split_hid(0, 0)
                expert(0, 0, 0, True, False)
                expert(1, 1, 0, False, False)
                with dve.Fori(1, PAIRS - 1) as j:
                    for i in range(2):
                        expert(2 * j + i, i, j, False, False)
                expert(E - 2, 0, PAIRS - 1, False, False)
                expert(E - 1, 1, PAIRS - 1, False, True)
                finish(E - 1, 1, PAIRS - 1)

            @block.tensor
            def _(pe):
                def turn(e, s):
                    if s == 0:
                        pe.wait_ge(gathered, 16 * ST * (e + 1))
                    if isinstance(e, int) and e == 0:
                        if s >= 3:
                            pe.wait_ge(x_lo, s - 2)
                    else:
                        pe.wait_ge(x_lo, ST * e + s)
                    for k in range(KT):
                        last = pe.transpose(bank(e, s)[:, k * P:(k + 1) * P], rows[:, s, k * P:(k + 1) * P], ident[:, :])
                    last.then_inc(x_turned, 1)

                def first(e, i, f, tiles):
                    n, r = FT * e + f, f % RING
                    pe.wait_ge(w_lo, n + 1)
                    if f == 0:
                        pe.wait_ge(x_lo, ST * (e + 1))
                    parts = {FEWEST: PARTS[:1], ST - 1: ONE_BANK, ST: PARTS}[tiles]
                    for h, part in enumerate(parts):
                        pe.wait_ge(first_free, 2 * n + h + 1)
                        for k in range(KT):
                            last = split_matmul(pe, first_ps[h][:, 0:part.stop - part.start],
                                                w1_hi[r][:, k, :], w1_lo[r][:, k, :],
                                                xT_hi[i][:, k, part], xT_lo[i][:, k, part], k == 0, k == KT - 1)
                        last.then_inc(first_done, 2 // len(parts))

                def second(e, f, tiles):
                    n, r = FT * e + f, f % RING
                    pe.wait_ge(hid_free, n + 3)
                    for s in range(tiles):
                        if f == 0:
                            pe.wait_ge(acc_free, ST * e + s + 1)
                        sl = slice(s * P, (s + 1) * P)
                        last = split_matmul(pe, acc[:, s, :], hid_hi[f % 2][:, sl], hid_lo[f % 2][:, sl],
                                            w2_hi[r][:, :], w2_lo[r][:, :], f == 0, f == FT - 1)
                        if f == FT - 1 and s < FEWEST - 1:
                            last.then_inc(acc_done, 1)
                    last.then_inc(w_free, 1)

                def steps(e, i, last, tiles):
                    for f in range(FT):
                        if f + 1 < FT:
                            first(e, i, f + 1, tiles)
                        elif not last:
                            first(e + 1, 1 - i, 0, ST)
                        if f in X_STEPS and not last:
                            turn(e + 1, X_STEPS.index(f))
                        second(e, f, tiles)

                def expert(e, i, last=False):
                    in_use = pe.value_load(used[0:1, ds(e, 1)], min_val=FEWEST, max_val=ST)
                    for tiles in range(FEWEST, ST + 1):
                        with pe.If(in_use == tiles):
                            steps(e, i, last, tiles)

                pe.wait_ge(ident_ready, 2)
                pe.wait_ge(b1_loaded, 16)
                for h in range(2):
                    last = pe.transpose(turned[:, h * P:(h + 1) * P], b1_raw[:, h, :], ident[:, :])
                last.then_inc(b1_turned, 1)
                pe.wait_ge(b1_ready, 1)
                pe.wait_ge(first_free, 2)
                for s in range(ST):
                    turn(0, s)
                first(0, 0, 0, ST)
                with pe.Fori(0, PAIRS - 1) as j:
                    for i in range(2):
                        expert(2 * j + i, i)
                expert(E - 2, 0)
                expert(E - 1, 1, last=True)


INPUTS = ("x", "ctx_1024", "g_xattn", "g_ffn", "L0_xattn_Wq", "L0_xattn_bq", "L0_xattn_Wk", "L0_xattn_bk",
          "L0_xattn_Wv", "L0_xattn_bv", "L0_xattn_Wo", "L0_xattn_bo", "L0_ffn_router_w", "L0_ffn_router_b",
          "L0_ffn_w1", "L0_ffn_b1", "L0_ffn_w2", "L0_ffn_b2")


def gated_attention_and_experts(nc, z, a, out):
    def dram(name, shape, dt=F32):
        return nc.dram_tensor(name, shape, dt).ap()

    scr = dict(qk=dram("scr_qk", [2, 2, z.KT, P, z.TOK]),
               v=dram("scr_v", [z.TOK, z.D]),
               o=dram("scr_o", [z.D, z.TOK]),
               xn=dram("scr_xn", [z.TOK + z.CAP, z.D]),
               weight=dram("scr_weight", [2 * z.TOK + z.CAP, 1]),
               user_of=dram("scr_user_of", [z.E * z.CAP, 2], I32),
               out=out)
    with ExitStack() as ctx:
        stacks = Stacks(nc, ctx, z, 0)
        project_inputs(nc, z, a, scr, stacks)
        attend(nc, z, scr, stacks)
    with ExitStack() as ctx:
        weights = ExpertWeights(nc, ctx, z, a)
        used = ctx.enter_context(nc.sbuf_tensor("used", [P, z.E], I32))
        route(nc, z, a, scr, weights, used)
        run_experts(nc, z, a, scr, weights, used)


def kernel(**inputs):
    import numpy as np
    from concourse import bacc
    from concourse.bass_utils import run_bass_kernel_spmd

    nc = bacc.Bacc("TRN2", target_bir_lowering=False, num_devices=1)
    z = Shapes(inputs["x"], inputs["L0_ffn_w1"])
    arrays, a = {}, {}
    for name in INPUTS:
        v = np.ascontiguousarray(inputs[name])
        if name in ("x", "ctx_1024"):
            v = v.reshape(z.TOK, z.D)
        arrays[name] = v
        short = {"ctx_1024": "ctx"}.get(name, name.removeprefix("L0_xattn_").removeprefix("L0_ffn_"))
        a[short] = nc.dram_tensor(name, v.shape, mybir.dt.from_np(v.dtype), kind="ExternalInput").ap()
    out = nc.dram_tensor("out", (z.TOK + z.CAP, z.D), F32, kind="ExternalOutput").ap()
    gated_attention_and_experts(nc, z, a, out)
    result = run_bass_kernel_spmd(nc, [arrays], core_ids=[0])
    return result.results[0]["out"][:z.TOK].reshape(z.B, z.S, z.D)
```
